# Optimizing a Trainium2 kernel written in Bass

```python
import numpy as np
import jax
import jax.numpy as jnp

def _softmax(x, axis=-1):
    return jax.nn.softmax(x, axis=axis)

def _gelu(x):
    return jax.nn.gelu(x, approximate=True)

def _silu(x):
    return jax.nn.silu(x)

def _sigmoid(x):
    return jax.nn.sigmoid(x)

def _layernorm(x, axis=-1, eps=1e-05):
    m = jnp.mean(x, axis=axis, keepdims=True)
    v = jnp.var(x, axis=axis, keepdims=True)
    return (x - m) / jnp.sqrt(v + eps)

def _scatter_add(tgt, idx, src, axis=0):
    return tgt.at[idx].add(src)

def _segment_sum(src, seg, n):
    return jax.ops.segment_sum(src, seg, n)
kernel_name = 'mk_perceiver_d2_seqx_r4_ae4c87'

def setup_inputs(seed: int=0):
    np.random.seed(seed)
    _w = jnp.asarray

    def _rec_inputs():
        import jax
        import jax.numpy as jnp
        _rk = jax.random.key(seed)
        x = -0.0005146 + 1 * jax.random.normal(jax.random.fold_in(_rk, 1), (32, 64, 256), jnp.float32)
        _lenS = 64 - jax.random.randint(jax.random.fold_in(_rk, 7), (32,), 0, max(1, 64 // 4) + 1, jnp.int32)
        _lenS2 = 256 - jax.random.randint(jax.random.fold_in(_rk, 8), (32,), 0, max(1, 256 // 4) + 1, jnp.int32)
        _ctx_1024P = jax.random.normal(jax.random.fold_in(_rk, 11), (32, 16, 256), jnp.float32)
        _ctx_1024c = jax.random.dirichlet(jax.random.fold_in(_rk, 511), 0.3 * jnp.ones((16,), jnp.float32), (32, 256))
        _ctx_1024t = jnp.einsum('bsk,bkd->bsd', _ctx_1024c, _ctx_1024P)
        _ctx_1024t = _ctx_1024t * jax.lax.rsqrt(jnp.mean(jnp.square(_ctx_1024t)) + 1e-12) * 0.953939
        ctx_1024 = -0.000392918 + 0.999932 * (_ctx_1024t + 0.3 * jax.random.normal(jax.random.fold_in(_rk, 611), (32, 256, 256), jnp.float32))
        _validS = jnp.arange(64)[None, :] < _lenS[:, None]
        _validS2 = jnp.arange(256)[None, :] < _lenS2[:, None]
        _causal = jnp.tril(jnp.ones((64, 64), dtype=bool))
        mask_1x1xSxS2_ik1 = jnp.where(jnp.broadcast_to(_validS2[0:1, None, None, :], (1, 1, 64, 256)), 1, 0).astype(jnp.int32)
        return (x, ctx_1024, mask_1x1xSxS2_ik1)
    x, ctx_1024, mask_1x1xSxS2_ik1 = _rec_inputs()

    def _L0_xattn_setup():
        import jax, jax.numpy as jnp
        import numpy as np
        DIM = 256
        DIM_HEAD = 64
        HEADS = 16
        INNER = DIM_HEAD * HEADS
        EPS = 1e-05

        def layer_norm(x, g, b):
            m = jnp.mean(x, axis=-1, keepdims=True)
            v = jnp.mean(jnp.square(x - m), axis=-1, keepdims=True)
            return (x - m) * jax.lax.rsqrt(v + EPS) * g + b
        key = jax.random.key(seed)
        ks = jax.random.split(key, 8)
        B, N_IMG, N_LAT = (4, 1024, 128)
        std = 1.0 / np.sqrt(DIM)
        return {'image_embeds': jax.random.normal(ks[0], (B, N_IMG, DIM), dtype=jnp.float32), 'latents': jax.random.normal(ks[1], (B, N_LAT, DIM), dtype=jnp.float32), 'ln1_g': jnp.ones((DIM,), jnp.float32), 'ln1_b': jnp.zeros((DIM,), jnp.float32), 'ln2_g': jnp.ones((DIM,), jnp.float32), 'ln2_b': jnp.zeros((DIM,), jnp.float32), 'Wq': jax.random.normal(ks[2], (DIM, INNER), dtype=jnp.float32) * std, 'Wkv': jax.random.normal(ks[3], (DIM, 2 * INNER), dtype=jnp.float32) * std, 'Wo': jax.random.normal(ks[4], (INNER, DIM), dtype=jnp.float32) * std}
    _L0_xattn_all = _L0_xattn_setup()
    _L0_xattn_in = {k: v for k, v in _L0_xattn_all.items() if k in ('ln1_g', 'ln1_b', 'ln2_g', 'ln2_b', 'Wq', 'Wkv', 'Wo')}
    del _L0_xattn_all

    def _L0_attn_setup():
        import jax, jax.numpy as jnp
        import numpy as np
        DIM = 256
        H = 16
        HD = DIM // H
        EPS_DENOM = 1e-06
        EPS_LN = 1e-05
        key = jax.random.key(seed)
        ks = jax.random.split(key, 8)
        B, N = (4, 1024)
        s = 1.0 / np.sqrt(DIM)
        return {'x': jax.random.normal(ks[0], (B, N, DIM), dtype=jnp.float32), 'Wq': jax.random.normal(ks[1], (DIM, DIM), dtype=jnp.float32) * s, 'bq': jnp.zeros((DIM,), dtype=jnp.float32), 'Wk': jax.random.normal(ks[2], (DIM, DIM), dtype=jnp.float32) * s, 'bk': jnp.zeros((DIM,), dtype=jnp.float32), 'Wv': jax.random.normal(ks[3], (DIM, DIM), dtype=jnp.float32) * s, 'bv': jnp.zeros((DIM,), dtype=jnp.float32), 'gamma': jnp.ones((DIM,), dtype=jnp.float32), 'beta': jnp.zeros((DIM,), dtype=jnp.float32)}
    _L0_attn_all = _L0_attn_setup()
    _L0_attn_in = {k: v for k, v in _L0_attn_all.items() if k in ('Wq', 'bq', 'Wk', 'bk', 'Wv', 'bv', 'gamma', 'beta')}
    del _L0_attn_all

    def _L0_ffn_setup():
        import jax, jax.numpy as jnp
        import numpy as np
        DIM = 256
        HIDDEN = 768
        SCALE = 1.0 / 127.0

        def _dequant(w_int, dtype):
            return w_int.astype(dtype) * jnp.asarray(SCALE, dtype)
        key = jax.random.key(seed)
        k_x, k_g, k_u, k_d = jax.random.split(key, 4)
        x = jax.random.normal(k_x, (4, 512, DIM), dtype=jnp.float32)
        w_gate = jax.random.randint(k_g, (HIDDEN, DIM), -127, 128, dtype=jnp.int32)
        w_up = jax.random.randint(k_u, (HIDDEN, DIM), -127, 128, dtype=jnp.int32)
        w_down = jax.random.randint(k_d, (DIM, HIDDEN), -127, 128, dtype=jnp.int32)
        return {'x': x, 'w_gate': w_gate, 'w_up': w_up, 'w_down': w_down}
    _L0_ffn_all = _L0_ffn_setup()
    _L0_ffn_in = {k: v for k, v in _L0_ffn_all.items() if k in ('w_gate', 'w_up', 'w_down')}
    del _L0_ffn_all

    def _L1_xattn_setup():
        import jax, jax.numpy as jnp
        import numpy as np
        D_MODEL = 256
        NUM_HEADS = 16
        HEAD_DIM = D_MODEL // NUM_HEADS
        B, S = (4, 512)
        key = jax.random.key(seed)
        ks = jax.random.split(key, 12)
        scale = 1.0 / np.sqrt(D_MODEL)
        inp = {'query': jax.random.normal(ks[0], (B, S, D_MODEL), jnp.float32), 'key': jax.random.normal(ks[1], (B, S, D_MODEL), jnp.float32), 'value': jax.random.normal(ks[2], (B, S, D_MODEL), jnp.float32), 'mask': jax.random.randint(ks[3], (1, 1, S, S), 0, 2, jnp.int32), 'Wq': jax.random.normal(ks[4], (D_MODEL, D_MODEL), jnp.float32) * scale, 'bq': jnp.zeros((D_MODEL,), jnp.float32), 'Wk': jax.random.normal(ks[5], (D_MODEL, D_MODEL), jnp.float32) * scale, 'bk': jnp.zeros((D_MODEL,), jnp.float32), 'Wv': jax.random.normal(ks[6], (D_MODEL, D_MODEL), jnp.float32) * scale, 'bv': jnp.zeros((D_MODEL,), jnp.float32), 'Wo': jax.random.normal(ks[7], (D_MODEL, D_MODEL), jnp.float32) * scale, 'bo': jnp.zeros((D_MODEL,), jnp.float32)}
        return inp
    _L1_xattn_all = _L1_xattn_setup()
    _L1_xattn_in = {k: v for k, v in _L1_xattn_all.items() if k in ('Wq', 'bq', 'Wk', 'bk', 'Wv', 'bv', 'Wo', 'bo')}
    del _L1_xattn_all

    def _L1_attn_setup():
        import jax, jax.numpy as jnp
        import numpy as np
        B, S, D, N = (8, 1024, 256, 64)
        EPS = 1e-05
        key = jax.random.key(seed)
        ks = jax.random.split(key, 6)
        sD = 1.0 / np.sqrt(D)
        sN = 1.0 / np.sqrt(N)
        return {'x': jax.random.normal(ks[0], (B, S, D), dtype=jnp.float32), 'ln_w': jnp.ones((D,), jnp.float32), 'ln_b': jnp.zeros((D,), jnp.float32), 'Wi': jax.random.normal(ks[1], (N, D), jnp.float32) * sD, 'bi': jnp.zeros((N,), jnp.float32), 'Wf': jax.random.normal(ks[2], (N, D), jnp.float32) * sD, 'bf': jnp.zeros((N,), jnp.float32), 'Wz': jax.random.normal(ks[3], (N, D), jnp.float32) * sD, 'bz': jnp.zeros((N,), jnp.float32), 'Wo': jax.random.normal(ks[4], (N, D), jnp.float32) * sD, 'bo': jnp.zeros((N,), jnp.float32), 'Wp': jax.random.normal(ks[5], (D, N), jnp.float32) * sN, 'bp': jnp.zeros((D,), jnp.float32)}
    _L1_attn_all = _L1_attn_setup()
    _L1_attn_in = {k: v for k, v in _L1_attn_all.items() if k in ('ln_w', 'ln_b', 'Wi', 'bi', 'Wf', 'bf', 'Wz', 'bz', 'Wo', 'bo', 'Wp', 'bp')}
    del _L1_attn_all

    def _L1_ffn_setup():
        import jax, jax.numpy as jnp
        import numpy as np
        ALPHA = 1.5
        TEMP = 1.0
        N_ITER = 25
        THRESH = 1e-09

        def entmax_bisect(X, alpha=ALPHA, n_iter=N_ITER):
            d = X.shape[-1]
            inv_am1 = 1.0 / (alpha - 1.0)
            Xs = X * (alpha - 1.0)
            max_val = jnp.max(Xs, axis=-1, keepdims=True)
            tau_lo = max_val - 1.0
            tau_hi = max_val - (1.0 / d) ** (alpha - 1.0)
            f_lo = jnp.sum(jnp.maximum(Xs - tau_lo, 0.0) ** inv_am1, axis=-1, keepdims=True) - 1.0

            def body(i, carry):
                tau_lo, dm, _ = carry
                dm = dm * 0.5
                tau_m = tau_lo + dm
                f_m = jnp.sum(jnp.maximum(Xs - tau_m, 0.0) ** inv_am1, axis=-1, keepdims=True) - 1.0
                tau_lo = jnp.where(f_m * f_lo >= 0.0, tau_m, tau_lo)
                return (tau_lo, dm, tau_m)
            dm0 = tau_hi - tau_lo
            _, _, tau_m = jax.lax.fori_loop(0, n_iter, body, (tau_lo, dm0, tau_lo))
            p = jnp.maximum(Xs - tau_m, 0.0) ** inv_am1
            return p / jnp.sum(p, axis=-1, keepdims=True)
        key = jax.random.key(seed)
        ks = jax.random.split(key, 8)
        B, S, D, E = (2, 256, 256, 8)
        F = 4 * D
        return {'x': jax.random.normal(ks[0], (B, S, D), jnp.float32), 'Wr': jax.random.normal(ks[1], (D, E), jnp.float32) * 0.02, 'br': jnp.zeros((E,), jnp.float32), 'W1': jax.random.normal(ks[2], (E, D, F), jnp.float32) * 0.02, 'b1': jnp.zeros((E, F), jnp.float32), 'W2': jax.random.normal(ks[3], (E, F, D), jnp.float32) * 0.02, 'b2': jnp.zeros((E, D), jnp.float32)}
    _L1_ffn_all = _L1_ffn_setup()
    _L1_ffn_in = {k: v for k, v in _L1_ffn_all.items() if k in ('Wr', 'br', 'W1', 'b1', 'W2', 'b2')}
    del _L1_ffn_all
    return {'x': x, 'ctx_1024': ctx_1024, 'mask_1x1xSxS2_ik1': mask_1x1xSxS2_ik1, 'L0_xattn_ln1_g': _L0_xattn_in['ln1_g'], 'L0_xattn_ln1_b': _L0_xattn_in['ln1_b'], 'L0_xattn_ln2_g': _L0_xattn_in['ln2_g'], 'L0_xattn_ln2_b': _L0_xattn_in['ln2_b'], 'L0_xattn_Wq': _L0_xattn_in['Wq'], 'L0_xattn_Wkv': _L0_xattn_in['Wkv'], 'L0_xattn_Wo': _L0_xattn_in['Wo'], 'L0_attn_Wq': _L0_attn_in['Wq'], 'L0_attn_bq': _L0_attn_in['bq'], 'L0_attn_Wk': _L0_attn_in['Wk'], 'L0_attn_bk': _L0_attn_in['bk'], 'L0_attn_Wv': _L0_attn_in['Wv'], 'L0_attn_bv': _L0_attn_in['bv'], 'L0_attn_gamma': _L0_attn_in['gamma'], 'L0_attn_beta': _L0_attn_in['beta'], 'L0_ffn_w_gate': _L0_ffn_in['w_gate'], 'L0_ffn_w_up': _L0_ffn_in['w_up'], 'L0_ffn_w_down': _L0_ffn_in['w_down'], 'L1_xattn_Wq': _L1_xattn_in['Wq'], 'L1_xattn_bq': _L1_xattn_in['bq'], 'L1_xattn_Wk': _L1_xattn_in['Wk'], 'L1_xattn_bk': _L1_xattn_in['bk'], 'L1_xattn_Wv': _L1_xattn_in['Wv'], 'L1_xattn_bv': _L1_xattn_in['bv'], 'L1_xattn_Wo': _L1_xattn_in['Wo'], 'L1_xattn_bo': _L1_xattn_in['bo'], 'L1_attn_ln_w': _L1_attn_in['ln_w'], 'L1_attn_ln_b': _L1_attn_in['ln_b'], 'L1_attn_Wi': _L1_attn_in['Wi'], 'L1_attn_bi': _L1_attn_in['bi'], 'L1_attn_Wf': _L1_attn_in['Wf'], 'L1_attn_bf': _L1_attn_in['bf'], 'L1_attn_Wz': _L1_attn_in['Wz'], 'L1_attn_bz': _L1_attn_in['bz'], 'L1_attn_Wo': _L1_attn_in['Wo'], 'L1_attn_bo': _L1_attn_in['bo'], 'L1_attn_Wp': _L1_attn_in['Wp'], 'L1_attn_bp': _L1_attn_in['bp'], 'L1_ffn_Wr': _L1_ffn_in['Wr'], 'L1_ffn_br': _L1_ffn_in['br'], 'L1_ffn_W1': _L1_ffn_in['W1'], 'L1_ffn_b1': _L1_ffn_in['b1'], 'L1_ffn_W2': _L1_ffn_in['W2'], 'L1_ffn_b2': _L1_ffn_in['b2']}

def reference(x, ctx_1024, mask_1x1xSxS2_ik1, L0_xattn_ln1_g, L0_xattn_ln1_b, L0_xattn_ln2_g, L0_xattn_ln2_b, L0_xattn_Wq, L0_xattn_Wkv, L0_xattn_Wo, L0_attn_Wq, L0_attn_bq, L0_attn_Wk, L0_attn_bk, L0_attn_Wv, L0_attn_bv, L0_attn_gamma, L0_attn_beta, L0_ffn_w_gate, L0_ffn_w_up, L0_ffn_w_down, L1_xattn_Wq, L1_xattn_bq, L1_xattn_Wk, L1_xattn_bk, L1_xattn_Wv, L1_xattn_bv, L1_xattn_Wo, L1_xattn_bo, L1_attn_ln_w, L1_attn_ln_b, L1_attn_Wi, L1_attn_bi, L1_attn_Wf, L1_attn_bf, L1_attn_Wz, L1_attn_bz, L1_attn_Wo, L1_attn_bo, L1_attn_Wp, L1_attn_bp, L1_ffn_Wr, L1_ffn_br, L1_ffn_W1, L1_ffn_b1, L1_ffn_W2, L1_ffn_b2):
    import jax
    import jax.numpy as jnp

    def _L0_xattn_ref(image_embeds, latents, ln1_g, ln1_b, ln2_g, ln2_b, Wq, Wkv, Wo):
        import jax, jax.numpy as jnp
        import numpy as np
        DIM = 256
        DIM_HEAD = 64
        HEADS = 16
        INNER = DIM_HEAD * HEADS
        EPS = 1e-05

        def layer_norm(x, g, b):
            m = jnp.mean(x, axis=-1, keepdims=True)
            v = jnp.mean(jnp.square(x - m), axis=-1, keepdims=True)
            return (x - m) * jax.lax.rsqrt(v + EPS) * g + b
        B, S_lat, _ = latents.shape
        x = layer_norm(image_embeds, ln1_g, ln1_b)
        l = layer_norm(latents, ln2_g, ln2_b)
        q = l @ Wq
        kv_in = jnp.concatenate([x, l], axis=1)
        kv = kv_in @ Wkv
        k, v = jnp.split(kv, 2, axis=-1)

        def to_heads(t):
            return t.reshape(t.shape[0], t.shape[1], HEADS, DIM_HEAD).transpose(0, 2, 1, 3)
        q, k, v = (to_heads(q), to_heads(k), to_heads(v))
        scale = 1.0 / np.sqrt(np.sqrt(DIM_HEAD))
        w = jnp.einsum('bhqd,bhkd->bhqk', q * scale, k * scale)
        w = jax.nn.softmax(w.astype(jnp.float32), axis=-1).astype(q.dtype)
        out = jnp.einsum('bhqk,bhkd->bhqd', w, v)
        out = out.transpose(0, 2, 1, 3).reshape(B, S_lat, INNER)
        return out @ Wo

    def _L0_attn_ref(x, Wq, bq, Wk, bk, Wv, bv, gamma, beta):
        import jax, jax.numpy as jnp
        import numpy as np
        DIM = 256
        H = 16
        HD = DIM // H
        EPS_DENOM = 1e-06
        EPS_LN = 1e-05
        B, N, C = x.shape
        q = (x @ Wq.T + bq).reshape(B, N, H, HD)
        k = (x @ Wk.T + bk).reshape(B, N, H, HD)
        v = (x @ Wv.T + bv).reshape(B, N, H, HD)
        q = jax.nn.relu(q)
        k = jax.nn.relu(k)
        kv = jnp.einsum('bnhd,bnhp->bhdp', k, v)
        k_sum = k.sum(axis=1)
        denom = jnp.einsum('bnhd,bhd->bnh', q, k_sum)
        denom = jnp.maximum(denom, EPS_DENOM)[..., None]
        ctx = jnp.einsum('bnhd,bhdp->bnhp', q, kv)
        out = (ctx / denom).reshape(B, N, C)
        y = out + x
        mu = y.mean(axis=-1, keepdims=True)
        var = y.var(axis=-1, keepdims=True)
        return (y - mu) / jnp.sqrt(var + EPS_LN) * gamma + beta

    def _L0_ffn_ref(x, w_gate, w_up, w_down):
        import jax, jax.numpy as jnp
        import numpy as np
        DIM = 256
        HIDDEN = 768
        SCALE = 1.0 / 127.0

        def _dequant(w_int, dtype):
            return w_int.astype(dtype) * jnp.asarray(SCALE, dtype)
        wg = _dequant(w_gate, x.dtype)
        wu = _dequant(w_up, x.dtype)
        wd = _dequant(w_down, x.dtype)
        gate = jnp.einsum('bsd,hd->bsh', x, wg)
        up = jnp.einsum('bsd,hd->bsh', x, wu)
        h = jax.nn.silu(gate) * up
        return jnp.einsum('bsh,dh->bsd', h, wd)

    def _L1_xattn_ref(query, key, value, mask, Wq, bq, Wk, bk, Wv, bv, Wo, bo):
        import jax, jax.numpy as jnp
        import numpy as np
        D_MODEL = 256
        NUM_HEADS = 16
        HEAD_DIM = D_MODEL // NUM_HEADS
        B, S = (4, 512)
        b = query.shape[0]
        Q = query @ Wq.T + bq
        K = key @ Wk.T + bk
        V = value @ Wv.T + bv
        Q = Q.reshape(b, -1, NUM_HEADS, HEAD_DIM).transpose(0, 2, 1, 3)
        K = K.reshape(b, -1, NUM_HEADS, HEAD_DIM).transpose(0, 2, 1, 3)
        V = V.reshape(b, -1, NUM_HEADS, HEAD_DIM).transpose(0, 2, 1, 3)
        energy = jnp.einsum('bhqd,bhkd->bhqk', Q, K) / np.sqrt(HEAD_DIM).astype(np.float32)
        energy = jnp.where(mask == 0, jnp.float32(-1e+20), energy)
        attention = jax.nn.softmax(energy, axis=-1)
        x = jnp.einsum('bhqk,bhkd->bhqd', attention, V)
        x = x.transpose(0, 2, 1, 3).reshape(b, -1, D_MODEL)
        return x @ Wo.T + bo

    def _L1_attn_ref(x, ln_w, ln_b, Wi, bi, Wf, bf, Wz, bz, Wo, bo, Wp, bp):
        import jax, jax.numpy as jnp
        import numpy as np
        B, S, D, N = (8, 1024, 256, 64)
        EPS = 1e-05
        mu = jnp.mean(x, axis=-1, keepdims=True)
        var = jnp.mean(jnp.square(x - mu), axis=-1, keepdims=True)
        xn = (x - mu) * jax.lax.rsqrt(var + EPS) * ln_w + ln_b
        log_i = jnp.clip(jnp.einsum('bsd,nd->bsn', xn, Wi) + bi, -20.0, 20.0)
        log_f = jnp.clip(jnp.einsum('bsd,nd->bsn', xn, Wf) + bf, -20.0, 20.0)
        z = jnp.tanh(jnp.einsum('bsd,nd->bsn', xn, Wz) + bz)
        o = jax.nn.sigmoid(jnp.einsum('bsd,nd->bsn', xn, Wo) + bo)

        def step(carry, inp):
            c, m = carry
            li, lf, zt, ot = inp
            m_new = jnp.maximum(m + lf, li)
            i_s = jnp.exp(li - m_new)
            f_s = jnp.exp(m + lf - m_new)
            c = f_s * c + i_s * zt
            h = ot * jnp.tanh(c)
            return ((c, m_new), h)
        c0 = jnp.zeros((x.shape[0], log_i.shape[-1]), x.dtype)
        m0 = jnp.zeros_like(c0)
        tm = lambda a: jnp.swapaxes(a, 0, 1)
        _, h_seq = jax.lax.scan(step, (c0, m0), (tm(log_i), tm(log_f), tm(z), tm(o)))
        h_seq = jnp.swapaxes(h_seq, 0, 1)
        return jnp.einsum('bsn,dn->bsd', h_seq, Wp) + bp

    def _L1_ffn_ref(x, Wr, br, W1, b1, W2, b2):
        import jax, jax.numpy as jnp
        import numpy as np
        ALPHA = 1.5
        TEMP = 1.0
        N_ITER = 25
        THRESH = 1e-09

        def entmax_bisect(X, alpha=ALPHA, n_iter=N_ITER):
            d = X.shape[-1]
            inv_am1 = 1.0 / (alpha - 1.0)
            Xs = X * (alpha - 1.0)
            max_val = jnp.max(Xs, axis=-1, keepdims=True)
            tau_lo = max_val - 1.0
            tau_hi = max_val - (1.0 / d) ** (alpha - 1.0)
            f_lo = jnp.sum(jnp.maximum(Xs - tau_lo, 0.0) ** inv_am1, axis=-1, keepdims=True) - 1.0

            def body(i, carry):
                tau_lo, dm, _ = carry
                dm = dm * 0.5
                tau_m = tau_lo + dm
                f_m = jnp.sum(jnp.maximum(Xs - tau_m, 0.0) ** inv_am1, axis=-1, keepdims=True) - 1.0
                tau_lo = jnp.where(f_m * f_lo >= 0.0, tau_m, tau_lo)
                return (tau_lo, dm, tau_m)
            dm0 = tau_hi - tau_lo
            _, _, tau_m = jax.lax.fori_loop(0, n_iter, body, (tau_lo, dm0, tau_lo))
            p = jnp.maximum(Xs - tau_m, 0.0) ** inv_am1
            return p / jnp.sum(p, axis=-1, keepdims=True)
        B, S, D = x.shape
        xt = x.reshape(B * S, D)
        logits = (xt @ Wr + br) / TEMP
        gates = entmax_bisect(logits)
        gates = jnp.where(gates > THRESH, gates, 0.0)
        h = jax.nn.relu(jnp.einsum('td,edf->etf', xt, W1) + b1[:, None, :])
        y = jnp.einsum('etf,efd->etd', h, W2) + b2[:, None, :]
        out = jnp.einsum('etd,te->td', y, gates)
        return out.reshape(B, S, D)
    x = x + _L0_xattn_ref(ctx_1024, _layernorm(x, axis=-1), L0_xattn_ln1_g, L0_xattn_ln1_b, L0_xattn_ln2_g, L0_xattn_ln2_b, L0_xattn_Wq, L0_xattn_Wkv, L0_xattn_Wo)
    x = x + _L0_attn_ref(_layernorm(x, axis=-1), L0_attn_Wq, L0_attn_bq, L0_attn_Wk, L0_attn_bk, L0_attn_Wv, L0_attn_bv, L0_attn_gamma, L0_attn_beta)
    x = x + _L0_ffn_ref(_layernorm(x, axis=-1), L0_ffn_w_gate, L0_ffn_w_up, L0_ffn_w_down)
    x = x + _L1_xattn_ref(_layernorm(x, axis=-1), ctx_1024, ctx_1024, mask_1x1xSxS2_ik1, L1_xattn_Wq, L1_xattn_bq, L1_xattn_Wk, L1_xattn_bk, L1_xattn_Wv, L1_xattn_bv, L1_xattn_Wo, L1_xattn_bo)
    x = x + _L1_attn_ref(_layernorm(x, axis=-1), L1_attn_ln_w, L1_attn_ln_b, L1_attn_Wi, L1_attn_bi, L1_attn_Wf, L1_attn_bf, L1_attn_Wz, L1_attn_bz, L1_attn_Wo, L1_attn_bo, L1_attn_Wp, L1_attn_bp)
    x = x + _L1_ffn_ref(_layernorm(x, axis=-1), L1_ffn_Wr, L1_ffn_br, L1_ffn_W1, L1_ffn_b1, L1_ffn_W2, L1_ffn_b2)
    return x

_drawn_inputs = setup_inputs


def setup_inputs(seed=0):
    import zlib

    import numpy as np

    out = dict(_drawn_inputs(seed))
    spreads = {'L0_xattn_ln1_g': (1.0, 0.2),
     'L0_xattn_ln1_b': (0.0, 0.1),
     'L0_xattn_ln2_g': (1.0, 0.2),
     'L0_xattn_ln2_b': (0.0, 0.1),
     'L0_attn_bq': (0.0, 2.0),
     'L0_attn_bk': (0.0, 2.0),
     'L0_attn_bv': (0.0, 0.1),
     'L0_attn_gamma': (1.0, 0.2),
     'L0_attn_beta': (0.0, 0.1),
     'L1_xattn_bq': (0.0, 2.0),
     'L1_xattn_bk': (0.0, 2.0),
     'L1_xattn_bv': (0.0, 2.0),
     'L1_xattn_bo': (0.0, 2.0),
     'L1_attn_ln_w': (1.0, 0.6),
     'L1_attn_ln_b': (0.0, 2.0),
     'L1_attn_bi': (0.0, 2.0),
     'L1_attn_bf': (0.0, 2.0),
     'L1_attn_bz': (0.0, 2.0),
     'L1_attn_bo': (0.0, 2.0),
     'L1_attn_bp': (0.0, 2.0),
     'L1_ffn_br': (0.0, 2.0),
     'L1_ffn_b1': (0.0, 2.0),
     'L1_ffn_b2': (0.0, 2.0)}
    factors = {'L1_xattn_Wq': 8.0,
     'L1_xattn_Wk': 8.0,
     'L1_xattn_Wv': 8.0,
     'L1_xattn_Wo': 8.0,
     'L1_attn_Wi': 64.0,
     'L1_attn_Wf': 64.0,
     'L1_attn_Wz': 64.0,
     'L1_attn_Wo': 64.0,
     'L1_attn_Wp': 64.0,
     'L1_ffn_Wr': 58.591,
     'L1_ffn_W1': 64.0,
     'L1_ffn_W2': 53.105}
    for name, (base, spread) in spreads.items():
        noise = np.random.default_rng([zlib.crc32(name.encode()), seed]).standard_normal(out[name].shape)
        drawn = base * np.exp(spread * noise) if base else spread * noise
        out[name] = jnp.asarray(drawn.astype(out[name].dtype))
    for name, factor in factors.items():
        out[name] = (out[name] * factor).astype(out[name].dtype)
    return out
```

```python
from contextlib import ExitStack

import concourse.bass as bass
from concourse import mybir

F32 = mybir.dt.float32
F32R = mybir.dt.float32r
I32 = mybir.dt.int32
ALU = mybir.AluOpType
ACT = mybir.ActivationFunctionType
AX = mybir.AxisListType

P = 128
D = 256
KD = D // P
B = 32
S = 64
S2 = 256
T = B * S
NT = T // P
CH = 512
NCH = T // CH
EPS = 1e-5
PASSES = ((0, 0), (0, 1), (1, 0))


def rows(w):
    return w.rearrange("(k p) n -> p k n", p=P)


def column(v):
    return v.rearrange("(k p) -> p k", p=P)


def everywhere(v):
    return v.partition_broadcast(P)


class Tools:

    def __init__(self, nc, ctx, stage):
        self.nc, self.ctx, self.stage = nc, ctx, stage

    def sb(self, name, shape, dt=F32):
        return self.ctx.enter_context(self.nc.sbuf_tensor(f"{self.stage}_{name}", shape, dt))


class Sem:

    def __init__(self, sem):
        self.sem, self.n = sem, 0

    def give(self, ins):
        ins.then_inc(self.sem, 1)
        self.n += 1
        return self.n


def wait(eng, sem, value):
    if isinstance(value, int) and value <= 0:
        return
    eng.wait_ge(sem, value)


def product3(pe, out, lhs, rhs, first=True, last=True):
    mm = None
    for k in range(KD):
        for n, (a, b) in enumerate(PASSES):
            mm = pe.matmul(out, lhs(a, k), rhs(b, k), start=first and k == 0 and n == 0,
                           stop=last and k == KD - 1 and n == 2)
    return mm


class NormStats:

    def __init__(self, tools, n, stats, rstd_ready, tag=""):
        self.n = n
        self.raw = tools.sb("st_raw" + tag, [P, n, 6])
        self.tmp = tools.sb("st_tmp" + tag, [P, 5, n])
        self.mean = tools.sb("st_mean" + tag, [P, n])
        self.vareps = tools.sb("st_var" + tag, [P, n])
        self.rstd = tools.sb("st_rstd" + tag, [P, n])
        self.half = tools.sb("st_half" + tag, [P, n])
        self.stats, self.rstd_ready = stats, rstd_ready
        self.steps = n + 7

    def gather(self, dve, row, base):
        n, raw, tmp = self.n, self.raw, self.tmp
        for t in range(n):
            dve.bn_stats(raw[:, t, :], row(t)).then_inc(self.stats, 1)
        dve.wait_ge(self.stats, base + n)
        dve.tensor_tensor(tmp[:, 0, :], raw[:, :, 1], raw[:, :, 4], ALU.add).then_inc(self.stats, 1)
        dve.tensor_tensor(tmp[:, 1, :], raw[:, :, 1], raw[:, :, 4], ALU.subtract).then_inc(self.stats, 1)
        dve.tensor_tensor(tmp[:, 2, :], raw[:, :, 2], raw[:, :, 5], ALU.add).then_inc(self.stats, 1)
        dve.wait_ge(self.stats, base + n + 3)
        dve.tensor_scalar(self.mean[:, :], tmp[:, 0, :], 0.5, None, ALU.mult).then_inc(self.stats, 1)
        dve.tensor_tensor(tmp[:, 3, :], tmp[:, 1, :], tmp[:, 1, :], ALU.mult).then_inc(self.stats, 1)
        dve.tensor_scalar(tmp[:, 4, :], tmp[:, 2, :], 1.0 / D, EPS, ALU.mult, ALU.add).then_inc(self.stats, 1)
        dve.wait_ge(self.stats, base + n + 6)
        dve.scalar_tensor_tensor(out=self.vareps[:, :], in0=tmp[:, 3, :], scalar=0.25, in1=tmp[:, 4, :],
                                 op0=ALU.mult, op1=ALU.add).then_inc(self.stats, 1)

    def power_setup(self, pool, consts_ready):
        pool.memset(self.half[:, :], -0.5).then_inc(consts_ready, 1)

    def power(self, pool, base):
        pool.wait_ge(self.stats, base + self.steps)
        pool.tensor_tensor(self.rstd[:, :], self.vareps[:, :], self.half[:, :], ALU.pow).then_inc(self.rstd_ready, 1)

    def apply(self, dve, out, row, t):
        return dve.tensor_scalar(out, row, self.mean[:, t:t + 1], self.rstd[:, t:t + 1], ALU.subtract, ALU.mult)


class NormTranspose:

    def __init__(self, tools, sem, x_sb, ident, banks, split=False, double=False, affine=None):
        self.affine, self.per_tile = affine, KD if affine else 1
        self.x_sb, self.ident, self.banks, self.split, self.double = x_sb, ident, banks, split, double
        self.xn = tools.sb("xn", [P, NT, D])
        self.xt = tools.sb("xt", [P, 2 if split else 1, KD, T], F32R if split else F32)
        self.consts = sem("half_ready")
        self.norm = NormStats(tools, NT, sem("norm_stats"), sem("rstd_ready"))
        self.xn_ready, self.xt_psum = sem("xn_ready"), sem("xt_psum")
        self.xt_hi, self.xt_done = sem("xt_hi"), sem("xt_done")

    def pool(self, pool):
        self.norm.power_setup(pool, self.consts)
        pool.wait_ge(self.consts, 1)
        self.norm.power(pool, 0)
        if self.double:
            self.norm.power(pool, self.norm.steps)

    def dve(self, dve):
        norm = self.norm
        norm.gather(dve, lambda t: self.x_sb[:, t, :], 0)
        dve.wait_ge(norm.rstd_ready, 1)
        for t in range(NT):
            norm.apply(dve, self.xn[:, t, :], self.x_sb[:, t, :], t).then_inc(self.xn_ready, 1)
        done = NT
        if self.double:
            dve.wait_ge(self.xn_ready, NT)
            norm.gather(dve, lambda t: self.xn[:, t, :], norm.steps)
            dve.wait_ge(norm.rstd_ready, 2)
            for t in range(NT):
                norm.apply(dve, self.xn[:, t, :], self.xn[:, t, :], t).then_inc(self.xn_ready, 1)
            done = 2 * NT
        self.xn_count = done
        if self.split:
            for t in range(NT):
                dve.wait_ge(self.xt_hi, t + 1)
                dve.tensor_tensor(self.tile(1, t), self.turned(t), self.tile(0, t).bitcast(F32),
                                  ALU.subtract).then_inc(self.xt_done, 1)

    def tile(self, part, t):
        return self.xt[:, part, :, t * P:(t + 1) * P]

    def turned(self, t):
        return self.banks[t % 2][:, 0:D].rearrange("p (k n) -> p k n", k=KD)

    def pe(self, pe):
        base = NT if self.double else 0
        for t in range(NT):
            pe.wait_ge(self.xn_ready, base + t + 1)
            if t >= 2:
                pe.wait_ge(self.xt_done, self.per_tile * (t - 1))
            for k in range(KD):
                mm = pe.transpose(self.banks[t % 2][:, k * P:(k + 1) * P], self.xn[:, t, k * P:(k + 1) * P],
                                  self.ident)
            mm.then_inc(self.xt_psum, 1)

    def act(self, act):
        for t in range(NT):
            act.wait_ge(self.xt_psum, t + 1)
            if self.affine:
                scale, bias = self.affine
                for k in range(KD):
                    act.activation(self.tile(0, t)[:, k], self.turned(t)[:, k], ACT.Identity, bias=bias[:, k:k + 1],
                                   scale=scale[:, k:k + 1]).then_inc(self.xt_done, 1)
            else:
                act.copy(self.tile(0, t), self.turned(t)).then_inc(self.xt_hi if self.split else self.xt_done, 1)


def linear_attention(nc, k, x_sb, banks, w):
    with ExitStack() as ctx:
        tools = Tools(nc, ctx, "lin")
        sem = lambda name: k.stage_sem("lin_" + name)
        front = NormTranspose(tools, sem, x_sb, k.ident[:, :], banks[0:2])
        wq = tools.sb("wq", [P, KD, D])
        wkv = tools.sb("wkv", [P, KD, 2 * D])
        bq = tools.sb("bq", [P, KD])
        bkv = tools.sb("bkv", [P, 2 * D])
        gamma = tools.sb("gamma", [P, D])
        beta = tools.sb("beta", [P, D])
        qt = tools.sb("qt", [P, KD, T])
        vext = tools.sb("vext", [P, 2, KD, P + 1])
        kk = tools.sb("kk", [P, 2, D])
        kpre = tools.sb("kpre", [P, 2, D])
        kvm = tools.sb("kvm", [P, 2, 2, KD, P + 8])
        mask = tools.sb("mask", [P, P])
        rden = tools.sb("rden", [P, 2, 16])
        dmax = tools.sb("dmax", [P, 2, 16])
        ctxn = tools.sb("ctxn", [P, 2, D])
        y = tools.sb("y", [P, NT, D])
        norm2 = NormStats(tools, NT, sem("y_stats"), sem("y_rstd"), "y")
        loads, consts = sem("loads"), sem("consts")
        q_psum, q_done = sem("q_psum"), sem("q_done")
        kv_psum, k_ready, k_pre, v_ready = sem("kv_psum"), sem("k_ready"), sem("k_pre"), sem("v_ready")
        state_psum, state_ready = sem("state_psum"), sem("state_ready")
        ctx_psum, den_step, ctx_step, y_ready = sem("ctx_psum"), sem("den_step"), sem("ctx_step"), sem("y_ready")
        tail = sem("tail")
        kv_bank, st_bank, ctx_bank, q_bank = banks[2], banks[3:5], banks[5], banks[6:8]

        block = ctx.enter_context(nc.Block())

        @block.sync
        def _(sp):
            sp.dma_start(wq[:, :, :], rows(w["L0_attn_Wq"])).then_inc(loads, 16)
            sp.dma_start(wkv[:, :, 0:D], rows(w["L0_attn_Wk"])).then_inc(loads, 16)
            sp.dma_start(wkv[:, :, D:2 * D], rows(w["L0_attn_Wv"])).then_inc(loads, 16)
            with nc.allow_non_contiguous_dma(reason="a bias as a column"):
                sp.dma_start(bq[:, :], column(w["L0_attn_bq"])).then_inc(loads, 16)
            sp.dma_start(bkv[:, 0:D], everywhere(w["L0_attn_bk"])).then_inc(loads, 16)
            sp.dma_start(bkv[:, D:2 * D], everywhere(w["L0_attn_bv"])).then_inc(loads, 16)
            sp.dma_start(gamma[:, :], everywhere(w["L0_attn_gamma"])).then_inc(loads, 16)
            sp.dma_start(beta[:, :], everywhere(w["L0_attn_beta"])).then_inc(loads, 16)
            sp.wait_ge(loads, 128)

        @block.gpsimd
        def _(pool):
            pool.memset(vext[:, :, :, P:P + 1], 1.0).then_inc(consts, 1)
            pool.tensor_copy(mask[:, :].rearrange("p (h d) -> p h d", d=16),
                             k.head_mask[:, :].unsqueeze(2).to_broadcast([P, 8, 16])).then_inc(consts, 1)
            front.pool(pool)
            norm2.power_setup(pool, consts)
            pool.wait_ge(consts, 3)
            norm2.power(pool, 0)

        @block.tensor
        def _(pe):
            front.pe(pe)
            pe.wait_ge(loads, 128)
            xt = front.xt
            for n in range(KD * NCH):
                m, c = n % KD, n // KD
                pe.wait_ge(front.xt_done, 4 * c + 4)
                if n >= 2:
                    pe.wait_ge(q_done, n - 1)
                for kd in range(KD):
                    mm = pe.matmul(q_bank[n % 2][:, :], wq[:, kd, m * P:(m + 1) * P], xt[:, 0, kd, c * CH:(c + 1) * CH],
                                   start=kd == 0, stop=kd == KD - 1)
                mm.then_inc(q_psum, 1)
            pe.wait_ge(q_done, KD * NCH)

            def keys_values(t):
                if t >= 1:
                    pe.wait_ge(v_ready, t)
                for kd in range(KD):
                    mm = pe.matmul(kv_bank[:, :], xt[:, 0, kd, t * P:(t + 1) * P], wkv[:, kd, :],
                                   start=kd == 0, stop=kd == KD - 1)
                mm.then_inc(kv_psum, 1)

            def states(t):
                pe.wait_ge(k_ready, t + 1)
                pe.wait_ge(v_ready, t + 1)
                if t >= 1:
                    pe.wait_ge(state_ready, 4 * t)
                for b in range(2):
                    for m in range(KD):
                        mm = pe.matmul(st_bank[b][:, m * (P + 1):(m + 1) * (P + 1)],
                                       kk[b * S:(b + 1) * S, t % 2, m * P:(m + 1) * P],
                                       vext[b * S:(b + 1) * S, t % 2, m, :], start=True, stop=True)
                mm.then_inc(state_psum, 1)

            def contexts(t):
                pe.wait_ge(state_ready, 4 * t + 4)
                if t >= 1:
                    pe.wait_ge(y_ready, t)
                for b in range(2):
                    for m in range(KD):
                        at = t * P + b * S
                        mm = pe.matmul(ctx_bank[b * S:(b + 1) * S, m * (P + 8):(m + 1) * (P + 8)],
                                       qt[:, m, at:at + S], kvm[:, t % 2, b, m, :], start=True, stop=True)
                mm.then_inc(ctx_psum, 1)

            keys_values(0)
            for t in range(NT):
                states(t)
                if t + 1 < NT:
                    keys_values(t + 1)
                contexts(t)

        @block.scalar
        def _(act):
            front.act(act)
            act.wait_ge(loads, 128)
            act.wait_ge(consts, 1)
            for n in range(KD * NCH):
                m, c = n % KD, n // KD
                act.wait_ge(q_psum, n + 1)
                act.activation(qt[:, m, c * CH:(c + 1) * CH], q_bank[n % 2][:, :], ACT.Relu,
                               bias=bq[:, m:m + 1]).then_inc(q_done, 1)
            for t in range(NT):
                act.wait_ge(k_pre, t + 1)
                if t >= 2:
                    act.wait_ge(state_psum, t - 1)
                act.activation(kk[:, t % 2, :], kpre[:, t % 2, :], ACT.Relu).then_inc(k_ready, 1)

        @block.vector
        def _(dve):
            front.dve(dve)
            dve.wait_ge(loads, 128)
            dve.wait_ge(consts, 2)

            def keys_values(t):
                dve.wait_ge(kv_psum, t + 1)
                if t >= 2:
                    dve.wait_ge(k_ready, t - 1)
                    dve.wait_ge(state_psum, t - 1)
                dve.tensor_tensor(kpre[:, t % 2, :], kv_bank[:, 0:D], bkv[:, 0:D], ALU.add).then_inc(k_pre, 1)
                dve.tensor_tensor(vext[:, t % 2, :, 0:P],
                                  kv_bank[:, D:2 * D].rearrange("p (m n) -> p m n", m=KD),
                                  bkv[:, D:2 * D].rearrange("p (m n) -> p m n", m=KD), ALU.add).then_inc(v_ready, 1)

            def states(t):
                dve.wait_ge(state_psum, t + 1)
                if t >= 2:
                    dve.wait_ge(ctx_psum, t - 1)
                for b in range(2):
                    src = st_bank[b][:, 0:KD * (P + 1)].rearrange("p (m n) -> p m n", m=KD)
                    dve.tensor_tensor(kvm[:, t % 2, b, :, 0:P], src[:, :, 0:P],
                                      mask[:, :].unsqueeze(1).to_broadcast([P, KD, P]), ALU.mult).then_inc(state_ready, 1)
                    dve.tensor_tensor(kvm[:, t % 2, b, :, P:P + 8], src[:, :, P:P + 1].to_broadcast([P, KD, 8]),
                                      k.head_mask[:, :].unsqueeze(1).to_broadcast([P, KD, 8]),
                                      ALU.mult).then_inc(state_ready, 1)

            def contexts(t):
                dve.wait_ge(ctx_psum, t + 1)
                src = ctx_bank[:, 0:KD * (P + 8)].rearrange("p (m n) -> p m n", m=KD)
                den = dmax[:, t % 2, :].rearrange("p (m h) -> p m h", m=KD)
                dve.tensor_scalar(den, src[:, :, P:P + 8], 1e-6, None, ALU.max).then_inc(den_step, 1)
                dve.wait_ge(den_step, 2 * t + 1)
                dve.reciprocal(rden[:, t % 2, :], dmax[:, t % 2, :]).then_inc(den_step, 1)
                dve.wait_ge(den_step, 2 * t + 2)
                for m in range(KD):
                    dve.tensor_tensor(ctxn[:, t % 2, m * P:(m + 1) * P].rearrange("p (h d) -> p h d", d=16),
                                      src[:, m, 0:P].rearrange("p (h d) -> p h d", d=16),
                                      rden[:, t % 2, m * 8:(m + 1) * 8].unsqueeze(2).to_broadcast([P, 8, 16]),
                                      ALU.mult).then_inc(ctx_step, 1)
                dve.wait_ge(ctx_step, 2 * t + 2)
                dve.tensor_tensor(y[:, t, :], ctxn[:, t % 2, :], front.xn[:, t, :], ALU.add).then_inc(y_ready, 1)

            keys_values(0)
            for t in range(NT):
                states(t)
                if t + 1 < NT:
                    keys_values(t + 1)
                contexts(t)
            dve.wait_ge(y_ready, NT)
            norm2.gather(dve, lambda t: y[:, t, :], 0)
            dve.wait_ge(norm2.rstd_ready, 1)
            for t in range(NT):
                norm2.apply(dve, y[:, t, :], y[:, t, :], t).then_inc(tail, 1)
            dve.wait_ge(tail, NT)
            wide = lambda v: v[:, :].unsqueeze(1).to_broadcast([P, NT, D])
            dve.tensor_tensor(y[:, :, :], y[:, :, :], wide(gamma), ALU.mult).then_inc(tail, 1)
            dve.tensor_tensor(x_sb[:, :, :], x_sb[:, :, :], wide(beta), ALU.add).then_inc(tail, 1)
            dve.wait_ge(tail, NT + 2)
            dve.tensor_tensor(x_sb[:, :, :], x_sb[:, :, :], y[:, :, :], ALU.add).then_inc(tail, 1)
            dve.wait_ge(tail, NT + 3)


def feed_forward(nc, k, x_sb, banks, w):
    HID = 768
    NH = HID // P
    with ExitStack() as ctx:
        tools = Tools(nc, ctx, "ffn")
        sem = lambda name: k.stage_sem("ffn_" + name)
        front = NormTranspose(tools, sem, x_sb, k.ident[:, :], banks[0:2], split=True)
        wi = tools.sb("wi", [P, KD, 2, HID], I32)
        wdi = tools.sb("wdi", [P, NH, D], I32)
        wf = tools.sb("wf", [P, KD, 2, HID])
        wdf = tools.sb("wdf", [P, NH, D])
        wgu = tools.sb("wgu", [P, 2, KD, 2, HID], F32R)
        wd = tools.sb("wd", [P, 2, NH, D], F32R)
        silu = tools.sb("silu", [P, 2, CH])
        hf = tools.sb("hf", [P, 2, CH])
        ht = tools.sb("ht", [P, 2, NH, CH], F32R)
        loads, w_step, wd_step = sem("loads"), sem("w_step"), sem("wd_step")
        gate_psum, up_psum, silu_done, h_done = sem("gate_psum"), sem("up_psum"), sem("silu_done"), sem("h_done")
        hi_done, lo_done, down_psum, x_done = sem("hi_done"), sem("lo_done"), sem("down_psum"), sem("x_done")
        gate_bank, up_bank, down_bank = banks[2:4], banks[4:6], banks[6:8]
        block = ctx.enter_context(nc.Block())

        @block.sync
        def _(sp):
            sp.dma_start(wi[:, :, 0, :], rows(w["L0_ffn_w_gate"])).then_inc(loads, 16)
            sp.dma_start(wi[:, :, 1, :], rows(w["L0_ffn_w_up"])).then_inc(loads, 16)
            sp.dma_start(wdi[:, :, :], rows(w["L0_ffn_w_down"])).then_inc(loads, 16)
            sp.wait_ge(loads, 48)

        @block.gpsimd
        def _(pool):
            front.pool(pool)
            pool.wait_ge(w_step, 2)
            pool.tensor_tensor(wgu[:, 1], wf[:, :], wgu[:, 0].bitcast(F32), ALU.subtract).then_inc(w_step, 1)
            pool.wait_ge(wd_step, 2)
            pool.tensor_tensor(wd[:, 1], wdf[:, :], wd[:, 0].bitcast(F32), ALU.subtract).then_inc(wd_step, 1)

        @block.tensor
        def _(pe):
            front.pe(pe)
            pe.wait_ge(w_step, 3)
            for c in range(NCH):
                pe.wait_ge(front.xt_done, 4 * c + 4)
                for h in range(NH):
                    n = c * NH + h
                    for g, (bank, done, freed) in enumerate(((gate_bank, gate_psum, silu_done), (up_bank, up_psum, h_done))):
                        if n >= 2:
                            pe.wait_ge(freed, n - 1)
                        product3(pe, bank[n % 2][:, :], lambda a, kd: wgu[:, a, kd, g, h * P:(h + 1) * P],
                                 lambda a, kd: front.xt[:, a, kd, c * CH:(c + 1) * CH]).then_inc(done, 1)
                if c == 0:
                    pe.wait_ge(wd_step, 3)
                for tt in range(4):
                    n = 4 * c + tt
                    if n >= 2:
                        pe.wait_ge(x_done, n - 1)
                    for h in range(NH):
                        if tt == 0:
                            pe.wait_ge(lo_done, c * NH + h + 1)
                        for j, (a, b) in enumerate(PASSES):
                            mm = pe.matmul(down_bank[n % 2][:, 0:D], ht[:, a, h, tt * P:(tt + 1) * P], wd[:, b, h, :],
                                           start=h == 0 and j == 0, stop=h == NH - 1 and j == 2)
                    mm.then_inc(down_psum, 1)

        @block.scalar
        def _(act):
            act.wait_ge(w_step, 1)
            act.copy(wgu[:, 0], wf[:, :]).then_inc(w_step, 1)
            act.wait_ge(wd_step, 1)
            act.copy(wd[:, 0], wdf[:, :]).then_inc(wd_step, 1)
            front.act(act)
            for c in range(NCH):
                for h in range(NH):
                    n = c * NH + h
                    act.wait_ge(gate_psum, n + 1)
                    if n >= 2:
                        act.wait_ge(h_done, n - 1)
                    act.activation(silu[:, n % 2, :], gate_bank[n % 2][:, :], ACT.Silu).then_inc(silu_done, 1)
                    act.wait_ge(h_done, n + 1)
                    if c >= 1 and h == 0:
                        act.wait_ge(down_psum, 4 * c)
                    act.copy(ht[:, 0, h, :], hf[:, n % 2, :]).then_inc(hi_done, 1)

        @block.vector
        def _(dve):
            dve.wait_ge(loads, 48)
            dve.tensor_scalar(wf[:, :], wi[:, :], 1.0 / 127.0, None, ALU.mult).then_inc(w_step, 1)
            dve.tensor_scalar(wdf[:, :], wdi[:, :], 1.0 / 127.0, None, ALU.mult).then_inc(wd_step, 1)
            front.dve(dve)

            def residual(c):
                for tt in range(4):
                    n = 4 * c + tt
                    dve.wait_ge(down_psum, n + 1)
                    dve.tensor_tensor(x_sb[:, n, :], x_sb[:, n, :], down_bank[n % 2][:, 0:D], ALU.add).then_inc(x_done, 1)

            for c in range(NCH):
                for h in range(NH):
                    n = c * NH + h
                    dve.wait_ge(silu_done, n + 1)
                    dve.wait_ge(up_psum, n + 1)
                    if n >= 2:
                        dve.wait_ge(hi_done, n - 1)
                        dve.wait_ge(lo_done, n - 1)
                    dve.tensor_tensor(hf[:, n % 2, :], silu[:, n % 2, :], up_bank[n % 2][:, :], ALU.mult).then_inc(h_done, 1)
                    dve.wait_ge(hi_done, n + 1)
                    dve.tensor_tensor(ht[:, 1, h, :], hf[:, n % 2, :], ht[:, 0, h, :].bitcast(F32),
                                      ALU.subtract).then_inc(lo_done, 1)
                residual(c)
            dve.wait_ge(x_done, NT)


def recurrence(nc, k, x_sb, banks, w):
    N = 64
    HALF = T // 2
    SEG = HALF // S
    FORGET = -1e30
    with ExitStack() as ctx:
        tools = Tools(nc, ctx, "rec")
        sem = lambda name: k.stage_sem("rec_" + name)
        lnw, lnb = tools.sb("lnw", [P, KD]), tools.sb("lnb", [P, KD])
        front = NormTranspose(tools, sem, x_sb, k.ident[:, :], banks[0:2], double=True, affine=(lnw, lnb))
        wg = tools.sb("wg", [P, KD, 4, N])
        bias = tools.sb("bias", [P, 4])
        wp = tools.sb("wp", [P, D])
        bp = tools.sb("bp", [P, D])
        log_i, log_f, z, o, d1, m, a, f, c = (tools.sb(n, [P, HALF]) for n in
                                              ("log_i", "log_f", "z", "o", "d1", "m", "a", "f", "c"))
        seg = lambda v: v[:, :].rearrange("p (g s) -> p g s", s=S)
        loads, psum, gate_done = sem("loads"), sem("psum"), sem("gate_done")
        step, expo, zo_done, tanh_done, h_ready = sem("step"), sem("expo"), sem("zo_done"), sem("tanh_done"), sem("h_ready")
        exps_ready = sem("exps_ready")
        out_psum, x_done = sem("out_psum"), sem("x_done")
        gate_bank, out_bank = banks[2:4], banks[4:6]
        block = ctx.enter_context(nc.Block())

        @block.sync
        def _(sp):
            for g, n in enumerate("ifzo"):
                sp.dma_start(wg[:, :, g, :], rows(w[f"L1_attn_W{n}"])).then_inc(loads, 16)
            with nc.allow_non_contiguous_dma(reason="biases as columns"):
                for g, n in enumerate("ifzo"):
                    for half in range(2):
                        sp.dma_start(bias[half * N:(half + 1) * N, g:g + 1],
                                     w[f"L1_attn_b{n}"].rearrange("(p a) -> p a", a=1)).then_inc(loads, 16)
                sp.dma_start(lnw[:, :], column(w["L1_attn_ln_w"])).then_inc(loads, 16)
                sp.dma_start(lnb[:, :], column(w["L1_attn_ln_b"])).then_inc(loads, 16)
            for half in range(2):
                sp.dma_start(wp[half * N:(half + 1) * N, :], w["L1_attn_Wp"]).then_inc(loads, 16)
            sp.dma_start(bp[:, :], everywhere(w["L1_attn_bp"])).then_inc(loads, 16)
            sp.wait_ge(loads, 16 * 17)

        @block.gpsimd
        def _(pool):
            front.pool(pool)

        @block.tensor
        def _(pe):
            front.pe(pe)
            pe.wait_ge(loads, 16 * 17)
            for n in range(8):
                g, c2 = n // 2, n % 2
                if n == 0:
                    pe.wait_ge(front.xt_done, KD * NT)
                if n >= 2:
                    pe.wait_ge(gate_done, n - 1)
                for half in range(2):
                    at = half * HALF + c2 * CH
                    for kd in range(KD):
                        mm = pe.matmul(gate_bank[n % 2][half * N:(half + 1) * N, :], wg[:, kd, g, :],
                                       front.xt[:, 0, kd, at:at + CH], start=kd == 0, stop=kd == KD - 1)
                mm.then_inc(psum, 1)
            pe.wait_ge(h_ready, 1)
            for t in range(NT):
                half, at = t // (NT // 2), t % (NT // 2) * P
                if t >= 2:
                    pe.wait_ge(x_done, t - 1)
                pe.matmul(out_bank[t % 2][:, 0:D], a[half * N:(half + 1) * N, at:at + P],
                          wp[half * N:(half + 1) * N, :], start=True, stop=True).then_inc(out_psum, 1)

        @block.scalar
        def _(act):
            act.wait_ge(loads, 16 * 17)
            front.act(act)
            for n in range(4, 8):
                g, c2 = n // 2, n % 2
                act.wait_ge(psum, n + 1)
                act.wait_ge(gate_done, n)
                act.activation((z if g == 2 else o)[:, c2 * CH:(c2 + 1) * CH], gate_bank[n % 2][:, :],
                               ACT.Tanh if g == 2 else ACT.Sigmoid, bias=bias[:, g:g + 1]).then_inc(gate_done, 1)
            act.wait_ge(exps_ready, 2)
            act.activation(d1[:, :], d1[:, :], ACT.Exp).then_inc(expo, 1)
            act.activation(f[:, :], f[:, :], ACT.Exp).then_inc(expo, 1)
            act.wait_ge(exps_ready, 3)
            act.activation(a[:, :], c[:, :], ACT.Tanh).then_inc(tanh_done, 1)

        @block.vector
        def _(dve):
            front.dve(dve)
            s = Sem(step)
            dve.wait_ge(loads, 16 * 17)
            for n in range(4):
                g, c2 = n // 2, n % 2
                dve.wait_ge(psum, n + 1)
                dve.tensor_scalar((log_f if g else log_i)[:, c2 * CH:(c2 + 1) * CH], gate_bank[n % 2][:, :],
                                  bias[:, g:g + 1], 20.0, ALU.add, ALU.min).then_inc(gate_done, 1)
            dve.wait_ge(gate_done, 4)
            s.give(dve.tensor_scalar(log_i[:, :], log_i[:, :], -20.0, None, ALU.max))
            s.give(dve.tensor_scalar(log_f[:, :], log_f[:, :], -20.0, None, ALU.max))
            dve.wait_ge(step, s.n)
            s.give(dve.tensor_copy(d1[:, :], log_i[:, :]))
            dve.wait_ge(step, s.n)
            s.give(dve.tensor_tensor(seg(d1)[:, :, 0:1], seg(log_i)[:, :, 0:1], seg(log_f)[:, :, 0:1], ALU.max))
            dve.wait_ge(step, s.n)
            s.give(dve.memset(seg(log_f)[:, :, 0:1], FORGET))
            dve.wait_ge(step, s.n)
            s.give(dve.tensor_tensor_scan(m[:, :], log_f[:, :], d1[:, :], 0.0, ALU.add, ALU.max))
            dve.wait_ge(step, s.n)
            dve.tensor_tensor(d1[:, :], log_i[:, :], m[:, :], ALU.subtract).then_inc(exps_ready, 1)
            s.give(dve.tensor_tensor(seg(f)[:, :, 1:S], seg(log_f)[:, :, 1:S], seg(m)[:, :, 0:S - 1], ALU.add))
            s.give(dve.memset(seg(f)[:, :, 0:1], FORGET))
            dve.wait_ge(step, s.n)
            dve.tensor_tensor(f[:, :], f[:, :], m[:, :], ALU.subtract).then_inc(exps_ready, 1)
            dve.wait_ge(expo, 2)
            dve.wait_ge(gate_done, 8)
            s.give(dve.tensor_tensor(d1[:, :], d1[:, :], z[:, :], ALU.mult))
            dve.wait_ge(step, s.n)
            dve.tensor_tensor_scan(c[:, :], f[:, :], d1[:, :], 0.0, ALU.mult, ALU.add).then_inc(exps_ready, 1)
            s.give(dve.tensor_tensor(x_sb[:, :, :], x_sb[:, :, :], bp[:, :].unsqueeze(1).to_broadcast([P, NT, D]), ALU.add))
            dve.wait_ge(tanh_done, 1)
            dve.tensor_tensor(a[:, :], a[:, :], o[:, :], ALU.mult).then_inc(h_ready, 1)
            dve.wait_ge(step, s.n)
            for t in range(NT):
                dve.wait_ge(out_psum, t + 1)
                dve.tensor_tensor(x_sb[:, t, :], x_sb[:, t, :], out_bank[t % 2][:, 0:D], ALU.add).then_inc(x_done, 1)
            dve.wait_ge(x_done, NT)


def masked_attention(nc, k, x_sb, banks, w):
    HD = 16
    HP = 8
    VW = 2 * HD + 2
    KEYS = 2 * S2
    MASKED = 1e20
    with ExitStack() as ctx:
        tools = Tools(nc, ctx, "mat")
        sem = lambda name: k.stage_sem("mat_" + name)
        front = NormTranspose(tools, sem, x_sb, k.ident[:, :], banks[0:2])
        wq, wkr, wvr, wo = (tools.sb(n, [P, KD, D]) for n in ("wq", "wkr", "wvr", "wo"))
        wk, wv = (tools.sb(n, [P, 2, KD, D], F32R) for n in ("wk", "wv"))
        bq, nbq, bk = (tools.sb(n, [P, KD]) for n in ("bq", "nbq", "bk"))
        bv, bo = tools.sb("bv", [P, D]), tools.sb("bo", [P, D])
        mask_i = tools.sb("mask_i", [P, S2], I32)
        mask = tools.sb("mask", [P, S2])
        half_mask = tools.sb("half_mask", [P, 2])
        qf = tools.sb("qf", [P, 2, CH])
        qt = tools.sb("qt", [P, 2, KD, T], F32R)
        ctx_raw = tools.sb("ctx_raw", [P, KD, KEYS])
        ctx_t = tools.sb("ctx_t", [P, 2, KD, KEYS], F32R)
        q_bd = tools.sb("q_bd", [P, 2, 2, KD, 8, S], F32R)
        kt = tools.sb("kt", [P, 2, KD, KEYS], F32R)
        v = tools.sb("v", [P, 2, 4, HP * VW], F32R)
        mark = tools.sb("mark", [P, 1])
        ones = tools.sb("ones", [P, 4 * HP * 2])
        sc = tools.sb("sc", [P, 2, 2, S2])
        neg_max = tools.sb("neg_max", [P, 16])
        p = tools.sb("p", [P, 2, 2, S2])
        pt = tools.sb("pt", [P, 2, 2, 512], F32R)
        rsum = tools.sb("rsum", [P, HP])
        rmask = tools.sb("rmask", [P, HP, 2])
        o = tools.sb("o", [P, D])
        ot = tools.sb("ot", [P, KD, P])
        loads, consts, pre = sem("loads"), sem("consts"), sem("pre")
        w_hi = sem("w_hi")
        q_psum, q_hi, q_f, q_lo = sem("q_psum"), sem("q_hi"), sem("q_f"), sem("q_lo")
        ctx_in, ctx_split, q_bd_ready = sem("ctx_in"), sem("ctx_split"), sem("q_bd_ready")
        proj_psum, proj_hi, proj_lo = sem("proj_psum"), sem("proj_hi"), sem("proj_lo")
        s_psum, s_min, p_ready = sem("s_psum"), sem("s_min"), sem("p_ready")
        pt_psum, pt_hi, pt_lo = sem("pt_psum"), sem("pt_hi"), sem("pt_lo")
        o_psum, o_step, ot_psum, ot_ready = sem("o_psum"), sem("o_step"), sem("ot_psum"), sem("ot_ready")
        wo_psum, x_done = sem("wo_psum"), sem("x_done")
        proj_bank, s_bank, pt_bank, o_bank, end_bank = banks[0:2], banks[2:4], banks[4], banks[5:7], banks[7]
        s_q = -1.0 / HD ** 0.5
        number = lambda i, kind, b: 4 * i + 2 * b + ("k", "v").index(kind)
        bank_of = {"k": proj_bank[0], "v": proj_bank[1]}
        fillers = {0: ("k", 0, 1), 3: ("v", 0, 1), 6: ("k", 1, 0), 7: ("v", 1, 0)}
        block = ctx.enter_context(nc.Block())

        @block.sync
        def _(sp):
            for dst, n in ((wq, "Wq"), (wkr, "Wk"), (wvr, "Wv"), (wo, "Wo")):
                sp.dma_start(dst[:, :, :], rows(w["L1_xattn_" + n])).then_inc(loads, 16)
            with nc.allow_non_contiguous_dma(reason="biases as columns"):
                sp.dma_start(bq[:, :], column(w["L1_xattn_bq"])).then_inc(loads, 16)
                sp.dma_start(bk[:, :], column(w["L1_xattn_bk"])).then_inc(loads, 16)
            sp.dma_start(bv[:, :], everywhere(w["L1_xattn_bv"])).then_inc(loads, 16)
            sp.dma_start(bo[:, :], everywhere(w["L1_xattn_bo"])).then_inc(loads, 16)
            for half in range(2):
                sp.dma_start(mask_i[half * S:(half + 1) * S, :], w["mask_1x1xSxS2_ik1"]).then_inc(loads, 16)
            keys = rows(w["ctx_turned"])
            sp.dma_start(ctx_raw[:, :, :], keys[:, :, 0:KEYS]).then_inc(ctx_in, 16)
            with sp.Fori(1, NT) as i:
                sp.wait_ge(ctx_split, 2 * i)
                sp.dma_start(ctx_raw[:, :, :], keys[:, :, bass.ds(i * KEYS, KEYS)]).then_inc(ctx_in, 16)
            sp.wait_ge(ctx_in, 16 * NT)
            sp.wait_ge(loads, 16 * 10)

        @block.gpsimd
        def _(pool):
            pool.memset(half_mask[:, :], 1.0).then_inc(consts, 1)
            pool.memset(ones[:, :], 1.0).then_inc(consts, 1)
            pool.wait_ge(consts, 2)
            pool.affine_select(out=half_mask[:, 1:2], in_=half_mask[:, 1:2], compare_op=ALU.is_ge, fill=0.0, base=-S,
                               pattern=[[0, 1]], channel_multiplier=1).then_inc(consts, 1)
            pool.affine_select(out=half_mask[:, 0:1], in_=half_mask[:, 0:1], compare_op=ALU.is_ge, fill=0.0, base=S - 1,
                               pattern=[[0, 1]], channel_multiplier=-1).then_inc(consts, 1)
            front.pool(pool)
            per_head = k.head_mask[:, :].unsqueeze(2).to_broadcast([P, 8, S])

            def split_keys(i):
                pool.wait_ge(ctx_split, 2 * i + 1)
                pool.tensor_tensor(ctx_t[:, 1], ctx_raw[:, :, :], ctx_t[:, 0].bitcast(F32), ALU.subtract).then_inc(ctx_split, 1)

            def block_queries(i, b):
                wait(pool, s_psum, 8 * i - 4 + 4 * b)
                for part in range(2):
                    for m in range(KD):
                        pool.tensor_tensor(q_bd[:, b, part, m],
                                           qt[:, part, m, bass.ds(i * P + b * S, S)].bitcast(F32).unsqueeze(1)
                                           .to_broadcast([P, 8, S]), per_head, ALU.mult).then_inc(q_bd_ready, 1)

            split_keys(0)
            pool.wait_ge(q_lo, 2 * KD * NCH // 2)
            block_queries(0, 0)
            block_queries(0, 1)
            with pool.Fori(1, NT) as i:
                split_keys(i)
                block_queries(i, 0)
                block_queries(i, 1)

        @block.tensor
        def _(pe):
            front.pe(pe)
            pe.wait_ge(loads, 16 * 10)
            for n in range(KD * NCH):
                m, c = n % KD, n // KD
                pe.wait_ge(front.xt_done, max(4 * c + 4, NT if n < 2 else 0))
                if n >= 2:
                    pe.wait_ge(q_lo, n - 1)
                for kd in range(KD):
                    mm = pe.matmul(proj_bank[n % 2][:, :], wq[:, kd, m * P:(m + 1) * P],
                                   front.xt[:, 0, kd, c * CH:(c + 1) * CH], start=kd == 0, stop=kd == KD - 1)
                mm.then_inc(q_psum, 1)
            pe.wait_ge(q_lo, KD * NCH)
            pe.wait_ge(pre, 2)

            def keys_proj(i, b):
                if b == 0:
                    pe.wait_ge(ctx_split, 2 * i + 2)
                wait(pe, proj_lo, number(i, "k", b) - 1)
                for m in range(KD):
                    mm = product3(pe, bank_of["k"][:, m * S2:(m + 1) * S2], lambda a, kd: wk[:, a, kd, m * P:(m + 1) * P],
                                  lambda a, kd: ctx_t[:, a, kd, b * S2:(b + 1) * S2])
                mm.then_inc(proj_psum, 1)

            def values_proj(i, b):
                wait(pe, proj_lo, number(i, "v", b) - 1)
                for t in range(2):
                    at = (2 * b + t) * P
                    mm = product3(pe, bank_of["v"][:, t * D:(t + 1) * D], lambda a, kd: ctx_t[:, a, kd, at:at + P],
                                  lambda a, kd: wv[:, a, kd, :])
                mm.then_inc(proj_psum, 1)

            def energies(i, g):
                b, j = g // 4, g % 4
                if j == 0:
                    pe.wait_ge(q_bd_ready, 8 * i + 4 * b + 4)
                    pe.wait_ge(proj_lo, number(i, "k", b) + 1)
                wait(pe, s_min, 2 * (8 * i + g - 1))
                for n in range(2):
                    u = 2 * j + n
                    m, h = u // 4, u % 4 * 2
                    for jj, (a, c) in enumerate(PASSES):
                        mm = pe.matmul(s_bank[g % 2][:, n * S2:(n + 1) * S2],
                                       q_bd[:, b, a, m, h:h + 2, :].rearrange("p h q -> p (h q)"),
                                       kt[:, c, m, b * S2:(b + 1) * S2], start=jj == 0, stop=jj == 2)
                mm.then_inc(s_psum, 1)

            def turn(i, g):
                pe.wait_ge(p_ready, 2 * (8 * i + g) + 2)
                wait(pe, pt_lo, 8 * i + g)
                for n in range(2):
                    for t in range(2):
                        mm = pe.transpose(pt_bank[:, (2 * n + t) * P:(2 * n + t + 1) * P], p[:, g % 2, n, t * P:(t + 1) * P],
                                          k.ident[:, :])
                mm.then_inc(pt_psum, 1)

            def weigh(i, g):
                b, j = g // 4, g % 4
                pe.wait_ge(pt_lo, 8 * i + g + 1)
                if j == 0:
                    pe.wait_ge(proj_lo, number(i, "v", b) + 1)
                    wait(pe, o_step, 8 * i - 5 + 4 * b if not isinstance(i, int) or i > 0 else 0)
                for n in range(2):
                    u = 2 * j + n
                    for t in range(2):
                        for jj, (a, c) in enumerate(PASSES):
                            mm = pe.matmul(o_bank[b][:, u * VW:(u + 1) * VW], pt[:, g % 2, a, (2 * n + t) * P:(2 * n + t + 1) * P],
                                           v[:, c, 2 * b + t, u * VW:(u + 1) * VW], start=t == 0 and jj == 0,
                                           stop=t == 1 and jj == 2)
                if j == 3:
                    mm.then_inc(o_psum, 1)

            def turn_output(i, b):
                pe.wait_ge(o_step, 4 * (2 * i + b) + 4)
                wait(pe, ot_ready, 2 * i + b)
                wait(pe, x_done, i)
                for m in range(KD):
                    mm = pe.transpose(end_bank[:, m * P:(m + 1) * P], o[:, m * P:(m + 1) * P], k.ident[:, :])
                mm.then_inc(ot_psum, 1)

            def project_output(i):
                pe.wait_ge(ot_ready, 2 * i + 2)
                for kd in range(KD):
                    mm = pe.matmul(end_bank[:, 0:D], ot[:, kd, :], wo[:, kd, :], start=kd == 0, stop=kd == KD - 1)
                mm.then_inc(wo_psum, 1)

            def slot(i, g, first):
                before = (lambda back: (i, g - back) if g >= back else (i - 1, g + 8 - back))
                if g >= 2 or not first:
                    turn(*before(2))
                energies(i, g)
                if g >= 3 or not first:
                    weigh(*before(3))

            def outputs(i, g):
                if g == 0:
                    turn_output(i - 1, 0)
                if g == 4:
                    turn_output(i - 1, 1)
                if g == 5:
                    project_output(i - 1)

            def pair(i, first=False, last=False):
                for g in range(8):
                    slot(i, g, first)
                    if not first:
                        outputs(i, g)
                    if g in fillers:
                        kind, ahead, b = fillers[g]
                        if not (ahead and last):
                            (keys_proj if kind == "k" else values_proj)(i + ahead, b)

            keys_proj(0, 0)
            values_proj(0, 0)
            pair(0, first=True)
            with pe.Fori(1, NT - 1) as i:
                pair(i)
            pair(NT - 1, last=True)
            for g in range(3):
                if g < 2:
                    turn(NT - 1, g + 6)
                weigh(NT - 1, g + 5)
            for g in (0, 4, 5):
                outputs(NT, g)

        @block.scalar
        def _(act):
            act.wait_ge(loads, 16 * 10)
            act.copy(wk[:, 0], wkr[:, :, :]).then_inc(w_hi, 1)
            act.copy(wv[:, 0], wvr[:, :, :]).then_inc(w_hi, 1)
            front.act(act)
            act.wait_ge(pre, 1)
            for n in range(KD * NCH):
                m, c = n % KD, n // KD
                act.wait_ge(q_psum, n + 1)
                if n >= 2:
                    act.wait_ge(q_lo, n - 1)
                act.activation(qf[:, n % 2, :], proj_bank[n % 2][:, :], ACT.Identity, bias=nbq[:, m:m + 1],
                               scale=s_q).then_inc(q_f, 1)

            def keys_proj(i, b):
                act.wait_ge(proj_psum, number(i, "k", b) + 1)
                for m in range(KD):
                    ins = act.activation(kt[:, 0, m, b * S2:(b + 1) * S2], bank_of["k"][:, m * S2:(m + 1) * S2],
                                         ACT.Identity, bias=bk[:, m:m + 1])
                ins.then_inc(proj_hi, 1)

            def values_proj(i, b):
                act.wait_ge(proj_psum, number(i, "v", b) + 1)
                for t in range(2):
                    ins = act.copy(v[:, 0, 2 * b + t, :].rearrange("p (u e) -> p u e", e=VW)[:, :, 0:2 * HD],
                                   bank_of["v"][:, t * D:(t + 1) * D].rearrange("p (u e) -> p u e", e=2 * HD))
                ins.then_inc(proj_hi, 1)

            def weights(i, g):
                for n in range(2):
                    u = 2 * g + n
                    act.wait_ge(s_min, 16 * i + u + 1)
                    act.activation(p[:, g % 2, n, :], sc[:, g % 2, n, :], ACT.Exp, bias=neg_max[:, u:u + 1],
                                   scale=-1.0).then_inc(p_ready, 1)

            def turn(i, g):
                act.wait_ge(pt_psum, 8 * i + g + 1)
                act.copy(pt[:, g % 2, 0, :], pt_bank[:, :]).then_inc(pt_hi, 1)

            def pair(i, first=False):
                for g in range(8):
                    if g == 0 and not first:
                        values_proj(i, 0)
                    if g - 1 in fillers:
                        kind, ahead, b = fillers[g - 1]
                        if ahead == 0 or not isinstance(i, int) or i < NT - 1:
                            (keys_proj if kind == "k" else values_proj)(i + ahead, b)
                    if g >= 2 or not first:
                        turn(*((i, g - 2) if g >= 2 else (i - 1, g + 6)))
                    weights(i, g)

            keys_proj(0, 0)
            values_proj(0, 0)
            pair(0, first=True)
            with act.Fori(1, NT - 1) as i:
                pair(i)
            pair(NT - 1)
            turn(NT - 1, 6)
            turn(NT - 1, 7)

        @block.vector
        def _(dve):
            dve.wait_ge(loads, 16 * 10)
            dve.tensor_scalar(nbq[:, :], bq[:, :], s_q, None, ALU.mult).then_inc(pre, 1)
            s = Sem(sem("vec_pre"))
            dve.wait_ge(w_hi, 2)
            s.give(dve.tensor_tensor(wk[:, 1], wkr[:, :, :], wk[:, 0].bitcast(F32), ALU.subtract))
            s.give(dve.tensor_tensor(wv[:, 1], wvr[:, :, :], wv[:, 0].bitcast(F32), ALU.subtract))
            dve.wait_ge(consts, 4)
            s.give(dve.tensor_scalar(mask[:, :], mask_i[:, :], 0.0, MASKED, ALU.is_equal, ALU.mult))
            s.give(dve.tensor_tensor(bv[:, :].rearrange("p (u h e) -> p u h e", h=2, e=HD),
                                     bv[:, :].rearrange("p (u h e) -> p u h e", h=2, e=HD),
                                     half_mask[:, :].unsqueeze(1).unsqueeze(3).to_broadcast([P, HP, 2, HD]), ALU.mult))
            for part in range(2):
                dst = v[:, part].rearrange("p t (u e) -> p (t u) e", e=VW)[:, :, 2 * HD:VW]
                if part == 0:
                    s.give(dve.tensor_copy(dst, ones[:, :].rearrange("p (t e) -> p t e", e=2)))
                else:
                    s.give(dve.tensor_scalar(dst, ones[:, :].rearrange("p (t e) -> p t e", e=2), 0.0, None, ALU.mult))
            dve.wait_ge(s.sem, s.n)
            dve.engine_nop().then_inc(pre, 1)
            front.dve(dve)
            dve.wait_ge(front.xn_ready, NT)
            dve.tensor_tensor(x_sb[:, :, :], x_sb[:, :, :], bo[:, :].unsqueeze(1).to_broadcast([P, NT, D]),
                              ALU.add).then_inc(q_hi, 1)
            for n in range(KD * NCH):
                m, c = n % KD, n // KD
                dve.wait_ge(q_f, n + 1)
                dve.tensor_copy(qt[:, 0, m, c * CH:(c + 1) * CH], qf[:, n % 2, :]).then_inc(q_hi, 1)
                dve.wait_ge(q_hi, n + 2)
                dve.tensor_tensor(qt[:, 1, m, c * CH:(c + 1) * CH], qf[:, n % 2, :],
                                  qt[:, 0, m, c * CH:(c + 1) * CH].bitcast(F32), ALU.subtract).then_inc(q_lo, 1)

            def keys_proj(i, b):
                dve.wait_ge(proj_hi, number(i, "k", b) + 1)
                for m in range(KD):
                    cols = lambda part: kt[:, part, m, b * S2:(b + 1) * S2]
                    ins = dve.scalar_tensor_tensor(out=cols(1), in0=bank_of["k"][:, m * S2:(m + 1) * S2],
                                                   scalar=bk[:, m:m + 1], in1=cols(0).bitcast(F32), op0=ALU.add,
                                                   op1=ALU.subtract)
                ins.then_inc(proj_lo, 1)

            def values_proj(i, b):
                dve.wait_ge(proj_hi, number(i, "v", b) + 1)
                cols = lambda part: v[:, part, 2 * b:2 * b + 2, :].rearrange(
                    "p t (u e) -> p (t u) e", e=VW)[:, :, 0:2 * HD]
                dve.tensor_tensor(cols(1), bank_of["v"][:, :].rearrange("p (u e) -> p u e", e=2 * HD),
                                  cols(0).bitcast(F32), ALU.subtract).then_inc(proj_lo, 1)

            def energies(i, g):
                dve.wait_ge(s_psum, 8 * i + g + 1)
                wait(dve, p_ready, 2 * (8 * i + g - 1))
                dve.memset(mark[:, :], 0.0)
                for n in range(2):
                    u = 2 * g + n
                    dve.tensor_tensor_reduce(sc[:, g % 2, n, :], s_bank[g % 2][:, n * S2:(n + 1) * S2], mask[:, :],
                                             1.0, 3e38, ALU.add, ALU.min, neg_max[:, u:u + 1]).then_inc(s_min, 1)

            def turn(i, g):
                dve.wait_ge(pt_hi, 8 * i + g + 1)
                dve.tensor_tensor(pt[:, g % 2, 1, :], pt_bank[:, :], pt[:, g % 2, 0, :].bitcast(F32),
                                  ALU.subtract).then_inc(pt_lo, 1)

            def normalise(i, b):
                done = 4 * (2 * i + b)
                dve.wait_ge(o_psum, 2 * i + b + 1)
                src = o_bank[b][:, 0:HP * VW].rearrange("p (u e) -> p u e", e=VW)
                dve.reciprocal(rsum[:, :], src[:, :, 2 * HD]).then_inc(o_step, 1)
                dve.wait_ge(o_step, done + 1)
                dve.tensor_tensor(rmask[:, :, :], rsum[:, :].unsqueeze(2).to_broadcast([P, HP, 2]),
                                  half_mask[:, :].unsqueeze(1).to_broadcast([P, HP, 2]), ALU.mult).then_inc(o_step, 1)
                dve.wait_ge(o_step, done + 2)
                dve.tensor_tensor(o[:, :].rearrange("p (u h e) -> p u h e", h=2, e=HD),
                                  src[:, :, 0:2 * HD].rearrange("p u (h e) -> p u h e", h=2),
                                  rmask[:, :, :].unsqueeze(3).to_broadcast([P, HP, 2, HD]), ALU.mult).then_inc(o_step, 1)
                dve.wait_ge(o_step, done + 3)
                dve.tensor_tensor(o[:, :], o[:, :], bv[:, :], ALU.add).then_inc(o_step, 1)

            def turn_output(i, b):
                dve.wait_ge(ot_psum, 2 * i + b + 1)
                dve.tensor_reduce(ot[:, :, b * S:(b + 1) * S],
                                  end_bank[:, 0:KD * P].rearrange("p (m h q) -> p m q h", m=KD, h=2),
                                  AX.X, ALU.add).then_inc(ot_ready, 1)

            def residual(i):
                dve.wait_ge(wo_psum, i + 1)
                row = x_sb[:, bass.ds(i, 1), :].rearrange("p a d -> p (a d)")
                dve.tensor_tensor(row, row, end_bank[:, 0:D], ALU.add).then_inc(x_done, 1)

            def split_keys(i):
                dve.wait_ge(ctx_in, 16 * i + 16)
                dve.tensor_copy(ctx_t[:, 0], ctx_raw[:, :, :]).then_inc(ctx_split, 1)

            def outputs(i, g):
                if g == 0:
                    turn_output(i - 1, 0)
                if g == 3:
                    normalise(i - 1, 1)
                if g == 4:
                    turn_output(i - 1, 1)
                if g == 5:
                    residual(i - 1)

            def pair(i, first=False, last=False):
                for g in range(8):
                    if g == 0 and not first:
                        values_proj(i, 0)
                    if g - 1 in fillers:
                        kind, ahead, b = fillers[g - 1]
                        if not (ahead and last):
                            (keys_proj if kind == "k" else values_proj)(i + ahead, b)
                    if g == 4 and not last:
                        split_keys(i + 1)
                    if g >= 2 or not first:
                        turn(*((i, g - 2) if g >= 2 else (i - 1, g + 6)))
                    energies(i, g)
                    if not first:
                        outputs(i, g)
                    if g == 7:
                        normalise(i, 0)

            split_keys(0)
            keys_proj(0, 0)
            values_proj(0, 0)
            pair(0, first=True)
            with dve.Fori(1, NT - 1) as i:
                pair(i)
            pair(NT - 1, last=True)
            turn(NT - 1, 6)
            turn(NT - 1, 7)
            for g in (0, 3, 4, 5):
                outputs(NT, g)
            dve.wait_ge(x_done, NT)


def experts(nc, k, x_sb, banks, w):
    E, F = 8, 1024
    NF = F // P
    BISECTIONS = 25
    THRESH = 1e-9
    STEPS = NCH * NF
    with ExitStack() as ctx:
        tools = Tools(nc, ctx, "moe")
        sem = lambda name: k.stage_sem("moe_" + name)
        front = NormTranspose(tools, sem, x_sb, k.ident[:, :], banks[0:2], split=True)
        acc = front.xn[:, :, :].rearrange("p t d -> p (t d)").rearrange("p (m n) -> p m n", m=KD)
        wr, wrs = tools.sb("wr", [P, KD, E]), tools.sb("wrs", [P, 2, KD, E], F32R)
        br = tools.sb("br", [P, E])
        xs, dif, sq = (tools.sb(n, [P, NT, E]) for n in ("xs", "dif", "sq"))
        top, tau, dm, tau_m, f_lo, f_m, inc = (tools.sb(n, [P, NT]) for n in
                                               ("top", "tau", "dm", "tau_m", "f_lo", "f_m", "inc"))
        gates_t = tools.sb("gates_t", [P, P])
        gate8 = tools.sb("gate8", [E, T])
        b1r, b1 = tools.sb("b1r", [E * NF, P]), tools.sb("b1", [P, E * NF])
        b1e = tools.sb("b1e", [P, 2, NF])
        b2 = tools.sb("b2", [E, D])
        w1raw, w2raw = tools.sb("w1raw", [P, 2, KD, F]), tools.sb("w2raw", [P, 2, NF, D])
        w1, w2 = tools.sb("w1", [P, 2, 2, KD, F], F32R), tools.sb("w2", [P, 2, 2, NF, D], F32R)
        gate_all = tools.sb("gate_all", [P, 2, NT, P])
        h, hr = tools.sb("h", [P, 2, 2, CH], F32R), tools.sb("hr", [P, 2, CH])
        weighted = tools.sb("weighted", [P, 2, CH])
        loads, w_in, gate_in = sem("loads"), [sem("w_in0"), sem("w_in1")], [sem("gate_in0"), sem("gate_in1")]
        small_psum, small_done = sem("small_psum"), sem("small_done")
        split_step, ent, gates_ready = sem("split_step"), sem("ent"), sem("gates_ready")
        gate_stored, gate8_in = sem("gate_stored"), sem("gate8_in")
        acc_psum, acc_done = sem("acc_psum"), sem("acc_done")
        w_hi, w_lo, b1_cols = sem("w_hi"), sem("w_lo"), sem("b1_cols")
        h_psum, h_hi, h_relu, h_lo = sem("h_psum"), sem("h_hi"), sem("h_relu"), sem("h_lo")
        y_psum, y_weighted, acc_step = sem("y_psum"), sem("y_weighted"), sem("acc_step")
        back_psum, x_done = sem("back_psum"), sem("x_done")
        h_bank = [banks[0], banks[1], banks[6], banks[7]]
        y_bank = banks[2:6]
        small = banks[2]
        block = ctx.enter_context(nc.Block())

        @block.sync
        def _(sp):
            with nc.allow_non_contiguous_dma(reason="the router's weights are narrow"):
                sp.dma_start(wr[:, :, :], rows(w["L1_ffn_Wr"])).then_inc(loads, 16)
            sp.dma_start(br[:, :], everywhere(w["L1_ffn_br"])).then_inc(loads, 16)
            sp.dma_start(b1r[:, :], w["L1_ffn_b1"].rearrange("e (f p) -> (e f) p", p=P)).then_inc(loads, 16)
            sp.dma_start(b2[:, :], w["L1_ffn_b2"]).then_inc(loads, 16)

            def load_weights(e, par):
                wait(sp, w_lo, 2 * e - 2)
                wait(sp, w_hi, 2 * e - 2)
                sp.dma_start(w1raw[:, par], w["L1_ffn_W1"][bass.ds(e, 1), :, :].rearrange(
                    "a (k p) n -> p (a k) n", p=P)).then_inc(w_in[par], 16)
                sp.dma_start(w2raw[:, par], w["L1_ffn_W2"][bass.ds(e, 1), :, :].rearrange(
                    "a (k p) n -> p (a k) n", p=P)).then_inc(w_in[par], 16)

            def load_gates(e, par):
                wait(sp, y_weighted, 8 * e - 8)
                sp.dma_start(gate_all[:, par], k.scratch[:, bass.ds(e, 1), :].rearrange("t a p -> (t a) p")
                             .partition_broadcast(P)).then_inc(gate_in[par], 16)

            load_weights(0, 0)
            load_weights(1, 1)
            sp.wait_ge(gates_ready, 2)
            sp.dma_start(k.scratch.rearrange("t e p -> (t e) p"), gates_t[:, :]).then_inc(gate_stored, 16)
            sp.wait_ge(gate_stored, 16)
            sp.dma_start(gate8[:, :].rearrange("e (t p) -> e t p", p=P),
                         k.scratch.rearrange("t e p -> e t p")).then_inc(gate8_in, 16)
            load_gates(0, 0)
            load_gates(1, 1)
            with sp.Fori(1, E // 2) as i:
                for par in range(2):
                    load_weights(2 * i + par, par)
                    load_gates(2 * i + par, par)
            for par in range(2):
                sp.wait_ge(w_in[par], 32 * (E // 2))
                sp.wait_ge(gate_in[par], 16 * (E // 2))
            sp.wait_ge(loads, 64)
            sp.wait_ge(gate8_in, 16)

        @block.gpsimd
        def _(pool):
            front.pool(pool)

            def split_weights(i, par):
                e = 2 * i + par
                pool.wait_ge(w_in[par], 32 * i + 32)
                pool.wait_ge(w_hi, 2 * e + 1)
                pool.tensor_tensor(w1[:, par, 1], w1raw[:, par], w1[:, par, 0].bitcast(F32), ALU.subtract).then_inc(w_lo, 1)
                pool.tensor_copy(b1e[:, par, :], b1[:, bass.ds(e * NF, NF)]).then_inc(b1_cols, 1)
                pool.wait_ge(w_hi, 2 * e + 2)
                pool.tensor_tensor(w2[:, par, 1], w2raw[:, par], w2[:, par, 0].bitcast(F32), ALU.subtract).then_inc(w_lo, 1)

            pool.wait_ge(small_done, 1)
            with pool.Fori(0, E // 2) as i:
                for par in range(2):
                    split_weights(i, par)

        @block.tensor
        def _(pe):
            front.pe(pe)
            pe.wait_ge(loads, 64)
            pe.wait_ge(split_step, 2)
            pe.wait_ge(front.xt_done, NT)
            for t in range(NT):
                mm = product3(pe, small[:, t * E:(t + 1) * E], lambda a, kd: front.xt[:, a, kd, t * P:(t + 1) * P],
                              lambda a, kd: wrs[:, a, kd, :])
            mm.then_inc(small_psum, 1)
            pe.transpose(banks[3][:, 0:E * NF], b1r[:, :], k.ident[0:E * NF, 0:E * NF]).then_inc(small_psum, 1)
            pe.wait_ge(gates_ready, 1)
            pe.transpose(banks[4][:, 0:P], xs[:, :, :].rearrange("p t e -> p (t e)"), k.ident[:, :]).then_inc(small_psum, 1)
            pe.wait_ge(gate8_in, 16)
            pe.wait_ge(small_done, 1)
            for n in range(KD * NCH):
                m, c = n % KD, n // KD
                if n >= 2:
                    pe.wait_ge(acc_done, n - 1)
                pe.matmul(banks[2 + n % 2][:, :], b2[:, m * P:(m + 1) * P], gate8[:, c * CH:(c + 1) * CH],
                          start=True, stop=True).then_inc(acc_psum, 1)
            pe.wait_ge(acc_done, KD * NCH)

            def hidden(e, par, n):
                c, f = n // NF, n % NF
                if n == 0:
                    pe.wait_ge(w_lo, 2 * e + 1)
                step = STEPS * e + n
                wait(pe, h_relu, step - 3)
                product3(pe, h_bank[n % 4][:, :], lambda a, kd: w1[:, par, a, kd, f * P:(f + 1) * P],
                         lambda a, kd: front.xt[:, a, kd, c * CH:(c + 1) * CH]).then_inc(h_psum, 1)

            def output(e, par, n):
                c, f = n // NF, n % NF
                if n == 0:
                    pe.wait_ge(w_lo, 2 * e + 2)
                pe.wait_ge(h_lo, STEPS * e + n + 1)
                if f == 0:
                    wait(pe, y_weighted, 2 * (NCH * e + c) - 2)
                for m in range(KD):
                    for j, (a, b) in enumerate(PASSES):
                        mm = pe.matmul(y_bank[c % 2 * 2 + m][:, :], w2[:, par, a, f, m * P:(m + 1) * P], h[:, n % 2, b, :],
                                       start=f == 0 and j == 0, stop=f == NF - 1 and j == 2)
                if f == NF - 1:
                    mm.then_inc(y_psum, 1)

            def two_experts(i):
                for n in range(2 * STEPS):
                    hidden(2 * i + n // STEPS, n // STEPS, n % STEPS)
                    if n >= 1:
                        output(2 * i + (n - 1) // STEPS, (n - 1) // STEPS, (n - 1) % STEPS)
                output(2 * i + 1, 1, STEPS - 1)

            two_experts(0)
            with pe.Fori(1, E // 2) as i:
                two_experts(i)
            pe.wait_ge(acc_step, KD * NCH * E)
            for t in range(NT):
                if t >= 2:
                    pe.wait_ge(x_done, t - 1)
                for m in range(KD):
                    mm = pe.transpose(banks[t % 2][:, m * P:(m + 1) * P], acc[:, m, t * P:(t + 1) * P], k.ident[:, :])
                mm.then_inc(back_psum, 1)

        @block.scalar
        def _(act):
            front.act(act)
            act.wait_ge(loads, 64)
            act.copy(wrs[:, 0], wr[:, :, :]).then_inc(split_step, 1)

            def split_weights(i, par):
                e = 2 * i + par
                act.wait_ge(w_in[par], 32 * i + 32)
                wait(act, y_psum, NCH * (e - 1))
                act.copy(w1[:, par, 0], w1raw[:, par]).then_inc(w_hi, 1)
                act.copy(w2[:, par, 0], w2raw[:, par]).then_inc(w_hi, 1)

            split_weights(0, 0)
            act.wait_ge(small_psum, 2)
            act.copy(b1[:, :], banks[3][:, 0:E * NF]).then_inc(small_done, 1)
            act.wait_ge(small_psum, 3)
            act.copy(gates_t[:, :], banks[4][:, 0:P]).then_inc(gates_ready, 1)
            for n in range(KD * NCH):
                m, c = n % KD, n // KD
                act.wait_ge(acc_psum, n + 1)
                act.copy(acc[:, m, c * CH:(c + 1) * CH], banks[2 + n % 2][:, :]).then_inc(acc_done, 1)
            act.wait_ge(small_done, 1)

            def two_experts(i, last=False):
                for par in range(2):
                    e = 2 * i + par
                    for n in range(STEPS):
                        if n == 0:
                            act.wait_ge(b1_cols, e + 1)
                        wait(act, h_lo, STEPS * e + n - 1)
                        act.wait_ge(h_psum, STEPS * e + n + 1)
                        act.activation(hr[:, n % 2, :], h_bank[n % 4][:, :], ACT.Relu,
                                       bias=b1e[:, par, n % NF:n % NF + 1]).then_inc(h_relu, 1)
                        if n == STEPS // 2 and not (last and par == 1):
                            split_weights(i + par, 1 - par)

            two_experts(0)
            with act.Fori(1, E // 2 - 1) as i:
                two_experts(i)
            two_experts(E // 2 - 1, last=True)

        @block.vector
        def _(dve):
            front.dve(dve)
            dve.wait_ge(loads, 64)
            dve.wait_ge(split_step, 1)
            dve.tensor_tensor(wrs[:, 1], wr[:, :, :], wrs[:, 0].bitcast(F32), ALU.subtract).then_inc(split_step, 1)
            s = Sem(ent)
            each = lambda v: v[:, :].unsqueeze(2).to_broadcast([P, NT, E])

            def go(ins):
                s.give(ins)
                dve.wait_ge(ent, s.n)

            dve.wait_ge(small_psum, 1)
            go(dve.tensor_tensor(xs[:, :, :], small[:, 0:NT * E].rearrange("p (t e) -> p t e", e=E),
                                 br[:, :].unsqueeze(1).to_broadcast([P, NT, E]), ALU.add))
            go(dve.tensor_scalar(xs[:, :, :], xs[:, :, :], 0.5, None, ALU.mult))
            go(dve.tensor_reduce(top[:, :], xs[:, :, :], AX.X, ALU.max))
            s.give(dve.tensor_scalar(tau[:, :], top[:, :], 1.0, None, ALU.subtract))
            go(dve.tensor_scalar(dm[:, :], top[:, :], (1.0 / E) ** 0.5, None, ALU.subtract))
            go(dve.tensor_tensor(dm[:, :], dm[:, :], tau[:, :], ALU.subtract))
            go(dve.tensor_tensor(dif[:, :, :], xs[:, :, :], each(tau), ALU.subtract))
            go(dve.scalar_tensor_tensor(out=sq[:, :, :], in0=dif[:, :, :], scalar=0.0, in1=dif[:, :, :],
                                        op0=ALU.max, op1=ALU.mult))
            go(dve.tensor_reduce(f_lo[:, :], sq[:, :, :], AX.X, ALU.add))
            go(dve.tensor_scalar(f_lo[:, :], f_lo[:, :], 1.0, None, ALU.subtract))
            base, per = s.n, 8
            with dve.Fori(0, BISECTIONS) as it:
                def then(n, ins, it=it):
                    ins.then_inc(ent, 1)
                    dve.wait_ge(ent, it * per + (base + n))

                then(1, dve.tensor_scalar(dm[:, :], dm[:, :], 0.5, None, ALU.mult))
                then(2, dve.tensor_tensor(tau_m[:, :], tau[:, :], dm[:, :], ALU.add))
                then(3, dve.tensor_tensor(dif[:, :, :], xs[:, :, :], each(tau_m), ALU.subtract))
                then(4, dve.scalar_tensor_tensor(out=sq[:, :, :], in0=dif[:, :, :], scalar=0.0, in1=dif[:, :, :],
                                                 op0=ALU.max, op1=ALU.mult))
                then(5, dve.tensor_reduce(f_m[:, :], sq[:, :, :], AX.X, ALU.add))
                then(6, dve.scalar_tensor_tensor(out=f_m[:, :], in0=f_m[:, :], scalar=1.0, in1=f_lo[:, :],
                                                 op0=ALU.subtract, op1=ALU.mult))
                then(7, dve.scalar_tensor_tensor(out=inc[:, :], in0=f_m[:, :], scalar=0.0, in1=dm[:, :],
                                                 op0=ALU.is_ge, op1=ALU.mult))
                then(8, dve.tensor_tensor(tau[:, :], tau[:, :], inc[:, :], ALU.add))
            s.n = base + per * BISECTIONS
            go(dve.tensor_reduce(f_m[:, :], sq[:, :, :], AX.X, ALU.add))
            go(dve.reciprocal(f_m[:, :], f_m[:, :]))
            go(dve.tensor_tensor(dif[:, :, :], sq[:, :, :], each(f_m), ALU.mult))
            dve.scalar_tensor_tensor(out=xs[:, :, :], in0=dif[:, :, :], scalar=THRESH, in1=dif[:, :, :],
                                     op0=ALU.is_gt, op1=ALU.mult).then_inc(gates_ready, 1)
            dve.wait_ge(acc_done, KD * NCH)
            dve.wait_ge(small_done, 1)

            def hidden(i, par, n):
                e = 2 * i + par
                step = STEPS * e + n
                dve.wait_ge(h_relu, step + 1)
                dve.tensor_copy(h[:, n % 2, 0, :], hr[:, n % 2, :]).then_inc(h_hi, 1)
                dve.wait_ge(h_hi, step + 1)
                dve.tensor_tensor(h[:, n % 2, 1, :], hr[:, n % 2, :], h[:, n % 2, 0, :].bitcast(F32),
                                  ALU.subtract).then_inc(h_lo, 1)

            def add_output(i, par, c):
                e = 2 * i + par
                chunk = NCH * e + c
                if c == 0:
                    dve.wait_ge(gate_in[par], 16 * i + 16)
                dve.wait_ge(y_psum, chunk + 1)
                for m in range(KD):
                    dve.tensor_tensor(weighted[:, m, :], y_bank[c % 2 * 2 + m][:, :],
                                      gate_all[:, par, 4 * c:4 * c + 4, :].rearrange("p t n -> p (t n)"),
                                      ALU.mult).then_inc(y_weighted, 1)
                for m in range(KD):
                    dve.wait_ge(y_weighted, 2 * chunk + 1 + m)
                    dve.tensor_tensor(acc[:, m, c * CH:(c + 1) * CH], acc[:, m, c * CH:(c + 1) * CH], weighted[:, m, :],
                                      ALU.add).then_inc(acc_step, 1)

            def two_experts(i):
                for n in range(2 * STEPS):
                    hidden(i, n // STEPS, n % STEPS)
                    if n % NF == 1 and n > NF:
                        done = n // NF - 1
                        add_output(i, done // NCH, done % NCH)
                add_output(i, 1, NCH - 1)

            with dve.Fori(0, E // 2) as i:
                two_experts(i)
            for t in range(NT):
                dve.wait_ge(back_psum, t + 1)
                dve.tensor_tensor(x_sb[:, t, :], x_sb[:, t, :], banks[t % 2][:, 0:D], ALU.add).then_inc(x_done, 1)
            dve.wait_ge(x_done, NT)


def latent_attention(nc, k, x_sb, banks, w):
    INNER = 1024
    HD = 64
    NU = INNER // P
    KT = 5
    LK = S2 + S
    ALL = KT * P
    PROJ = 34
    with ExitStack() as ctx:
        tools = Tools(nc, ctx, "lat")
        sem = lambda name: k.stage_sem("lat_" + name)
        norm_x = NormStats(tools, NT, sem("x_stats"), sem("x_rstd"), "x")
        norm_c = NormStats(tools, 4, sem("c_stats"), sem("c_rstd"), "c")
        xl = tools.sb("xl", [P, NT, D])
        g_kv, b_kv, g_l, b_l = (tools.sb(n, [P, KD]) for n in ("g_kv", "b_kv", "g_l", "b_l"))
        wq, wk, wv = (tools.sb(n, [P, 2, KD, INNER], F32R) for n in ("wq", "wk", "wv"))
        wo = tools.sb("wo", [P, 2, NU, D], F32R)
        ctx_raw = tools.sb("ctx_raw", [P, 4, D])
        ctx_n = tools.sb("ctx_n", [P, 4, D])
        kv_t = tools.sb("kv_t", [P, 2, KD, 6 * P], F32R)
        kv_f = tools.sb("kv_f", [P, 2, 512])
        q_bd = tools.sb("q_bd", [P, 2, 2, NU, P], F32R)
        kt = tools.sb("kt", [P, 2, 2, ALL], F32R)
        v = tools.sb("v", [P, 2, 2, KT, 2 * P], F32R)
        p = tools.sb("p", [P, 4, 3 * P])
        pt = tools.sb("pt", [P, 2, 2, 3 * P], F32R)
        at = tools.sb("at", [P, 2, NU, P], F32R)
        raw = [xl[:, :, :].rearrange("p t d -> p (t d)")[:, n * KD * INNER:(n + 1) * KD * INNER] for n in range(2)]
        neg_max, rsum, rinv = (tools.sb(n, [P, 16]) for n in ("neg_max", "rsum", "rinv"))
        loads, consts, w_hi, w_lo = sem("loads"), sem("consts"), sem("w_hi"), sem("w_lo")
        w_in = [sem("w_in0"), sem("w_in1")]
        ctx_in, ctx_ready, xl_ready = sem("ctx_in"), sem("ctx_ready"), sem("xl_ready")
        proj_psum, proj_hi, proj_f, proj_lo = sem("proj_psum"), sem("proj_hi"), sem("proj_f"), sem("proj_lo")
        s_psum, s_max, p_exp, p_inv, p_ready = sem("s_psum"), sem("s_max"), sem("p_exp"), sem("p_inv"), sem("p_ready")
        pt_psum, pt_hi, pt_lo = sem("pt_psum"), sem("pt_hi"), sem("pt_lo")
        o_psum, o_hi, o_lo, wo_psum, x_done = sem("o_psum"), sem("o_hi"), sem("o_lo"), sem("wo_psum"), sem("x_done")
        proj_bank, s_bank, pt_bank, o_bank, wo_bank = banks[0:2], banks[2:4], banks[4], banks[5:7], banks[7]
        weights = ((wq, "L0_xattn_Wq", 0), (wk, "L0_xattn_Wkv", 0), (wv, "L0_xattn_Wkv", INNER), (wo, "L0_xattn_Wo", None))

        def fillers(u):
            steps = []
            hp = u // 2 + 1
            if hp < NU:
                steps.append(("k", hp, u % 2))
            if u % 4 < 3:
                steps.append(("v", u // 4, u % 4))
            return steps

        def numbered():
            steps = [("t", kd, n) for kd in range(KD) for n in range(2)] + [("q", 0, 0), ("q", 1, 0), ("k", 0, 0), ("k", 0, 1)]
            for u in range(16):
                steps += fillers(u)
            assert len(steps) == PROJ
            return {s: n for n, s in enumerate(steps)}

        number = numbered()
        HI = PROJ - 4 + 2

        def hi_number(n):
            return n + 1 - 4 + 2

        def both_contexts(part, kd):
            return kv_t[:, part, kd, :].rearrange("p (n c) -> p n c", n=2)[:, :, 0:2 * P]

        xl_now = tools.sb("xl_now", [P, D])

        block = ctx.enter_context(nc.Block())

        @block.sync
        def _(sp):
            with nc.allow_non_contiguous_dma(reason="vectors as columns"):
                for dst, n in ((g_kv, "ln1_g"), (b_kv, "ln1_b"), (g_l, "ln2_g"), (b_l, "ln2_b")):
                    sp.dma_start(dst[:, :], column(w["L0_xattn_" + n])).then_inc(loads, 16)
            pairs = w["ctx_1024"].rearrange("(t p) d -> p t d", p=P)
            sp.dma_start(ctx_raw[:, :, :], pairs[:, 0:4, :]).then_inc(ctx_in, 16)
            for n, (dst, name, col) in enumerate(weights):
                if n >= 2:
                    sp.wait_ge(w_lo, n - 1)
                stage = raw[n % 2]
                if col is None:
                    sp.dma_start(stage.rearrange("p (k n) -> p k n", n=D), rows(w[name])).then_inc(w_in[n % 2], 16)
                else:
                    sp.dma_start(stage.rearrange("p (k n) -> p k n", n=INNER),
                                 rows(w[name])[:, :, col:col + INNER]).then_inc(w_in[n % 2], 16)
            with sp.Fori(1, NT) as i:
                sp.wait_ge(ctx_ready, 4 * i)
                sp.dma_start(ctx_raw[:, :, :], pairs[:, bass.ds(4 * i, 4), :]).then_inc(ctx_in, 16)
            sp.wait_ge(ctx_in, 16 * NT)
            sp.wait_ge(loads, 64)
            for n in range(2):
                sp.wait_ge(w_in[n], 32)

        @block.gpsimd
        def _(pool):
            norm_x.power_setup(pool, consts)
            norm_c.power_setup(pool, consts)
            pool.memset(p[:, :, :], 0.0).then_inc(consts, 1)
            pool.memset(q_bd[:, :, :, :, :].bitcast(F32), 0.0).then_inc(consts, 1)
            pool.wait_ge(consts, 4)
            norm_x.power(pool, 0)
            norm_x.power(pool, norm_x.steps)
            norm_c.power(pool, 0)
            with pool.Fori(1, NT) as i:
                norm_c.power(pool, i * norm_c.steps)

        @block.tensor
        def _(pe):
            def bank(i, kind, a, b):
                n = number[kind, a, b]
                wait(pe, proj_lo, PROJ * i + n - 1)
                return proj_bank[n % 2]

            def turn_keys(i, kd):
                for half in range(2):
                    dst = bank(i, "t", kd, half)
                    if kd == 0 and half == 0:
                        pe.wait_ge(ctx_ready, 4 * i + 4)
                    for n, t in enumerate((0, 1, 2, 3) if half == 0 else (None,)):
                        src = xl_now[:, kd * P:(kd + 1) * P] if t is None else ctx_n[:, t, kd * P:(kd + 1) * P]
                        mm = pe.transpose(dst[:, n * P:(n + 1) * P], src, k.ident[:, :])
                    mm.then_inc(proj_psum, 1)

            def queries(i, half):
                dst = bank(i, "q", half, 0)
                if half == 0:
                    pe.wait_ge(proj_lo, PROJ * i + 4)
                for n in range(4):
                    u = 4 * half + n
                    mm = product3(pe, dst[:, n * P:(n + 1) * P], lambda a, kd: wq[:, a, kd, u * P:(u + 1) * P],
                                  lambda a, kd: kv_t[:, a, kd, 2 * P:3 * P])
                mm.then_inc(proj_psum, 1)

            def keys_proj(i, hp, half):
                dst = bank(i, "k", hp, half)
                product3(pe, dst[:, 0:LK], lambda a, kd: wk[:, a, kd, hp * P:(hp + 1) * P],
                         lambda a, kd: kv_t[:, a, kd, half * LK:(half + 1) * LK]).then_inc(proj_psum, 1)

            def values_proj(i, vp, part):
                dst = bank(i, "v", vp, part)
                for n, t in enumerate(range(2 * part, min(2 * part + 2, KT))):
                    mm = product3(pe, dst[:, n * 256:(n + 1) * 256], lambda a, kd: kv_t[:, a, kd, t * P:(t + 1) * P],
                                  lambda a, kd: wv[:, a, kd, vp * 256:(vp + 1) * 256])
                mm.then_inc(proj_psum, 1)

            def energies(i, u):
                hp, b = u // 2, u % 2
                pe.wait_ge(proj_lo, PROJ * i + number["k", hp, b] + 1)
                wait(pe, p_exp, 16 * i + u - 1)
                for j, (a, c) in enumerate(PASSES):
                    mm = pe.matmul(s_bank[b][:, 0:LK], q_bd[:, a, b, hp, :], kt[:, hp % 2, c, b * LK:(b + 1) * LK],
                                   start=j == 0, stop=j == 2)
                mm.then_inc(s_psum, 1)

            def turn(i, u):
                pe.wait_ge(p_ready, 16 * i + u + 1)
                wait(pe, pt_lo, 16 * i + u)
                for t in range(3):
                    mm = pe.transpose(pt_bank[:, t * P:(t + 1) * P], p[:, u % 4, t * P:(t + 1) * P], k.ident[:, :])
                mm.then_inc(pt_psum, 1)

            def weigh(i, u):
                hp, b = u // 2, u % 2
                pe.wait_ge(pt_lo, 16 * i + u + 1)
                if u % 4 == 0:
                    pe.wait_ge(proj_lo, PROJ * i + number["v", hp // 2, 2] + 1)
                if b == 0:
                    wait(pe, o_lo, 2 * (NU * i + hp) - 2)
                col = hp % 2 * P
                for t in range(3):
                    for j, (a, c) in enumerate(PASSES):
                        mm = pe.matmul(o_bank[hp % 2][:, b * P:(b + 1) * P], v[:, hp // 2 % 2, a, 2 * b + t, col:col + P],
                                       pt[:, u % 2, c, t * P:(t + 1) * P], start=t == 0 and j == 0, stop=t == 2 and j == 2)
                if b == 1:
                    mm.then_inc(o_psum, 1)

            def project_output(i):
                pe.wait_ge(o_lo, 2 * NU * i + 2 * NU)
                wait(pe, x_done, i)
                for hp in range(NU):
                    for j, (a, c) in enumerate(PASSES):
                        mm = pe.matmul(wo_bank[:, 0:D], at[:, a, hp, :], wo[:, c, hp, :], start=hp == 0 and j == 0,
                                       stop=hp == NU - 1 and j == 2)
                mm.then_inc(wo_psum, 1)

            def rest_first(i):
                turn(i, 13)
                weigh(i, 12)

            def rest_last(i):
                turn(i, 14)
                weigh(i, 13)
                turn(i, 15)
                weigh(i, 14)
                weigh(i, 15)

            def pair(i, first=False):
                turn_keys(i, 0)
                if not first:
                    rest_first(i - 1)
                turn_keys(i, 1)
                if not first:
                    rest_last(i - 1)
                for half in range(2):
                    queries(i, half)
                for half in range(2):
                    keys_proj(i, 0, half)
                if not first:
                    project_output(i - 1)
                for u in range(16):
                    energies(i, u)
                    if u >= 3:
                        turn(i, u - 3)
                    steps = fillers(u)
                    for kind, a, b in steps:
                        if kind == "k":
                            keys_proj(i, a, b)
                    if u >= 4:
                        weigh(i, u - 4)
                    for kind, a, b in steps:
                        if kind == "v":
                            values_proj(i, a, b)

            pe.wait_ge(w_lo, 4)
            pe.wait_ge(loads, 64)
            pair(0, first=True)
            with pe.Fori(1, NT) as i:
                pair(i)
            rest_first(NT - 1)
            rest_last(NT - 1)
            project_output(NT - 1)

        @block.scalar
        def _(act):
            for n, (dst, _, col) in enumerate(weights):
                act.wait_ge(w_in[n % 2], 16 * (n // 2) + 16)
                act.copy(dst[:, 0].rearrange("p k n -> p (k n)"), raw[n % 2]).then_inc(w_hi, 1)
            act.wait_ge(loads, 64)
            act.wait_ge(consts, 4)

            def turned(i, kd):
                for half, g, b in ((0, g_kv, b_kv), (1, g_l, b_l)):
                    n = number["t", kd, half]
                    act.wait_ge(proj_psum, PROJ * i + n + 1)
                    src = proj_bank[n % 2][:, 0:512] if half == 0 else proj_bank[n % 2][:, 0:P]
                    act.activation(kv_f[:, n % 2, 0:512] if half == 0 else kv_f[:, n % 2, 0:P], src, ACT.Identity,
                                   bias=b[:, kd:kd + 1], scale=g[:, kd:kd + 1])
                    if half == 0:
                        dst, src = both_contexts(0, kd), src.rearrange("p (n c) -> p n c", n=2)
                    else:
                        dst = kv_t[:, 0, kd, 2 * P:3 * P]
                    act.activation(dst, src, ACT.Identity, bias=b[:, kd:kd + 1], scale=g[:, kd:kd + 1]).then_inc(proj_f, 1)

            def queries(i, half):
                act.wait_ge(proj_psum, PROJ * i + number["q", half, 0] + 1)
                src = proj_bank[number["q", half, 0] % 2][:, :].rearrange("p (u b q) -> p b u q", b=2, q=S)
                for h in range(2):
                    act.activation(q_bd[h * HD:(h + 1) * HD, 0, :, 4 * half:4 * half + 4, h * S:(h + 1) * S],
                                   src[h * HD:(h + 1) * HD], ACT.Identity, scale=1.0 / 8).then_inc(proj_hi, 1)

            def keys_proj(i, hp, half):
                n = number["k", hp, half]
                act.wait_ge(proj_psum, PROJ * i + n + 1)
                act.copy(kt[:, hp % 2, 0, half * LK:(half + 1) * LK], proj_bank[n % 2][:, 0:LK]).then_inc(proj_hi, 1)

            def values_proj(i, vp, part):
                n = number["v", vp, part]
                act.wait_ge(proj_psum, PROJ * i + n + 1)
                wide = min(KT - 2 * part, 2)
                act.copy(v[:, vp % 2, 0, 2 * part:2 * part + wide, :].rearrange("p t n -> p (t n)"),
                         proj_bank[n % 2][:, 0:wide * 256]).then_inc(proj_hi, 1)

            def weights_of(i, u):
                act.wait_ge(s_max, 16 * i + u + 1)
                at_col = 0 if u % 2 == 0 else S
                act.activation(p[:, u % 4, at_col:at_col + LK], s_bank[u % 2][:, 0:LK], ACT.Exp,
                               bias=neg_max[:, u:u + 1], accum_out=rsum[:, u:u + 1]).then_inc(p_exp, 1)

            def turn(i, u):
                act.wait_ge(pt_psum, 16 * i + u + 1)
                act.copy(pt[:, u % 2, 0, :], pt_bank[:, 0:3 * P]).then_inc(pt_hi, 1)

            def output(i, hp):
                act.wait_ge(o_psum, NU * i + hp + 1)
                for h in range(2):
                    act.copy(at[h * HD:(h + 1) * HD, 0, hp, :].rearrange("p (b q) -> p b q", q=S),
                             o_bank[hp % 2][h * HD:(h + 1) * HD, 0:2 * P].rearrange("p (b h q) -> p b h q", b=2, h=2)[:, :, h, :]
                             ).then_inc(o_hi, 1)

            def rest_first(i):
                turn(i, 13)

            def rest_last(i):
                turn(i, 14)
                turn(i, 15)
                output(i, 6)
                output(i, 7)

            def pair(i, first=False):
                turned(i, 0)
                if not first:
                    rest_first(i - 1)
                turned(i, 1)
                if not first:
                    rest_last(i - 1)
                for half in range(2):
                    queries(i, half)
                for half in range(2):
                    keys_proj(i, 0, half)
                for u in range(16):
                    for kind, a, b in fillers(u - 1) if u else ():
                        if kind == "v":
                            values_proj(i, a, b)
                    if u >= 3:
                        turn(i, u - 3)
                    weights_of(i, u)
                    for kind, a, b in fillers(u):
                        if kind == "k":
                            keys_proj(i, a, b)
                    if u >= 4 and u % 2 == 1:
                        output(i, (u - 4) // 2)

            pair(0, first=True)
            with act.Fori(1, NT) as i:
                pair(i)
            rest_first(NT - 1)
            rest_last(NT - 1)

        @block.vector
        def _(dve):
            for n, (dst, _, col) in enumerate(weights):
                dve.wait_ge(w_hi, n + 1)
                dve.tensor_tensor(dst[:, 1].rearrange("p k n -> p (k n)"), raw[n % 2],
                                  dst[:, 0].rearrange("p k n -> p (k n)").bitcast(F32), ALU.subtract).then_inc(w_lo, 1)
            norm_x.gather(dve, lambda t: x_sb[:, t, :], 0)
            dve.wait_ge(norm_x.rstd_ready, 1)
            for t in range(NT):
                norm_x.apply(dve, xl[:, t, :], x_sb[:, t, :], t).then_inc(xl_ready, 1)
            dve.wait_ge(xl_ready, NT)
            norm_x.gather(dve, lambda t: xl[:, t, :], norm_x.steps)
            dve.wait_ge(norm_x.rstd_ready, 2)
            for t in range(NT):
                norm_x.apply(dve, xl[:, t, :], xl[:, t, :], t).then_inc(xl_ready, 1)
            dve.wait_ge(xl_ready, 2 * NT)
            dve.wait_ge(w_lo, 4)

            def context_stats(i):
                dve.wait_ge(ctx_in, 16 * i + 16)
                norm_c.gather(dve, lambda t: ctx_raw[:, t, :], i * norm_c.steps)

            def context_apply(i):
                dve.wait_ge(norm_c.rstd_ready, i + 1)
                wait(dve, proj_psum, PROJ * (i - 1) + 4)
                dve.tensor_copy(xl_now[:, :], xl[:, bass.ds(i, 1), :].rearrange("p a d -> p (a d)")).then_inc(xl_ready, 1)
                for t in range(4):
                    norm_c.apply(dve, ctx_n[:, t, :], ctx_raw[:, t, :], t).then_inc(ctx_ready, 1)

            def turned(i, kd):
                for half in range(2):
                    n = number["t", kd, half]
                    dve.wait_ge(proj_f, 4 * i + n + 1)
                    if half == 0:
                        dve.tensor_tensor(both_contexts(1, kd), kv_f[:, n % 2, :].rearrange("p (n c) -> p n c", n=2),
                                          both_contexts(0, kd).bitcast(F32), ALU.subtract).then_inc(proj_lo, 1)
                    else:
                        dve.tensor_tensor(kv_t[:, 1, kd, 2 * P:3 * P], kv_f[:, n % 2, 0:P],
                                          kv_t[:, 0, kd, 2 * P:3 * P].bitcast(F32), ALU.subtract).then_inc(proj_lo, 1)

            def queries(i, half):
                n = number["q", half, 0]
                dve.wait_ge(proj_hi, HI * i + 2 * half + 2)
                src = proj_bank[n % 2][:, :].rearrange("p (u b q) -> p b u q", b=2, q=S)
                for h in range(2):
                    for b in range(2):
                        block_of = lambda part: q_bd[h * HD:(h + 1) * HD, part, b, 4 * half:4 * half + 4, h * S:(h + 1) * S]
                        ins = dve.scalar_tensor_tensor(out=block_of(1), in0=src[h * HD:(h + 1) * HD, b], scalar=1.0 / 8,
                                                       in1=block_of(0).bitcast(F32), op0=ALU.mult, op1=ALU.subtract)
                ins.then_inc(proj_lo, 1)

            def keys_proj(i, hp, half):
                n = number["k", hp, half]
                dve.wait_ge(proj_hi, HI * i + hi_number(n))
                dve.tensor_tensor(kt[:, hp % 2, 1, half * LK:(half + 1) * LK], proj_bank[n % 2][:, 0:LK],
                                  kt[:, hp % 2, 0, half * LK:(half + 1) * LK].bitcast(F32), ALU.subtract).then_inc(proj_lo, 1)

            def values_proj(i, vp, part):
                n = number["v", vp, part]
                dve.wait_ge(proj_hi, HI * i + hi_number(n))
                wide = min(KT - 2 * part, 2)
                cols = lambda c: v[:, vp % 2, c, 2 * part:2 * part + wide, :].rearrange("p t n -> p (t n)")
                dve.tensor_tensor(cols(1), proj_bank[n % 2][:, 0:wide * 256], cols(0).bitcast(F32),
                                  ALU.subtract).then_inc(proj_lo, 1)

            def maximum(i, u):
                dve.wait_ge(s_psum, 16 * i + u + 1)
                dve.tensor_reduce(neg_max[:, u:u + 1], s_bank[u % 2][:, 0:LK], AX.X, ALU.max, negate=True).then_inc(s_max, 1)

            def normalise(i, u):
                dve.wait_ge(p_exp, 16 * i + u + 1)
                dve.reciprocal(rinv[:, u:u + 1], rsum[:, u:u + 1]).then_inc(p_inv, 1)
                dve.wait_ge(p_inv, 16 * i + u + 1)
                at_col = 0 if u % 2 == 0 else S
                cols = p[:, u % 4, at_col:at_col + LK]
                dve.tensor_scalar(cols, cols, rinv[:, u:u + 1], None, ALU.mult).then_inc(p_ready, 1)

            def turn(i, u):
                dve.wait_ge(pt_hi, 16 * i + u + 1)
                dve.tensor_tensor(pt[:, u % 2, 1, :], pt_bank[:, 0:3 * P], pt[:, u % 2, 0, :].bitcast(F32),
                                  ALU.subtract).then_inc(pt_lo, 1)

            def output(i, hp):
                dve.wait_ge(o_hi, 2 * (NU * i + hp) + 2)
                for h in range(2):
                    dst = lambda c: at[h * HD:(h + 1) * HD, c, hp, :].rearrange("p (b q) -> p b q", q=S)
                    dve.tensor_tensor(dst(1), o_bank[hp % 2][h * HD:(h + 1) * HD, 0:2 * P].rearrange(
                        "p (b h q) -> p b h q", b=2, h=2)[:, :, h, :], dst(0).bitcast(F32), ALU.subtract).then_inc(o_lo, 1)

            def residual(i):
                dve.wait_ge(wo_psum, i + 1)
                row = x_sb[:, bass.ds(i, 1), :].rearrange("p a d -> p (a d)")
                dve.tensor_tensor(row, row, wo_bank[:, 0:D], ALU.add).then_inc(x_done, 1)

            def rest_first(i):
                turn(i, 13)

            def rest_last(i):
                turn(i, 14)
                turn(i, 15)
                output(i, 6)
                output(i, 7)

            def pair(i, first=False, last=False):
                if not first:
                    normalise(i - 1, 15)
                turned(i, 0)
                if not first:
                    rest_first(i - 1)
                turned(i, 1)
                if not first:
                    rest_last(i - 1)
                for half in range(2):
                    queries(i, half)
                for half in range(2):
                    keys_proj(i, 0, half)
                for u in range(16):
                    maximum(i, u)
                    if u == 0 and not first:
                        residual(i - 1)
                    for kind, a, b in fillers(u - 1) if u else ():
                        if kind == "v":
                            values_proj(i, a, b)
                    if u >= 3:
                        turn(i, u - 3)
                    if u >= 1:
                        normalise(i, u - 1)
                    for kind, a, b in fillers(u):
                        if kind == "k":
                            keys_proj(i, a, b)
                    if u >= 4 and u % 2 == 1:
                        output(i, (u - 4) // 2)
                    if u == 8 and not last:
                        context_stats(i + 1)
                    if u == 12 and not last:
                        context_apply(i + 1)

            context_stats(0)
            context_apply(0)
            pair(0, first=True)
            with dve.Fori(1, NT - 1) as i:
                pair(i)
            pair(NT - 1, last=True)
            normalise(NT - 1, 15)
            rest_first(NT - 1)
            rest_last(NT - 1)
            residual(NT - 1)
            dve.wait_ge(x_done, NT)


STAGE_BODIES = {"latent_attention": latent_attention, "recurrence": recurrence, "experts": experts, "linear_attention": linear_attention, "feed_forward": feed_forward, "masked_attention": masked_attention}


class Shared:

    def __init__(self, nc, ctx):
        self.nc, self.ctx, self.of_stage = nc, ctx, []

    def sem(self, name):
        return self.ctx.enter_context(self.nc.semaphore(name))

    def stage_sem(self, name):
        self.of_stage.append(self.nc.alloc_semaphore(name=name))
        return self.of_stage[-1]

    def end_stage(self):
        self.nc.clear_and_free_semaphores(self.of_stage)
        self.nc.all_engine_barrier()
        self.of_stage = []


def constants_and_input(nc, k, x_sb, w):
    loads, made = k.sem("io_loads"), k.sem("io_made")
    with nc.Block() as block:

        @block.sync
        def _(sp):
            sp.dma_start(x_sb[:, :, :], w["x"].rearrange("(t p) d -> p t d", p=P)).then_inc(loads, 16)
            sp.wait_ge(loads, 16)

        @block.gpsimd
        def _(pool):
            pool.memset(k.ident[:, :], 0.0).then_inc(made, 1)
            pool.memset(k.head_mask[:, :], 1.0).then_inc(made, 1)
            pool.wait_ge(made, 2)
            pool.affine_select(out=k.ident[:, :], in_=k.ident[:, :], compare_op=ALU.not_equal, fill=1.0, base=0,
                               pattern=[[-1, P]], channel_multiplier=1).then_inc(made, 1)
            pool.affine_select(out=k.head_mask[:, :], in_=k.head_mask[:, :], compare_op=ALU.is_ge, fill=0.0, base=0,
                               pattern=[[-16, 8]], channel_multiplier=1).then_inc(made, 1)
            pool.wait_ge(made, 4)
            pool.affine_select(out=k.head_mask[:, :], in_=k.head_mask[:, :], compare_op=ALU.is_ge, fill=0.0, base=15,
                               pattern=[[16, 8]], channel_multiplier=-1).then_inc(made, 1)
            pool.wait_ge(made, 5)


def result(nc, k, x_sb, out):
    stored = k.sem("io_stored")
    with nc.Block() as block:

        @block.sync
        def _(sp):
            sp.dma_start(out.rearrange("(t p) d -> p t d", p=P), x_sb[:, :, :]).then_inc(stored, 16)
            sp.wait_ge(stored, 16)


STAGES = ["latent_attention", "linear_attention", "feed_forward", "masked_attention", "recurrence", "experts"]


def perceiver(nc, w, scratch, out):
    ctx = ExitStack()
    with ctx:
        k = Shared(nc, ctx)
        x_sb = ctx.enter_context(nc.sbuf_tensor("x_sb", [P, NT, D], F32))
        k.ident = ctx.enter_context(nc.sbuf_tensor("ident", [P, P], F32))
        k.head_mask = ctx.enter_context(nc.sbuf_tensor("head_mask", [P, 8], F32))
        banks = [ctx.enter_context(nc.psum_tensor(f"bank{i}", [P, 512], F32)) for i in range(8)]
        k.scratch = scratch
        constants_and_input(nc, k, x_sb, w)
        for stage in STAGES:
            STAGE_BODIES[stage](nc, k, x_sb, banks, w)
            k.end_stage()
        result(nc, k, x_sb, out)


_TURNED = ["L0_attn_Wq", "L0_attn_Wk", "L0_attn_Wv", "L0_ffn_w_gate", "L0_ffn_w_up", "L0_ffn_w_down",
           "L1_xattn_Wq", "L1_xattn_Wk", "L1_xattn_Wv", "L1_xattn_Wo",
           "L1_attn_Wi", "L1_attn_Wf", "L1_attn_Wz", "L1_attn_Wo", "L1_attn_Wp"]


def kernel(**inputs):
    import numpy as _np
    import concourse.bacc as _bacc
    from concourse import mybir as _mybir
    from concourse.bass_utils import run_bass_kernel_spmd as _run

    nc = _bacc.Bacc("TRN2", target_bir_lowering=False, num_devices=1)
    laid = {n: _np.asarray(a) for n, a in inputs.items()}
    laid["x"] = laid["x"].reshape(T, D)
    laid["ctx_1024"] = laid["ctx_1024"].reshape(B * S2, D)
    laid["ctx_turned"] = laid["ctx_1024"].T
    laid["mask_1x1xSxS2_ik1"] = laid["mask_1x1xSxS2_ik1"].reshape(S, S2)
    for n in _TURNED:
        laid[n] = laid[n].T
    arrays, aps = {}, {}
    for n, a in laid.items():
        a = _np.ascontiguousarray(a)
        arrays[f"in_{n}"] = a
        aps[n] = nc.dram_tensor(f"in_{n}", a.shape, _mybir.dt.from_np(a.dtype), kind="ExternalInput").ap()
    scratch = nc.dram_tensor("gate_rows", (NT, 8, P), F32, kind="Internal").ap()
    out = nc.dram_tensor("out_x", (T, D), F32, kind="ExternalOutput").ap()
    perceiver(nc, aps, scratch, out)
    r = _run(nc, [arrays], core_ids=[0])
    return r.results[0]["out_x"].reshape(B, S, D)
```

```python
from contextlib import ExitStack

import concourse.bass as bass
from concourse import mybir

F32 = mybir.dt.float32
F32R = mybir.dt.float32r
I32 = mybir.dt.int32
ALU = mybir.AluOpType
ACT = mybir.ActivationFunctionType
AX = mybir.AxisListType

P = 128
D = 256
KD = D // P
B = 32
S = 64
S2 = 256
T = B * S
NT = T // P
CH = 512
NCH = T // CH
EPS = 1e-5
PASSES = ((0, 0), (0, 1), (1, 0))


def rows(w):
    return w.rearrange("(k p) n -> p k n", p=P)


def column(v):
    return v.rearrange("(k p) -> p k", p=P)


def everywhere(v):
    return v.partition_broadcast(P)


class Tools:

    def __init__(self, nc, ctx, stage):
        self.nc, self.ctx, self.stage = nc, ctx, stage

    def sb(self, name, shape, dt=F32):
        return self.ctx.enter_context(self.nc.sbuf_tensor(f"{self.stage}_{name}", shape, dt))


class Sem:

    def __init__(self, sem):
        self.sem, self.n = sem, 0

    def give(self, ins):
        ins.then_inc(self.sem, 1)
        self.n += 1
        return self.n


def wait(eng, sem, value):
    if isinstance(value, int) and value <= 0:
        return
    eng.wait_ge(sem, value)


def product3(pe, out, lhs, rhs, first=True, last=True):
    mm = None
    for k in range(KD):
        for n, (a, b) in enumerate(PASSES):
            mm = pe.matmul(out, lhs(a, k), rhs(b, k), start=first and k == 0 and n == 0,
                           stop=last and k == KD - 1 and n == 2)
    return mm


class NormStats:

    def __init__(self, tools, n, stats, rstd_ready, tag=""):
        self.n = n
        self.raw = tools.sb("st_raw" + tag, [P, n, 6])
        self.tmp = tools.sb("st_tmp" + tag, [P, 5, n])
        self.mean = tools.sb("st_mean" + tag, [P, n])
        self.vareps = tools.sb("st_var" + tag, [P, n])
        self.rstd = tools.sb("st_rstd" + tag, [P, n])
        self.half = tools.sb("st_half" + tag, [P, n])
        self.stats, self.rstd_ready = stats, rstd_ready
        self.steps = n + 7

    def gather(self, dve, row, base):
        n, raw, tmp = self.n, self.raw, self.tmp
        for t in range(n):
            dve.bn_stats(raw[:, t, :], row(t)).then_inc(self.stats, 1)
        dve.wait_ge(self.stats, base + n)
        dve.tensor_tensor(tmp[:, 0, :], raw[:, :, 1], raw[:, :, 4], ALU.add).then_inc(self.stats, 1)
        dve.tensor_tensor(tmp[:, 1, :], raw[:, :, 1], raw[:, :, 4], ALU.subtract).then_inc(self.stats, 1)
        dve.tensor_tensor(tmp[:, 2, :], raw[:, :, 2], raw[:, :, 5], ALU.add).then_inc(self.stats, 1)
        dve.wait_ge(self.stats, base + n + 3)
        dve.tensor_scalar(self.mean[:, :], tmp[:, 0, :], 0.5, None, ALU.mult).then_inc(self.stats, 1)
        dve.tensor_tensor(tmp[:, 3, :], tmp[:, 1, :], tmp[:, 1, :], ALU.mult).then_inc(self.stats, 1)
        dve.tensor_scalar(tmp[:, 4, :], tmp[:, 2, :], 1.0 / D, EPS, ALU.mult, ALU.add).then_inc(self.stats, 1)
        dve.wait_ge(self.stats, base + n + 6)
        dve.scalar_tensor_tensor(out=self.vareps[:, :], in0=tmp[:, 3, :], scalar=0.25, in1=tmp[:, 4, :],
                                 op0=ALU.mult, op1=ALU.add).then_inc(self.stats, 1)

    def power_setup(self, pool, consts_ready):
        pool.memset(self.half[:, :], -0.5).then_inc(consts_ready, 1)

    def power(self, pool, base):
        pool.wait_ge(self.stats, base + self.steps)
        pool.tensor_tensor(self.rstd[:, :], self.vareps[:, :], self.half[:, :], ALU.pow).then_inc(self.rstd_ready, 1)

    def apply(self, dve, out, row, t):
        return dve.tensor_scalar(out, row, self.mean[:, t:t + 1], self.rstd[:, t:t + 1], ALU.subtract, ALU.mult)


class NormTranspose:

    def __init__(self, tools, sem, x_sb, ident, banks, split=False, double=False, affine=None):
        self.affine, self.per_tile = affine, KD if affine else 1
        self.x_sb, self.ident, self.banks, self.split, self.double = x_sb, ident, banks, split, double
        self.xn = tools.sb("xn", [P, NT, D])
        self.xt = tools.sb("xt", [P, 2 if split else 1, KD, T], F32R if split else F32)
        self.consts = sem("half_ready")
        self.norm = NormStats(tools, NT, sem("norm_stats"), sem("rstd_ready"))
        self.xn_ready, self.xt_psum = sem("xn_ready"), sem("xt_psum")
        self.xt_hi, self.xt_done = sem("xt_hi"), sem("xt_done")

    def pool(self, pool):
        self.norm.power_setup(pool, self.consts)
        pool.wait_ge(self.consts, 1)
        self.norm.power(pool, 0)
        if self.double:
            self.norm.power(pool, self.norm.steps)

    def dve(self, dve):
        self.dve_stats(dve)
        self.dve_apply(dve)
        self.dve_split(dve)

    def dve_stats(self, dve):
        self.norm.gather(dve, lambda t: self.x_sb[:, t, :], 0)

    def dve_apply(self, dve):
        norm = self.norm
        dve.wait_ge(norm.rstd_ready, 1)
        for t in range(NT):
            norm.apply(dve, self.xn[:, t, :], self.x_sb[:, t, :], t).then_inc(self.xn_ready, 1)
        if self.double:
            dve.wait_ge(self.xn_ready, NT)
            norm.gather(dve, lambda t: self.xn[:, t, :], norm.steps)
            dve.wait_ge(norm.rstd_ready, 2)
            for t in range(NT):
                norm.apply(dve, self.xn[:, t, :], self.xn[:, t, :], t).then_inc(self.xn_ready, 1)

    def dve_split(self, dve):
        if self.split:
            for t in range(NT):
                dve.wait_ge(self.xt_hi, t + 1)
                dve.tensor_tensor(self.tile(1, t), self.turned(t), self.tile(0, t).bitcast(F32),
                                  ALU.subtract).then_inc(self.xt_done, 1)

    def tile(self, part, t):
        return self.xt[:, part, :, t * P:(t + 1) * P]

    def turned(self, t):
        return self.banks[t % 2][:, 0:D].rearrange("p (k n) -> p k n", k=KD)

    def pe(self, pe):
        base = NT if self.double else 0
        for t in range(NT):
            pe.wait_ge(self.xn_ready, base + t + 1)
            if t >= 2:
                pe.wait_ge(self.xt_done, self.per_tile * (t - 1))
            for k in range(KD):
                mm = pe.transpose(self.banks[t % 2][:, k * P:(k + 1) * P], self.xn[:, t, k * P:(k + 1) * P],
                                  self.ident)
            mm.then_inc(self.xt_psum, 1)

    def act(self, act):
        for t in range(NT):
            act.wait_ge(self.xt_psum, t + 1)
            if self.affine:
                scale, bias = self.affine
                for k in range(KD):
                    act.activation(self.tile(0, t)[:, k], self.turned(t)[:, k], ACT.Identity, bias=bias[:, k:k + 1],
                                   scale=scale[:, k:k + 1]).then_inc(self.xt_done, 1)
            else:
                act.copy(self.tile(0, t), self.turned(t)).then_inc(self.xt_hi if self.split else self.xt_done, 1)


def linear_attention(nc, k, x_sb, banks, w):
    with ExitStack() as ctx:
        tools = Tools(nc, ctx, "lin")
        sem = lambda name: k.stage_sem("lin_" + name)
        front = NormTranspose(tools, sem, x_sb, k.ident[:, :], banks[0:2])
        wq = tools.sb("wq", [P, KD, D])
        wkv = tools.sb("wkv", [P, KD, 2 * D])
        bq = tools.sb("bq", [P, KD])
        bkv = tools.sb("bkv", [P, 2 * D])
        gamma = tools.sb("gamma", [P, D])
        beta = tools.sb("beta", [P, D])
        qt = tools.sb("qt", [P, KD, T])
        vext = tools.sb("vext", [P, 2, KD, P + 1])
        kk = tools.sb("kk", [P, 2, D])
        kpre = tools.sb("kpre", [P, 2, D])
        kvm = tools.sb("kvm", [P, 2, 2, KD, P + 8])
        mask = tools.sb("mask", [P, P])
        rden = tools.sb("rden", [P, 2, 16])
        dmax = tools.sb("dmax", [P, 2, 16])
        ctxn = tools.sb("ctxn", [P, 2, D])
        y = tools.sb("y", [P, NT, D])
        norm2 = NormStats(tools, NT, sem("y_stats"), sem("y_rstd"), "y")
        loads, consts = sem("loads"), sem("consts")
        q_psum, q_done = sem("q_psum"), sem("q_done")
        kv_psum, k_ready, k_pre, v_ready = sem("kv_psum"), sem("k_ready"), sem("k_pre"), sem("v_ready")
        state_psum, state_ready = sem("state_psum"), sem("state_ready")
        ctx_psum, den_step, ctx_step, y_ready = sem("ctx_psum"), sem("den_step"), sem("ctx_step"), sem("y_ready")
        tail, beta_added, x_done = sem("tail"), sem("beta_added"), sem("x_done")
        kv_bank, st_bank, ctx_bank, q_bank = banks[2], banks[3:5], banks[5], banks[6:8]

        block = ctx.enter_context(nc.Block())

        @block.sync
        def _(sp):
            sp.dma_start(wq[:, :, :], rows(w["L0_attn_Wq"])).then_inc(loads, 16)
            sp.dma_start(wkv[:, :, 0:D], rows(w["L0_attn_Wk"])).then_inc(loads, 16)
            sp.dma_start(wkv[:, :, D:2 * D], rows(w["L0_attn_Wv"])).then_inc(loads, 16)
            with nc.allow_non_contiguous_dma(reason="a bias as a column"):
                sp.dma_start(bq[:, :], column(w["L0_attn_bq"])).then_inc(loads, 16)
            sp.dma_start(bkv[:, 0:D], everywhere(w["L0_attn_bk"])).then_inc(loads, 16)
            sp.dma_start(bkv[:, D:2 * D], everywhere(w["L0_attn_bv"])).then_inc(loads, 16)
            sp.dma_start(gamma[:, :], everywhere(w["L0_attn_gamma"])).then_inc(loads, 16)
            sp.dma_start(beta[:, :], everywhere(w["L0_attn_beta"])).then_inc(loads, 16)
            sp.wait_ge(loads, 128)

        @block.gpsimd
        def _(pool):
            pool.memset(vext[:, :, :, P:P + 1], 1.0).then_inc(consts, 1)
            pool.tensor_copy(mask[:, :].rearrange("p (h d) -> p h d", d=16),
                             k.head_mask[:, :].unsqueeze(2).to_broadcast([P, 8, 16])).then_inc(consts, 1)
            front.pool(pool)
            norm2.power_setup(pool, consts)
            pool.wait_ge(loads, 128)
            pool.wait_ge(front.xn_ready, NT)
            pool.tensor_tensor(x_sb[:, :, :], x_sb[:, :, :], beta[:, :].unsqueeze(1).to_broadcast([P, NT, D]),
                               ALU.add).then_inc(beta_added, 1)
            pool.wait_ge(consts, 3)
            norm2.power(pool, 0)

        @block.tensor
        def _(pe):
            front.pe(pe)
            pe.wait_ge(loads, 128)
            xt = front.xt
            for n in range(KD * NCH):
                m, c = n % KD, n // KD
                pe.wait_ge(front.xt_done, 4 * c + 4)
                if n >= 2:
                    pe.wait_ge(q_done, n - 1)
                for kd in range(KD):
                    mm = pe.matmul(q_bank[n % 2][:, :], wq[:, kd, m * P:(m + 1) * P], xt[:, 0, kd, c * CH:(c + 1) * CH],
                                   start=kd == 0, stop=kd == KD - 1)
                mm.then_inc(q_psum, 1)
            pe.wait_ge(q_done, KD * NCH)

            def keys_values(t):
                if t >= 1:
                    pe.wait_ge(v_ready, t)
                for kd in range(KD):
                    mm = pe.matmul(kv_bank[:, :], xt[:, 0, kd, t * P:(t + 1) * P], wkv[:, kd, :],
                                   start=kd == 0, stop=kd == KD - 1)
                mm.then_inc(kv_psum, 1)

            def states(t):
                pe.wait_ge(k_ready, t + 1)
                pe.wait_ge(v_ready, t + 1)
                if t >= 1:
                    pe.wait_ge(state_ready, 4 * t)
                for b in range(2):
                    for m in range(KD):
                        mm = pe.matmul(st_bank[b][:, m * (P + 1):(m + 1) * (P + 1)],
                                       kk[b * S:(b + 1) * S, t % 2, m * P:(m + 1) * P],
                                       vext[b * S:(b + 1) * S, t % 2, m, :], start=True, stop=True)
                mm.then_inc(state_psum, 1)

            def contexts(t):
                pe.wait_ge(state_ready, 4 * t + 4)
                if t >= 1:
                    pe.wait_ge(y_ready, t)
                for b in range(2):
                    for m in range(KD):
                        at = t * P + b * S
                        mm = pe.matmul(ctx_bank[b * S:(b + 1) * S, m * (P + 8):(m + 1) * (P + 8)],
                                       qt[:, m, at:at + S], kvm[:, t % 2, b, m, :], start=True, stop=True)
                mm.then_inc(ctx_psum, 1)

            keys_values(0)
            for t in range(NT):
                states(t)
                if t + 1 < NT:
                    keys_values(t + 1)
                contexts(t)

        @block.scalar
        def _(act):
            front.act(act)
            act.wait_ge(loads, 128)
            act.wait_ge(consts, 1)
            for n in range(KD * NCH):
                m, c = n % KD, n // KD
                act.wait_ge(q_psum, n + 1)
                act.activation(qt[:, m, c * CH:(c + 1) * CH], q_bank[n % 2][:, :], ACT.Relu,
                               bias=bq[:, m:m + 1]).then_inc(q_done, 1)
            for t in range(NT):
                act.wait_ge(k_pre, t + 1)
                if t >= 2:
                    act.wait_ge(state_psum, t - 1)
                act.activation(kk[:, t % 2, :], kpre[:, t % 2, :], ACT.Relu).then_inc(k_ready, 1)

        @block.vector
        def _(dve):
            front.dve(dve)
            dve.wait_ge(loads, 128)
            dve.wait_ge(consts, 2)

            def keys_values(t):
                dve.wait_ge(kv_psum, t + 1)
                if t >= 2:
                    dve.wait_ge(k_ready, t - 1)
                    dve.wait_ge(state_psum, t - 1)
                dve.tensor_tensor(kpre[:, t % 2, :], kv_bank[:, 0:D], bkv[:, 0:D], ALU.add).then_inc(k_pre, 1)
                dve.tensor_tensor(vext[:, t % 2, :, 0:P],
                                  kv_bank[:, D:2 * D].rearrange("p (m n) -> p m n", m=KD),
                                  bkv[:, D:2 * D].rearrange("p (m n) -> p m n", m=KD), ALU.add).then_inc(v_ready, 1)

            def states(t):
                dve.wait_ge(state_psum, t + 1)
                if t >= 2:
                    dve.wait_ge(ctx_psum, t - 1)
                for b in range(2):
                    src = st_bank[b][:, 0:KD * (P + 1)].rearrange("p (m n) -> p m n", m=KD)
                    dve.tensor_tensor(kvm[:, t % 2, b, :, 0:P], src[:, :, 0:P],
                                      mask[:, :].unsqueeze(1).to_broadcast([P, KD, P]), ALU.mult).then_inc(state_ready, 1)
                    dve.tensor_tensor(kvm[:, t % 2, b, :, P:P + 8], src[:, :, P:P + 1].to_broadcast([P, KD, 8]),
                                      k.head_mask[:, :].unsqueeze(1).to_broadcast([P, KD, 8]),
                                      ALU.mult).then_inc(state_ready, 1)

            def contexts(t):
                dve.wait_ge(ctx_psum, t + 1)
                src = ctx_bank[:, 0:KD * (P + 8)].rearrange("p (m n) -> p m n", m=KD)
                den = dmax[:, t % 2, :].rearrange("p (m h) -> p m h", m=KD)
                dve.tensor_scalar(den, src[:, :, P:P + 8], 1e-6, None, ALU.max).then_inc(den_step, 1)
                dve.wait_ge(den_step, 2 * t + 1)
                dve.reciprocal(rden[:, t % 2, :], dmax[:, t % 2, :]).then_inc(den_step, 1)
                dve.wait_ge(den_step, 2 * t + 2)
                for m in range(KD):
                    dve.tensor_tensor(ctxn[:, t % 2, m * P:(m + 1) * P].rearrange("p (h d) -> p h d", d=16),
                                      src[:, m, 0:P].rearrange("p (h d) -> p h d", d=16),
                                      rden[:, t % 2, m * 8:(m + 1) * 8].unsqueeze(2).to_broadcast([P, 8, 16]),
                                      ALU.mult).then_inc(ctx_step, 1)
                dve.wait_ge(ctx_step, 2 * t + 2)
                dve.tensor_tensor(y[:, t, :], ctxn[:, t % 2, :], front.xn[:, t, :], ALU.add).then_inc(y_ready, 1)

            keys_values(0)
            for t in range(NT):
                states(t)
                if t + 1 < NT:
                    keys_values(t + 1)
                contexts(t)
            dve.wait_ge(y_ready, NT)
            norm2.gather(dve, lambda t: y[:, t, :], 0)
            dve.wait_ge(norm2.rstd_ready, 1)
            dve.wait_ge(beta_added, 1)
            for t in range(NT + 1):
                if t < NT:
                    dve.scalar_tensor_tensor(out=y[:, t, :], in0=y[:, t, :], scalar=norm2.mean[:, t:t + 1], in1=gamma[:, :],
                                             op0=ALU.subtract, op1=ALU.mult).then_inc(tail, 1)
                if t >= 1:
                    dve.wait_ge(tail, t)
                    dve.scalar_tensor_tensor(out=x_sb[:, t - 1, :], in0=y[:, t - 1, :], scalar=norm2.rstd[:, t - 1:t],
                                             in1=x_sb[:, t - 1, :], op0=ALU.mult, op1=ALU.add).then_inc(x_done, 1)
            dve.wait_ge(x_done, NT)


def feed_forward(nc, k, x_sb, banks, w):
    HID = 768
    NH = HID // P
    with ExitStack() as ctx:
        tools = Tools(nc, ctx, "ffn")
        sem = lambda name: k.stage_sem("ffn_" + name)
        front = NormTranspose(tools, sem, x_sb, k.ident[:, :], banks[0:2], split=True)
        wi = tools.sb("wi", [P, KD, 2, HID], I32)
        wdi = tools.sb("wdi", [P, NH, D], I32)
        wf = tools.sb("wf", [P, KD, 2, HID])
        wdf = tools.sb("wdf", [P, NH, D])
        wgu = tools.sb("wgu", [P, 2, KD, 2, HID], F32R)
        wd = tools.sb("wd", [P, 2, NH, D], F32R)
        silu = tools.sb("silu", [P, 2, CH])
        hf = tools.sb("hf", [P, 2, CH])
        ht = tools.sb("ht", [P, 2, NH, CH], F32R)
        loads, w_step, wd_step = sem("loads"), sem("w_step"), sem("wd_step")
        gate_psum, up_psum, silu_done, h_done = sem("gate_psum"), sem("up_psum"), sem("silu_done"), sem("h_done")
        hi_done, lo_done, down_psum, x_done = sem("hi_done"), sem("lo_done"), sem("down_psum"), sem("x_done")
        gate_bank, up_bank, down_bank = banks[2:4], banks[4:6], banks[6:8]
        block = ctx.enter_context(nc.Block())

        @block.sync
        def _(sp):
            sp.dma_start(wi[:, :, 0, :], rows(w["L0_ffn_w_gate"])).then_inc(loads, 16)
            sp.dma_start(wi[:, :, 1, :], rows(w["L0_ffn_w_up"])).then_inc(loads, 16)
            sp.dma_start(wdi[:, :, :], rows(w["L0_ffn_w_down"])).then_inc(loads, 16)
            sp.wait_ge(loads, 48)

        @block.gpsimd
        def _(pool):
            front.pool(pool)
            pool.wait_ge(w_step, 2)
            pool.tensor_tensor(wgu[:, 1], wf[:, :], wgu[:, 0].bitcast(F32), ALU.subtract).then_inc(w_step, 1)
            pool.wait_ge(wd_step, 2)
            pool.tensor_tensor(wd[:, 1], wdf[:, :], wd[:, 0].bitcast(F32), ALU.subtract).then_inc(wd_step, 1)

        @block.tensor
        def _(pe):
            front.pe(pe)
            pe.wait_ge(w_step, 3)
            for c in range(NCH):
                pe.wait_ge(front.xt_done, 4 * c + 4)
                for h in range(NH):
                    n = c * NH + h
                    for g, (bank, done, freed) in enumerate(((gate_bank, gate_psum, silu_done), (up_bank, up_psum, h_done))):
                        if n >= 2:
                            pe.wait_ge(freed, n - 1)
                        product3(pe, bank[n % 2][:, :], lambda a, kd: wgu[:, a, kd, g, h * P:(h + 1) * P],
                                 lambda a, kd: front.xt[:, a, kd, c * CH:(c + 1) * CH]).then_inc(done, 1)
                if c == 0:
                    pe.wait_ge(wd_step, 3)
                for tt in range(4):
                    n = 4 * c + tt
                    if n >= 2:
                        pe.wait_ge(x_done, n - 1)
                    for h in range(NH):
                        if tt == 0:
                            pe.wait_ge(lo_done, c * NH + h + 1)
                        for j, (a, b) in enumerate(PASSES):
                            mm = pe.matmul(down_bank[n % 2][:, 0:D], ht[:, a, h, tt * P:(tt + 1) * P], wd[:, b, h, :],
                                           start=h == 0 and j == 0, stop=h == NH - 1 and j == 2)
                    mm.then_inc(down_psum, 1)

        @block.scalar
        def _(act):
            act.wait_ge(w_step, 1)
            act.copy(wgu[:, 0], wf[:, :]).then_inc(w_step, 1)
            front.act(act)
            act.wait_ge(wd_step, 1)
            act.copy(wd[:, 0], wdf[:, :]).then_inc(wd_step, 1)
            for c in range(NCH):
                for h in range(NH):
                    n = c * NH + h
                    act.wait_ge(gate_psum, n + 1)
                    if n >= 2:
                        act.wait_ge(h_done, n - 1)
                    act.activation(silu[:, n % 2, :], gate_bank[n % 2][:, :], ACT.Silu).then_inc(silu_done, 1)
                    act.wait_ge(h_done, n + 1)
                    if c >= 1 and h == 0:
                        act.wait_ge(down_psum, 4 * c)
                    act.copy(ht[:, 0, h, :], hf[:, n % 2, :]).then_inc(hi_done, 1)

        @block.vector
        def _(dve):
            front.dve_stats(dve)
            dve.wait_ge(loads, 48)
            dve.tensor_scalar(wf[:, :], wi[:, :], 1.0 / 127.0, None, ALU.mult).then_inc(w_step, 1)
            front.dve_apply(dve)
            dve.tensor_scalar(wdf[:, :], wdi[:, :], 1.0 / 127.0, None, ALU.mult).then_inc(wd_step, 1)
            front.dve_split(dve)

            def residual(c):
                for tt in range(4):
                    n = 4 * c + tt
                    dve.wait_ge(down_psum, n + 1)
                    dve.tensor_tensor(x_sb[:, n, :], x_sb[:, n, :], down_bank[n % 2][:, 0:D], ALU.add).then_inc(x_done, 1)

            for c in range(NCH):
                for h in range(NH):
                    n = c * NH + h
                    dve.wait_ge(silu_done, n + 1)
                    dve.wait_ge(up_psum, n + 1)
                    if n >= 2:
                        dve.wait_ge(hi_done, n - 1)
                        dve.wait_ge(lo_done, n - 1)
                    dve.tensor_tensor(hf[:, n % 2, :], silu[:, n % 2, :], up_bank[n % 2][:, :], ALU.mult).then_inc(h_done, 1)
                    dve.wait_ge(hi_done, n + 1)
                    dve.tensor_tensor(ht[:, 1, h, :], hf[:, n % 2, :], ht[:, 0, h, :].bitcast(F32),
                                      ALU.subtract).then_inc(lo_done, 1)
                residual(c)
            dve.wait_ge(x_done, NT)


def recurrence(nc, k, x_sb, banks, w):
    N = 64
    HALF = T // 2
    SEG = HALF // S
    FORGET = -1e30
    with ExitStack() as ctx:
        tools = Tools(nc, ctx, "rec")
        sem = lambda name: k.stage_sem("rec_" + name)
        lnw, lnb = tools.sb("lnw", [P, KD]), tools.sb("lnb", [P, KD])
        front = NormTranspose(tools, sem, x_sb, k.ident[:, :], banks[0:2], double=True, affine=(lnw, lnb))
        wg = tools.sb("wg", [P, KD, 4, N])
        bias = tools.sb("bias", [P, 4])
        wp = tools.sb("wp", [P, D])
        bp = tools.sb("bp", [P, D])
        log_i, log_f, z, o, d1, m, a, f, c = (tools.sb(n, [P, HALF]) for n in
                                              ("log_i", "log_f", "z", "o", "d1", "m", "a", "f", "c"))
        seg = lambda v: v[:, :].rearrange("p (g s) -> p g s", s=S)
        ln_loads, loads, psum, gate_done = sem("ln_loads"), sem("loads"), sem("psum"), sem("gate_done")
        step, expo, zo_done, tanh_done, h_ready = sem("step"), sem("expo"), sem("zo_done"), sem("tanh_done"), sem("h_ready")
        exps_ready = sem("exps_ready")
        out_psum, x_done = sem("out_psum"), sem("x_done")
        gate_bank, out_bank = banks[2:4], banks[4:6]
        block = ctx.enter_context(nc.Block())

        @block.sync
        def _(sp):
            with nc.allow_non_contiguous_dma(reason="vectors as columns"):
                sp.dma_start(lnw[:, :], column(w["L1_attn_ln_w"])).then_inc(ln_loads, 16)
                sp.dma_start(lnb[:, :], column(w["L1_attn_ln_b"])).then_inc(ln_loads, 16)
            for g, n in enumerate("ifzo"):
                sp.dma_start(wg[:, :, g, :], rows(w[f"L1_attn_W{n}"])).then_inc(loads, 16)
            with nc.allow_non_contiguous_dma(reason="biases as columns"):
                for g, n in enumerate("ifzo"):
                    for half in range(2):
                        sp.dma_start(bias[half * N:(half + 1) * N, g:g + 1],
                                     w[f"L1_attn_b{n}"].rearrange("(p a) -> p a", a=1)).then_inc(loads, 16)
            for half in range(2):
                sp.dma_start(wp[half * N:(half + 1) * N, :], w["L1_attn_Wp"]).then_inc(loads, 16)
            sp.dma_start(bp[:, :], everywhere(w["L1_attn_bp"])).then_inc(loads, 16)
            sp.wait_ge(loads, 16 * 15)

        @block.gpsimd
        def _(pool):
            front.pool(pool)

        @block.tensor
        def _(pe):
            front.pe(pe)
            pe.wait_ge(loads, 16 * 15)
            for n in range(8):
                g, c2 = n // 2, n % 2
                if n == 0:
                    pe.wait_ge(front.xt_done, KD * NT)
                if n >= 2:
                    pe.wait_ge(gate_done, n - 1)
                for half in range(2):
                    at = half * HALF + c2 * CH
                    for kd in range(KD):
                        mm = pe.matmul(gate_bank[n % 2][half * N:(half + 1) * N, :], wg[:, kd, g, :],
                                       front.xt[:, 0, kd, at:at + CH], start=kd == 0, stop=kd == KD - 1)
                mm.then_inc(psum, 1)
            pe.wait_ge(h_ready, 1)
            for t in range(NT):
                half, at = t // (NT // 2), t % (NT // 2) * P
                if t >= 2:
                    pe.wait_ge(x_done, t - 1)
                pe.matmul(out_bank[t % 2][:, 0:D], a[half * N:(half + 1) * N, at:at + P],
                          wp[half * N:(half + 1) * N, :], start=True, stop=True).then_inc(out_psum, 1)

        @block.scalar
        def _(act):
            act.wait_ge(ln_loads, 32)
            front.act(act)
            act.wait_ge(loads, 16 * 15)
            for n in range(4, 8):
                g, c2 = n // 2, n % 2
                act.wait_ge(psum, n + 1)
                act.wait_ge(gate_done, n)
                act.activation((z if g == 2 else o)[:, c2 * CH:(c2 + 1) * CH], gate_bank[n % 2][:, :],
                               ACT.Tanh if g == 2 else ACT.Sigmoid, bias=bias[:, g:g + 1]).then_inc(gate_done, 1)
            act.wait_ge(exps_ready, 2)
            act.activation(d1[:, :], d1[:, :], ACT.Exp).then_inc(expo, 1)
            act.activation(f[:, :], f[:, :], ACT.Exp).then_inc(expo, 1)
            act.wait_ge(exps_ready, 3)
            act.activation(a[:, :], c[:, :], ACT.Tanh).then_inc(tanh_done, 1)

        @block.vector
        def _(dve):
            front.dve(dve)
            s = Sem(step)
            dve.wait_ge(loads, 16 * 15)
            for n in range(4):
                g, c2 = n // 2, n % 2
                dve.wait_ge(psum, n + 1)
                dve.tensor_scalar((log_f if g else log_i)[:, c2 * CH:(c2 + 1) * CH], gate_bank[n % 2][:, :],
                                  bias[:, g:g + 1], 20.0, ALU.add, ALU.min).then_inc(gate_done, 1)
            dve.wait_ge(gate_done, 4)
            s.give(dve.tensor_scalar(log_i[:, :], log_i[:, :], -20.0, None, ALU.max))
            s.give(dve.tensor_scalar(log_f[:, :], log_f[:, :], -20.0, None, ALU.max))
            dve.wait_ge(step, s.n)
            s.give(dve.tensor_copy(d1[:, :], log_i[:, :]))
            dve.wait_ge(step, s.n)
            s.give(dve.tensor_tensor(seg(d1)[:, :, 0:1], seg(log_i)[:, :, 0:1], seg(log_f)[:, :, 0:1], ALU.max))
            dve.wait_ge(step, s.n)
            s.give(dve.memset(seg(log_f)[:, :, 0:1], FORGET))
            dve.wait_ge(step, s.n)
            s.give(dve.tensor_tensor_scan(m[:, :], log_f[:, :], d1[:, :], 0.0, ALU.add, ALU.max))
            dve.wait_ge(step, s.n)
            dve.tensor_tensor(d1[:, :], log_i[:, :], m[:, :], ALU.subtract).then_inc(exps_ready, 1)
            s.give(dve.tensor_tensor(seg(f)[:, :, 1:S], seg(log_f)[:, :, 1:S], seg(m)[:, :, 0:S - 1], ALU.add))
            s.give(dve.memset(seg(f)[:, :, 0:1], FORGET))
            dve.wait_ge(step, s.n)
            dve.tensor_tensor(f[:, :], f[:, :], m[:, :], ALU.subtract).then_inc(exps_ready, 1)
            dve.wait_ge(expo, 2)
            dve.wait_ge(gate_done, 8)
            s.give(dve.tensor_tensor(d1[:, :], d1[:, :], z[:, :], ALU.mult))
            dve.wait_ge(step, s.n)
            dve.tensor_tensor_scan(c[:, :], f[:, :], d1[:, :], 0.0, ALU.mult, ALU.add).then_inc(exps_ready, 1)
            s.give(dve.tensor_tensor(x_sb[:, :, :], x_sb[:, :, :], bp[:, :].unsqueeze(1).to_broadcast([P, NT, D]), ALU.add))
            dve.wait_ge(tanh_done, 1)
            dve.tensor_tensor(a[:, :], a[:, :], o[:, :], ALU.mult).then_inc(h_ready, 1)
            dve.wait_ge(step, s.n)
            for t in range(NT):
                dve.wait_ge(out_psum, t + 1)
                dve.tensor_tensor(x_sb[:, t, :], x_sb[:, t, :], out_bank[t % 2][:, 0:D], ALU.add).then_inc(x_done, 1)
            dve.wait_ge(x_done, NT)


def masked_attention(nc, k, x_sb, banks, w):
    HD = 16
    HP = 8
    VW = 2 * HD + 2
    KEYS = 2 * S2
    MASKED = 1e20
    with ExitStack() as ctx:
        tools = Tools(nc, ctx, "mat")
        sem = lambda name: k.stage_sem("mat_" + name)
        front = NormTranspose(tools, sem, x_sb, k.ident[:, :], banks[0:2])
        wq, wkr, wvr, wo = (tools.sb(n, [P, KD, D]) for n in ("wq", "wkr", "wvr", "wo"))
        wk, wv = (tools.sb(n, [P, 2, KD, D], F32R) for n in ("wk", "wv"))
        bq, nbq, bk = (tools.sb(n, [P, KD]) for n in ("bq", "nbq", "bk"))
        bv, bo = tools.sb("bv", [P, D]), tools.sb("bo", [P, D])
        mask_i = tools.sb("mask_i", [P, S2], I32)
        mask = tools.sb("mask", [P, S2])
        half_mask = tools.sb("half_mask", [P, 2])
        qf = tools.sb("qf", [P, 2, CH])
        qt = tools.sb("qt", [P, 2, KD, T], F32R)
        ctx_raw = tools.sb("ctx_raw", [P, KD, KEYS])
        ctx_t = tools.sb("ctx_t", [P, 2, KD, KEYS], F32R)
        q_bd = tools.sb("q_bd", [P, 2, 2, KD, 8, S], F32R)
        kt = tools.sb("kt", [P, 2, KD, KEYS], F32R)
        v = tools.sb("v", [P, 2, 4, HP * VW], F32R)
        mark = tools.sb("mark", [P, 1])
        ones = tools.sb("ones", [P, 4 * HP * 2])
        sc = tools.sb("sc", [P, 2, 2, S2])
        neg_max = tools.sb("neg_max", [P, 16])
        p = tools.sb("p", [P, 2, 2, S2])
        pt = tools.sb("pt", [P, 2, 2, 512], F32R)
        rsum = tools.sb("rsum", [P, HP])
        rmask = tools.sb("rmask", [P, HP, 2])
        o = tools.sb("o", [P, D])
        ot = tools.sb("ot", [P, KD, P])
        loads, consts, pre = sem("loads"), sem("consts"), sem("pre")
        w_hi = sem("w_hi")
        q_psum, q_hi, q_f, q_lo = sem("q_psum"), sem("q_hi"), sem("q_f"), sem("q_lo")
        ctx_in, ctx_split, q_bd_ready = sem("ctx_in"), sem("ctx_split"), sem("q_bd_ready")
        proj_psum, proj_hi, proj_lo = sem("proj_psum"), sem("proj_hi"), sem("proj_lo")
        s_psum, s_min, p_ready = sem("s_psum"), sem("s_min"), sem("p_ready")
        pt_psum, pt_hi, pt_lo = sem("pt_psum"), sem("pt_hi"), sem("pt_lo")
        o_psum, o_step, ot_psum, ot_ready = sem("o_psum"), sem("o_step"), sem("ot_psum"), sem("ot_ready")
        wo_psum, x_done = sem("wo_psum"), sem("x_done")
        proj_bank, s_bank, pt_bank, o_bank, end_bank = banks[0:2], banks[2:4], banks[4], banks[5:7], banks[7]
        s_q = -1.0 / HD ** 0.5
        number = lambda i, kind, b: 4 * i + 2 * b + ("k", "v").index(kind)
        bank_of = {"k": proj_bank[0], "v": proj_bank[1]}
        fillers = {0: ("k", 0, 1), 3: ("v", 0, 1), 6: ("k", 1, 0), 7: ("v", 1, 0)}
        block = ctx.enter_context(nc.Block())

        @block.sync
        def _(sp):
            for dst, n in ((wq, "Wq"), (wkr, "Wk"), (wvr, "Wv"), (wo, "Wo")):
                sp.dma_start(dst[:, :, :], rows(w["L1_xattn_" + n])).then_inc(loads, 16)
            with nc.allow_non_contiguous_dma(reason="biases as columns"):
                sp.dma_start(bq[:, :], column(w["L1_xattn_bq"])).then_inc(loads, 16)
                sp.dma_start(bk[:, :], column(w["L1_xattn_bk"])).then_inc(loads, 16)
            sp.dma_start(bv[:, :], everywhere(w["L1_xattn_bv"])).then_inc(loads, 16)
            sp.dma_start(bo[:, :], everywhere(w["L1_xattn_bo"])).then_inc(loads, 16)
            for half in range(2):
                sp.dma_start(mask_i[half * S:(half + 1) * S, :], w["mask_1x1xSxS2_ik1"]).then_inc(loads, 16)
            keys = rows(w["ctx_turned"])
            sp.dma_start(ctx_raw[:, :, :], keys[:, :, 0:KEYS]).then_inc(ctx_in, 16)
            with sp.Fori(1, NT) as i:
                sp.wait_ge(ctx_split, 2 * i)
                sp.dma_start(ctx_raw[:, :, :], keys[:, :, bass.ds(i * KEYS, KEYS)]).then_inc(ctx_in, 16)
            sp.wait_ge(ctx_in, 16 * NT)
            sp.wait_ge(loads, 16 * 10)

        @block.gpsimd
        def _(pool):
            pool.memset(half_mask[:, :], 1.0).then_inc(consts, 1)
            pool.memset(ones[:, :], 1.0).then_inc(consts, 1)
            pool.wait_ge(consts, 2)
            pool.affine_select(out=half_mask[:, 1:2], in_=half_mask[:, 1:2], compare_op=ALU.is_ge, fill=0.0, base=-S,
                               pattern=[[0, 1]], channel_multiplier=1).then_inc(consts, 1)
            pool.affine_select(out=half_mask[:, 0:1], in_=half_mask[:, 0:1], compare_op=ALU.is_ge, fill=0.0, base=S - 1,
                               pattern=[[0, 1]], channel_multiplier=-1).then_inc(consts, 1)
            front.pool(pool)
            per_head = k.head_mask[:, :].unsqueeze(2).to_broadcast([P, 8, S])

            def split_keys(i):
                pool.wait_ge(ctx_split, 2 * i + 1)
                pool.tensor_tensor(ctx_t[:, 1], ctx_raw[:, :, :], ctx_t[:, 0].bitcast(F32), ALU.subtract).then_inc(ctx_split, 1)

            def block_queries(i, b):
                wait(pool, s_psum, 8 * i - 4 + 4 * b)
                for part in range(2):
                    for m in range(KD):
                        pool.tensor_tensor(q_bd[:, b, part, m],
                                           qt[:, part, m, bass.ds(i * P + b * S, S)].bitcast(F32).unsqueeze(1)
                                           .to_broadcast([P, 8, S]), per_head, ALU.mult).then_inc(q_bd_ready, 1)

            split_keys(0)
            pool.wait_ge(q_lo, 2 * KD * NCH // 2)
            block_queries(0, 0)
            block_queries(0, 1)
            with pool.Fori(1, NT) as i:
                split_keys(i)
                block_queries(i, 0)
                block_queries(i, 1)

        @block.tensor
        def _(pe):
            front.pe(pe)
            pe.wait_ge(loads, 16 * 10)
            for n in range(KD * NCH):
                m, c = n % KD, n // KD
                pe.wait_ge(front.xt_done, max(4 * c + 4, NT if n < 2 else 0))
                if n >= 2:
                    pe.wait_ge(q_lo, n - 1)
                for kd in range(KD):
                    mm = pe.matmul(proj_bank[n % 2][:, :], wq[:, kd, m * P:(m + 1) * P],
                                   front.xt[:, 0, kd, c * CH:(c + 1) * CH], start=kd == 0, stop=kd == KD - 1)
                mm.then_inc(q_psum, 1)
            pe.wait_ge(q_lo, KD * NCH)
            pe.wait_ge(pre, 2)

            def keys_proj(i, b):
                if b == 0:
                    pe.wait_ge(ctx_split, 2 * i + 2)
                wait(pe, proj_lo, number(i, "k", b) - 1)
                for m in range(KD):
                    mm = product3(pe, bank_of["k"][:, m * S2:(m + 1) * S2], lambda a, kd: wk[:, a, kd, m * P:(m + 1) * P],
                                  lambda a, kd: ctx_t[:, a, kd, b * S2:(b + 1) * S2])
                mm.then_inc(proj_psum, 1)

            def values_proj(i, b):
                wait(pe, proj_lo, number(i, "v", b) - 1)
                for t in range(2):
                    at = (2 * b + t) * P
                    mm = product3(pe, bank_of["v"][:, t * D:(t + 1) * D], lambda a, kd: ctx_t[:, a, kd, at:at + P],
                                  lambda a, kd: wv[:, a, kd, :])
                mm.then_inc(proj_psum, 1)

            def energies(i, g):
                b, j = g // 4, g % 4
                if j == 0:
                    pe.wait_ge(q_bd_ready, 8 * i + 4 * b + 4)
                    pe.wait_ge(proj_lo, number(i, "k", b) + 1)
                wait(pe, s_min, 2 * (8 * i + g - 1))
                for n in range(2):
                    u = 2 * j + n
                    m, h = u // 4, u % 4 * 2
                    for jj, (a, c) in enumerate(PASSES):
                        mm = pe.matmul(s_bank[g % 2][:, n * S2:(n + 1) * S2],
                                       q_bd[:, b, a, m, h:h + 2, :].rearrange("p h q -> p (h q)"),
                                       kt[:, c, m, b * S2:(b + 1) * S2], start=jj == 0, stop=jj == 2)
                mm.then_inc(s_psum, 1)

            def turn(i, g):
                pe.wait_ge(p_ready, 2 * (8 * i + g) + 2)
                wait(pe, pt_lo, 8 * i + g)
                for n in range(2):
                    for t in range(2):
                        mm = pe.transpose(pt_bank[:, (2 * n + t) * P:(2 * n + t + 1) * P], p[:, g % 2, n, t * P:(t + 1) * P],
                                          k.ident[:, :])
                mm.then_inc(pt_psum, 1)

            def weigh(i, g):
                b, j = g // 4, g % 4
                pe.wait_ge(pt_lo, 8 * i + g + 1)
                if j == 0:
                    pe.wait_ge(proj_lo, number(i, "v", b) + 1)
                    wait(pe, o_step, 8 * i - 5 + 4 * b if not isinstance(i, int) or i > 0 else 0)
                for n in range(2):
                    u = 2 * j + n
                    for t in range(2):
                        for jj, (a, c) in enumerate(PASSES):
                            mm = pe.matmul(o_bank[b][:, u * VW:(u + 1) * VW], pt[:, g % 2, a, (2 * n + t) * P:(2 * n + t + 1) * P],
                                           v[:, c, 2 * b + t, u * VW:(u + 1) * VW], start=t == 0 and jj == 0,
                                           stop=t == 1 and jj == 2)
                if j == 3:
                    mm.then_inc(o_psum, 1)

            def turn_output(i, b):
                pe.wait_ge(o_step, 4 * (2 * i + b) + 4)
                wait(pe, ot_ready, 2 * i + b)
                wait(pe, x_done, i)
                for m in range(KD):
                    mm = pe.transpose(end_bank[:, m * P:(m + 1) * P], o[:, m * P:(m + 1) * P], k.ident[:, :])
                mm.then_inc(ot_psum, 1)

            def project_output(i):
                pe.wait_ge(ot_ready, 2 * i + 2)
                for kd in range(KD):
                    mm = pe.matmul(end_bank[:, 0:D], ot[:, kd, :], wo[:, kd, :], start=kd == 0, stop=kd == KD - 1)
                mm.then_inc(wo_psum, 1)

            def slot(i, g, first):
                before = (lambda back: (i, g - back) if g >= back else (i - 1, g + 8 - back))
                if g >= 2 or not first:
                    turn(*before(2))
                energies(i, g)
                if g >= 3 or not first:
                    weigh(*before(3))

            def outputs(i, g):
                if g == 0:
                    turn_output(i - 1, 0)
                if g == 4:
                    turn_output(i - 1, 1)
                if g == 5:
                    project_output(i - 1)

            def pair(i, first=False, last=False):
                for g in range(8):
                    slot(i, g, first)
                    if not first:
                        outputs(i, g)
                    if g in fillers:
                        kind, ahead, b = fillers[g]
                        if not (ahead and last):
                            (keys_proj if kind == "k" else values_proj)(i + ahead, b)

            keys_proj(0, 0)
            values_proj(0, 0)
            pair(0, first=True)
            with pe.Fori(1, NT - 1) as i:
                pair(i)
            pair(NT - 1, last=True)
            for g in range(3):
                if g < 2:
                    turn(NT - 1, g + 6)
                weigh(NT - 1, g + 5)
            for g in (0, 4, 5):
                outputs(NT, g)

        @block.scalar
        def _(act):
            front.act(act)
            act.wait_ge(loads, 16 * 10)
            act.copy(wk[:, 0], wkr[:, :, :]).then_inc(w_hi, 1)
            act.copy(wv[:, 0], wvr[:, :, :]).then_inc(w_hi, 1)
            act.wait_ge(pre, 1)
            for n in range(KD * NCH):
                m, c = n % KD, n // KD
                act.wait_ge(q_psum, n + 1)
                if n >= 2:
                    act.wait_ge(q_lo, n - 1)
                act.activation(qf[:, n % 2, :], proj_bank[n % 2][:, :], ACT.Identity, bias=nbq[:, m:m + 1],
                               scale=s_q).then_inc(q_f, 1)

            def keys_proj(i, b):
                act.wait_ge(proj_psum, number(i, "k", b) + 1)
                for m in range(KD):
                    ins = act.activation(kt[:, 0, m, b * S2:(b + 1) * S2], bank_of["k"][:, m * S2:(m + 1) * S2],
                                         ACT.Identity, bias=bk[:, m:m + 1])
                ins.then_inc(proj_hi, 1)

            def values_proj(i, b):
                act.wait_ge(proj_psum, number(i, "v", b) + 1)
                for t in range(2):
                    ins = act.copy(v[:, 0, 2 * b + t, :].rearrange("p (u e) -> p u e", e=VW)[:, :, 0:2 * HD],
                                   bank_of["v"][:, t * D:(t + 1) * D].rearrange("p (u e) -> p u e", e=2 * HD))
                ins.then_inc(proj_hi, 1)

            def weights(i, g):
                for n in range(2):
                    u = 2 * g + n
                    act.wait_ge(s_min, 16 * i + u + 1)
                    act.activation(p[:, g % 2, n, :], sc[:, g % 2, n, :], ACT.Exp, bias=neg_max[:, u:u + 1],
                                   scale=-1.0).then_inc(p_ready, 1)

            def turn(i, g):
                act.wait_ge(pt_psum, 8 * i + g + 1)
                act.copy(pt[:, g % 2, 0, :], pt_bank[:, :]).then_inc(pt_hi, 1)

            def pair(i, first=False):
                for g in range(8):
                    if g == 0 and not first:
                        values_proj(i, 0)
                    if g - 1 in fillers:
                        kind, ahead, b = fillers[g - 1]
                        if ahead == 0 or not isinstance(i, int) or i < NT - 1:
                            (keys_proj if kind == "k" else values_proj)(i + ahead, b)
                    if g >= 2 or not first:
                        turn(*((i, g - 2) if g >= 2 else (i - 1, g + 6)))
                    weights(i, g)

            keys_proj(0, 0)
            values_proj(0, 0)
            pair(0, first=True)
            with act.Fori(1, NT - 1) as i:
                pair(i)
            pair(NT - 1)
            turn(NT - 1, 6)
            turn(NT - 1, 7)

        @block.vector
        def _(dve):
            front.dve(dve)
            dve.wait_ge(loads, 16 * 10)
            dve.tensor_scalar(nbq[:, :], bq[:, :], s_q, None, ALU.mult).then_inc(pre, 1)
            s = Sem(sem("vec_pre"))
            dve.wait_ge(w_hi, 2)
            s.give(dve.tensor_tensor(wk[:, 1], wkr[:, :, :], wk[:, 0].bitcast(F32), ALU.subtract))
            s.give(dve.tensor_tensor(wv[:, 1], wvr[:, :, :], wv[:, 0].bitcast(F32), ALU.subtract))
            dve.wait_ge(consts, 4)
            s.give(dve.tensor_scalar(mask[:, :], mask_i[:, :], 0.0, MASKED, ALU.is_equal, ALU.mult))
            s.give(dve.tensor_tensor(bv[:, :].rearrange("p (u h e) -> p u h e", h=2, e=HD),
                                     bv[:, :].rearrange("p (u h e) -> p u h e", h=2, e=HD),
                                     half_mask[:, :].unsqueeze(1).unsqueeze(3).to_broadcast([P, HP, 2, HD]), ALU.mult))
            for part in range(2):
                dst = v[:, part].rearrange("p t (u e) -> p (t u) e", e=VW)[:, :, 2 * HD:VW]
                if part == 0:
                    s.give(dve.tensor_copy(dst, ones[:, :].rearrange("p (t e) -> p t e", e=2)))
                else:
                    s.give(dve.tensor_scalar(dst, ones[:, :].rearrange("p (t e) -> p t e", e=2), 0.0, None, ALU.mult))
            dve.wait_ge(s.sem, s.n)
            dve.engine_nop().then_inc(pre, 1)
            dve.wait_ge(front.xn_ready, NT)
            dve.tensor_tensor(x_sb[:, :, :], x_sb[:, :, :], bo[:, :].unsqueeze(1).to_broadcast([P, NT, D]),
                              ALU.add).then_inc(q_hi, 1)
            for n in range(KD * NCH):
                m, c = n % KD, n // KD
                dve.wait_ge(q_f, n + 1)
                dve.tensor_copy(qt[:, 0, m, c * CH:(c + 1) * CH], qf[:, n % 2, :]).then_inc(q_hi, 1)
                dve.wait_ge(q_hi, n + 2)
                dve.tensor_tensor(qt[:, 1, m, c * CH:(c + 1) * CH], qf[:, n % 2, :],
                                  qt[:, 0, m, c * CH:(c + 1) * CH].bitcast(F32), ALU.subtract).then_inc(q_lo, 1)

            def keys_proj(i, b):
                dve.wait_ge(proj_hi, number(i, "k", b) + 1)
                for m in range(KD):
                    cols = lambda part: kt[:, part, m, b * S2:(b + 1) * S2]
                    ins = dve.scalar_tensor_tensor(out=cols(1), in0=bank_of["k"][:, m * S2:(m + 1) * S2],
                                                   scalar=bk[:, m:m + 1], in1=cols(0).bitcast(F32), op0=ALU.add,
                                                   op1=ALU.subtract)
                ins.then_inc(proj_lo, 1)

            def values_proj(i, b):
                dve.wait_ge(proj_hi, number(i, "v", b) + 1)
                cols = lambda part: v[:, part, 2 * b:2 * b + 2, :].rearrange(
                    "p t (u e) -> p (t u) e", e=VW)[:, :, 0:2 * HD]
                dve.tensor_tensor(cols(1), bank_of["v"][:, :].rearrange("p (u e) -> p u e", e=2 * HD),
                                  cols(0).bitcast(F32), ALU.subtract).then_inc(proj_lo, 1)

            def energies(i, g):
                dve.wait_ge(s_psum, 8 * i + g + 1)
                wait(dve, p_ready, 2 * (8 * i + g - 1))
                dve.memset(mark[:, :], 0.0)
                for n in range(2):
                    u = 2 * g + n
                    dve.tensor_tensor_reduce(sc[:, g % 2, n, :], s_bank[g % 2][:, n * S2:(n + 1) * S2], mask[:, :],
                                             1.0, 3e38, ALU.add, ALU.min, neg_max[:, u:u + 1]).then_inc(s_min, 1)

            def turn(i, g):
                dve.wait_ge(pt_hi, 8 * i + g + 1)
                dve.tensor_tensor(pt[:, g % 2, 1, :], pt_bank[:, :], pt[:, g % 2, 0, :].bitcast(F32),
                                  ALU.subtract).then_inc(pt_lo, 1)

            def normalise(i, b):
                done = 4 * (2 * i + b)
                dve.wait_ge(o_psum, 2 * i + b + 1)
                src = o_bank[b][:, 0:HP * VW].rearrange("p (u e) -> p u e", e=VW)
                dve.reciprocal(rsum[:, :], src[:, :, 2 * HD]).then_inc(o_step, 1)
                dve.wait_ge(o_step, done + 1)
                dve.tensor_tensor(rmask[:, :, :], rsum[:, :].unsqueeze(2).to_broadcast([P, HP, 2]),
                                  half_mask[:, :].unsqueeze(1).to_broadcast([P, HP, 2]), ALU.mult).then_inc(o_step, 1)
                dve.wait_ge(o_step, done + 2)
                dve.tensor_tensor(o[:, :].rearrange("p (u h e) -> p u h e", h=2, e=HD),
                                  src[:, :, 0:2 * HD].rearrange("p u (h e) -> p u h e", h=2),
                                  rmask[:, :, :].unsqueeze(3).to_broadcast([P, HP, 2, HD]), ALU.mult).then_inc(o_step, 1)
                dve.wait_ge(o_step, done + 3)
                dve.tensor_tensor(o[:, :], o[:, :], bv[:, :], ALU.add).then_inc(o_step, 1)

            def turn_output(i, b):
                dve.wait_ge(ot_psum, 2 * i + b + 1)
                dve.tensor_reduce(ot[:, :, b * S:(b + 1) * S],
                                  end_bank[:, 0:KD * P].rearrange("p (m h q) -> p m q h", m=KD, h=2),
                                  AX.X, ALU.add).then_inc(ot_ready, 1)

            def residual(i):
                dve.wait_ge(wo_psum, i + 1)
                row = x_sb[:, bass.ds(i, 1), :].rearrange("p a d -> p (a d)")
                dve.tensor_tensor(row, row, end_bank[:, 0:D], ALU.add).then_inc(x_done, 1)

            def split_keys(i):
                dve.wait_ge(ctx_in, 16 * i + 16)
                dve.tensor_copy(ctx_t[:, 0], ctx_raw[:, :, :]).then_inc(ctx_split, 1)

            def outputs(i, g):
                if g == 0:
                    turn_output(i - 1, 0)
                if g == 3:
                    normalise(i - 1, 1)
                if g == 4:
                    turn_output(i - 1, 1)
                if g == 5:
                    residual(i - 1)

            def pair(i, first=False, last=False):
                for g in range(8):
                    if g == 0 and not first:
                        values_proj(i, 0)
                    if g - 1 in fillers:
                        kind, ahead, b = fillers[g - 1]
                        if not (ahead and last):
                            (keys_proj if kind == "k" else values_proj)(i + ahead, b)
                    if g == 4 and not last:
                        split_keys(i + 1)
                    if g >= 2 or not first:
                        turn(*((i, g - 2) if g >= 2 else (i - 1, g + 6)))
                    energies(i, g)
                    if not first:
                        outputs(i, g)
                    if g == 7:
                        normalise(i, 0)

            split_keys(0)
            keys_proj(0, 0)
            values_proj(0, 0)
            pair(0, first=True)
            with dve.Fori(1, NT - 1) as i:
                pair(i)
            pair(NT - 1, last=True)
            turn(NT - 1, 6)
            turn(NT - 1, 7)
            for g in (0, 3, 4, 5):
                outputs(NT, g)
            dve.wait_ge(x_done, NT)


def experts(nc, k, x_sb, banks, w):
    E, F = 8, 1024
    NF = F // P
    BISECTIONS = 25
    THRESH = 1e-9
    STEPS = NCH * NF
    with ExitStack() as ctx:
        tools = Tools(nc, ctx, "moe")
        sem = lambda name: k.stage_sem("moe_" + name)
        front = NormTranspose(tools, sem, x_sb, k.ident[:, :], banks[0:2], split=True)
        acc = front.xn[:, :, :].rearrange("p t d -> p (t d)").rearrange("p (m n) -> p m n", m=KD)
        wr, wrs = tools.sb("wr", [P, KD, E]), tools.sb("wrs", [P, 2, KD, E], F32R)
        br = tools.sb("br", [P, E])
        xs, dif, sq = (tools.sb(n, [P, NT, E]) for n in ("xs", "dif", "sq"))
        top, tau, dm, tau_m, f_lo, f_m, inc = (tools.sb(n, [P, NT]) for n in
                                               ("top", "tau", "dm", "tau_m", "f_lo", "f_m", "inc"))
        gates_t = tools.sb("gates_t", [P, P])
        gate8 = tools.sb("gate8", [E, T])
        b1r, b1 = tools.sb("b1r", [E * NF, P]), tools.sb("b1", [P, E * NF])
        b1e = tools.sb("b1e", [P, 2, NF])
        b2 = tools.sb("b2", [E, D])
        w1raw, w2raw = tools.sb("w1raw", [P, 2, KD, F]), tools.sb("w2raw", [P, 2, NF, D])
        w1, w2 = tools.sb("w1", [P, 2, 2, KD, F], F32R), tools.sb("w2", [P, 2, 2, NF, D], F32R)
        gate_all = tools.sb("gate_all", [P, 2, NT, P])
        h, hr = tools.sb("h", [P, 2, 2, CH], F32R), tools.sb("hr", [P, 2, CH])
        weighted = tools.sb("weighted", [P, 2, CH])
        loads, w_in, gate_in = sem("loads"), [sem("w_in0"), sem("w_in1")], [sem("gate_in0"), sem("gate_in1")]
        small_psum, small_done = sem("small_psum"), sem("small_done")
        bias_psum = sem("bias_psum")
        w0_hi, w0_lo, b1_col0 = sem("w0_hi"), sem("w0_lo"), sem("b1_col0")
        split_step, ent, gates_ready = sem("split_step"), sem("ent"), sem("gates_ready")
        gate_stored, gate8_in = sem("gate_stored"), sem("gate8_in")
        b2_psum, b2_added = sem("b2_psum"), sem("b2_added")
        w_hi, w_lo, b1_cols = sem("w_hi"), sem("w_lo"), sem("b1_cols")
        h_psum, h_hi, h_lo = sem("h_psum"), sem("h_hi"), sem("h_lo")
        y_psum, y_read, acc_step = sem("y_psum"), sem("y_read"), sem("acc_step")
        back_psum, x_done = sem("back_psum"), sem("x_done")
        h_bank = banks[0:2]
        y_bank = banks[2:6]
        small, side = banks[6], banks[7]
        block = ctx.enter_context(nc.Block())

        @block.sync
        def _(sp):
            with nc.allow_non_contiguous_dma(reason="the router's weights are narrow"):
                sp.dma_start(wr[:, :, :], rows(w["L1_ffn_Wr"])).then_inc(loads, 16)
            sp.dma_start(br[:, :], everywhere(w["L1_ffn_br"])).then_inc(loads, 16)
            sp.dma_start(b1r[:, :], w["L1_ffn_b1"].rearrange("e (f p) -> (e f) p", p=P)).then_inc(loads, 16)
            sp.dma_start(b2[:, :], w["L1_ffn_b2"]).then_inc(loads, 16)

            def load_weights(e, par):
                if isinstance(e, int) and e == 2:
                    sp.wait_ge(w0_lo, 2)
                else:
                    wait(sp, w_lo, 2 * e - 4)
                sp.dma_start(w1raw[:, par], w["L1_ffn_W1"][bass.ds(e, 1), :, :].rearrange(
                    "a (k p) n -> p (a k) n", p=P)).then_inc(w_in[par], 16)
                sp.dma_start(w2raw[:, par], w["L1_ffn_W2"][bass.ds(e, 1), :, :].rearrange(
                    "a (k p) n -> p (a k) n", p=P)).then_inc(w_in[par], 16)

            def load_gates(e, par):
                wait(sp, acc_step, 8 * e - 8)
                sp.dma_start(gate_all[:, par], k.scratch[:, bass.ds(e, 1), :].rearrange("t a p -> (t a) p")
                             .partition_broadcast(P)).then_inc(gate_in[par], 16)

            load_weights(0, 0)
            load_weights(1, 1)
            sp.wait_ge(gates_ready, 2)
            sp.dma_start(k.scratch.rearrange("t e p -> (t e) p"), gates_t[:, :]).then_inc(gate_stored, 16)
            sp.wait_ge(gate_stored, 16)
            sp.dma_start(gate8[:, :].rearrange("e (t p) -> e t p", p=P),
                         k.scratch.rearrange("t e p -> e t p")).then_inc(gate8_in, 16)
            load_gates(0, 0)
            load_gates(1, 1)

            def load_two(i):
                for par in range(2):
                    load_weights(2 * i + par, par)
                    load_gates(2 * i + par, par)

            load_two(1)
            with sp.Fori(2, E // 2) as i:
                load_two(i)
            for par in range(2):
                sp.wait_ge(w_in[par], 32 * (E // 2))
                sp.wait_ge(gate_in[par], 16 * (E // 2))
            sp.wait_ge(loads, 64)
            sp.wait_ge(gate8_in, 16)

        @block.gpsimd
        def _(pool):
            front.pool(pool)
            pool.wait_ge(w0_hi, 1)
            pool.tensor_tensor(w1[:, 0, 1], w1raw[:, 0], w1[:, 0, 0].bitcast(F32), ALU.subtract).then_inc(w0_lo, 1)
            pool.wait_ge(w0_hi, 2)
            pool.tensor_tensor(w2[:, 0, 1], w2raw[:, 0], w2[:, 0, 0].bitcast(F32), ALU.subtract).then_inc(w0_lo, 1)
            with pool.Fori(0, E * STEPS // 2) as i:
                for par in range(2):
                    pool.wait_ge(h_hi, 2 * i + par + 1)
                    pool.tensor_tensor(h[:, par, 1, :], hr[:, par, :], h[:, par, 0, :].bitcast(F32),
                                       ALU.subtract).then_inc(h_lo, 1)

        @block.tensor
        def _(pe):
            front.pe(pe)
            pe.wait_ge(loads, 64)
            pe.transpose(side[:, 0:E * NF], b1r[:, :], k.ident[0:E * NF, 0:E * NF]).then_inc(bias_psum, 1)
            pe.wait_ge(split_step, 2)
            pe.wait_ge(front.xt_done, NT)
            for t in range(NT):
                mm = product3(pe, small[:, t * E:(t + 1) * E], lambda a, kd: front.xt[:, a, kd, t * P:(t + 1) * P],
                              lambda a, kd: wrs[:, a, kd, :])
            mm.then_inc(small_psum, 1)

            def turn_gates():
                pe.wait_ge(gates_ready, 1)
                pe.transpose(small[:, 0:P], xs[:, :, :].rearrange("p t e -> p (t e)"), k.ident[:, :]).then_inc(small_psum, 1)

            def gated_bias():
                pe.wait_ge(gate8_in, 16)
                for n in range(NT // 2):
                    if n >= 2:
                        pe.wait_ge(b2_added, n - 1)
                    if n == 0:
                        pe.wait_ge(gates_ready, 2)
                    for t in range(2):
                        at = (2 * n + t) * P
                        mm = pe.matmul(banks[6 + n % 2][:, t * D:(t + 1) * D], gate8[:, at:at + P], b2[:, :],
                                       start=True, stop=True)
                    mm.then_inc(b2_psum, 1)

            def split_ready(e, which):
                if isinstance(e, int) and e == 0:
                    pe.wait_ge(w0_lo, which)
                else:
                    pe.wait_ge(w_lo, 2 * e - 2 + which)

            def hidden(e, par, n):
                c, f = n // NF, n % NF
                if n == 0:
                    split_ready(e, 1)
                step = STEPS * e + n
                wait(pe, h_hi, step - 1)
                product3(pe, h_bank[n % 2][:, :], lambda a, kd: w1[:, par, a, kd, f * P:(f + 1) * P],
                         lambda a, kd: front.xt[:, a, kd, c * CH:(c + 1) * CH]).then_inc(h_psum, 1)

            def output(e, par, n):
                c, f = n // NF, n % NF
                if n == 0:
                    split_ready(e, 2)
                pe.wait_ge(h_hi, STEPS * e + n + 1)
                if f == 0:
                    wait(pe, y_read, 2 * (NCH * e + c) - 2)
                for a, b in ((0, 0), (1, 0), (0, 1)):
                    if b == 1:
                        pe.wait_ge(h_lo, STEPS * e + n + 1)
                    for m in range(KD):
                        mm = pe.matmul(y_bank[c % 2 * 2 + m][:, :], w2[:, par, a, f, m * P:(m + 1) * P], h[:, n % 2, b, :],
                                       start=f == 0 and (a, b) == (0, 0), stop=f == NF - 1 and b == 1)
                if f == NF - 1:
                    mm.then_inc(y_psum, 1)

            def two_experts(i, first=False):
                for n in range(2 * STEPS):
                    hidden(2 * i + n // STEPS, n // STEPS, n % STEPS)
                    if n >= 1:
                        output(2 * i + (n - 1) // STEPS, (n - 1) // STEPS, (n - 1) % STEPS)
                    if first and n == STEPS + 1:
                        turn_gates()
                    if first and n == STEPS + STEPS // 2:
                        gated_bias()
                output(2 * i + 1, 1, STEPS - 1)

            two_experts(0, first=True)
            with pe.Fori(1, E // 2) as i:
                two_experts(i)
            pe.wait_ge(acc_step, KD * NCH * E)
            for t in range(NT):
                if t >= 2:
                    pe.wait_ge(x_done, t - 1)
                for m in range(KD):
                    mm = pe.transpose(banks[t % 2][:, m * P:(m + 1) * P], acc[:, m, t * P:(t + 1) * P], k.ident[:, :])
                mm.then_inc(back_psum, 1)

        @block.scalar
        def _(act):
            act.wait_ge(w_in[0], 32)
            act.copy(w1[:, 0, 0], w1raw[:, 0]).then_inc(w0_hi, 1)
            front.act(act)
            act.copy(w2[:, 0, 0], w2raw[:, 0]).then_inc(w0_hi, 1)
            act.wait_ge(loads, 64)
            act.copy(wrs[:, 0], wr[:, :, :]).then_inc(split_step, 1)
            act.wait_ge(bias_psum, 1)
            act.copy(b1[:, :], side[:, 0:E * NF]).then_inc(small_done, 1)
            act.copy(b1e[:, 0, :], side[:, 0:NF]).then_inc(b1_col0, 1)

            def keep_output(c):
                act.wait_ge(y_psum, c + 1)
                for m in range(KD):
                    act.copy(acc[:, m, c * CH:(c + 1) * CH], y_bank[c % 2 * 2 + m][:, :]).then_inc(y_read, 1)

            def two_experts(i, first=False):
                for par in range(2):
                    e = 2 * i + par
                    for n in range(STEPS):
                        if n == 0:
                            wait(act, b1_cols, e)
                            if first and par == 0:
                                act.wait_ge(b1_col0, 1)
                        wait(act, h_lo, STEPS * e + n - 1)
                        act.wait_ge(h_psum, STEPS * e + n + 1)
                        act.activation(hr[:, n % 2, :], h_bank[n % 2][:, :], ACT.Relu, bias=b1e[:, par, n % NF:n % NF + 1])
                        act.activation(h[:, n % 2, 0, :], h_bank[n % 2][:, :], ACT.Relu,
                                       bias=b1e[:, par, n % NF:n % NF + 1]).then_inc(h_hi, 1)
                        step = par * STEPS + n
                        if first and step % NF == 1 and NF < step <= STEPS + 1:
                            keep_output(step // NF - 1)
                        if first and step == STEPS + 1:
                            act.wait_ge(small_psum, 2)
                            act.copy(gates_t[:, :], small[:, 0:P]).then_inc(gates_ready, 1)

            two_experts(0, first=True)
            with act.Fori(1, E // 2) as i:
                two_experts(i)

        @block.vector
        def _(dve):
            front.dve(dve)
            dve.wait_ge(loads, 64)
            dve.wait_ge(split_step, 1)
            dve.tensor_tensor(wrs[:, 1], wr[:, :, :], wrs[:, 0].bitcast(F32), ALU.subtract).then_inc(split_step, 1)

            def split_weights(i, par):
                e = 2 * i + par
                dve.wait_ge(w_in[par], 32 * i + 32)
                wait(dve, y_psum, NCH * (e - 1))
                dve.tensor_copy(w1[:, par, 0], w1raw[:, par]).then_inc(w_hi, 1)
                dve.tensor_copy(w2[:, par, 0], w2raw[:, par]).then_inc(w_hi, 1)
                dve.wait_ge(w_hi, 2 * e - 1)
                dve.tensor_tensor(w1[:, par, 1], w1raw[:, par], w1[:, par, 0].bitcast(F32), ALU.subtract).then_inc(w_lo, 1)
                dve.tensor_copy(b1e[:, par, :], b1[:, bass.ds(e * NF, NF)]).then_inc(b1_cols, 1)
                dve.wait_ge(w_hi, 2 * e)
                dve.tensor_tensor(w2[:, par, 1], w2raw[:, par], w2[:, par, 0].bitcast(F32), ALU.subtract).then_inc(w_lo, 1)

            s = Sem(ent)
            each = lambda v: v[:, :].unsqueeze(2).to_broadcast([P, NT, E])

            def go(ins):
                s.give(ins)
                dve.wait_ge(ent, s.n)

            dve.wait_ge(small_psum, 1)
            go(dve.tensor_tensor(xs[:, :, :], small[:, 0:NT * E].rearrange("p (t e) -> p t e", e=E),
                                 br[:, :].unsqueeze(1).to_broadcast([P, NT, E]), ALU.add))
            go(dve.tensor_scalar(xs[:, :, :], xs[:, :, :], 0.5, None, ALU.mult))
            go(dve.tensor_reduce(top[:, :], xs[:, :, :], AX.X, ALU.max))
            s.give(dve.tensor_scalar(tau[:, :], top[:, :], 1.0, None, ALU.subtract))
            go(dve.tensor_scalar(dm[:, :], top[:, :], (1.0 / E) ** 0.5, None, ALU.subtract))
            go(dve.tensor_tensor(dm[:, :], dm[:, :], tau[:, :], ALU.subtract))
            go(dve.tensor_tensor(dif[:, :, :], xs[:, :, :], each(tau), ALU.subtract))
            go(dve.scalar_tensor_tensor(out=sq[:, :, :], in0=dif[:, :, :], scalar=0.0, in1=dif[:, :, :],
                                        op0=ALU.max, op1=ALU.mult))
            go(dve.tensor_reduce(f_lo[:, :], sq[:, :, :], AX.X, ALU.add))
            go(dve.tensor_scalar(f_lo[:, :], f_lo[:, :], 1.0, None, ALU.subtract))
            base, per = s.n, 8
            with dve.Fori(0, BISECTIONS) as it:
                def then(n, ins, it=it):
                    ins.then_inc(ent, 1)
                    dve.wait_ge(ent, it * per + (base + n))

                then(1, dve.tensor_scalar(dm[:, :], dm[:, :], 0.5, None, ALU.mult))
                then(2, dve.tensor_tensor(tau_m[:, :], tau[:, :], dm[:, :], ALU.add))
                then(3, dve.tensor_tensor(dif[:, :, :], xs[:, :, :], each(tau_m), ALU.subtract))
                then(4, dve.scalar_tensor_tensor(out=sq[:, :, :], in0=dif[:, :, :], scalar=0.0, in1=dif[:, :, :],
                                                 op0=ALU.max, op1=ALU.mult))
                then(5, dve.tensor_reduce(f_m[:, :], sq[:, :, :], AX.X, ALU.add))
                then(6, dve.scalar_tensor_tensor(out=f_m[:, :], in0=f_m[:, :], scalar=1.0, in1=f_lo[:, :],
                                                 op0=ALU.subtract, op1=ALU.mult))
                then(7, dve.scalar_tensor_tensor(out=inc[:, :], in0=f_m[:, :], scalar=0.0, in1=dm[:, :],
                                                 op0=ALU.is_ge, op1=ALU.mult))
                then(8, dve.tensor_tensor(tau[:, :], tau[:, :], inc[:, :], ALU.add))
            s.n = base + per * BISECTIONS
            go(dve.tensor_reduce(f_m[:, :], sq[:, :, :], AX.X, ALU.add))
            go(dve.reciprocal(f_m[:, :], f_m[:, :]))
            go(dve.tensor_tensor(dif[:, :, :], sq[:, :, :], each(f_m), ALU.mult))
            dve.scalar_tensor_tensor(out=xs[:, :, :], in0=dif[:, :, :], scalar=THRESH, in1=dif[:, :, :],
                                     op0=ALU.is_gt, op1=ALU.mult).then_inc(gates_ready, 1)

            def add_output(i, par, c):
                e = 2 * i + par
                chunk = NCH * e + c
                if c == 0:
                    dve.wait_ge(gate_in[par], 16 * i + 16)
                dve.wait_ge(y_psum, chunk + 1)
                for m in range(KD):
                    dve.wait_ge(acc_step, 2 * chunk - 1 + m)
                    dve.tensor_tensor(weighted[:, m, :], y_bank[c % 2 * 2 + m][:, :],
                                      gate_all[:, par, 4 * c:4 * c + 4, :].rearrange("p t n -> p (t n)"),
                                      ALU.mult).then_inc(y_read, 1)
                for m in range(KD):
                    dve.wait_ge(y_read, 2 * chunk + 1 + m)
                    dve.tensor_tensor(acc[:, m, c * CH:(c + 1) * CH], acc[:, m, c * CH:(c + 1) * CH], weighted[:, m, :],
                                      ALU.add).then_inc(acc_step, 1)

            def weigh_first():
                dve.wait_ge(gate_in[0], 16)
                dve.wait_ge(y_read, KD * NCH)
                for c in range(NCH):
                    for m in range(KD):
                        part = acc[:, m, c * CH:(c + 1) * CH]
                        dve.tensor_tensor(part, part, gate_all[:, 0, 4 * c:4 * c + 4, :].rearrange("p t n -> p (t n)"),
                                          ALU.mult).then_inc(acc_step, 1)
                dve.wait_ge(acc_step, KD * NCH)

            def gated_bias():
                for n in range(NT // 2):
                    dve.wait_ge(b2_psum, n + 1)
                    two = x_sb[:, 2 * n:2 * n + 2, :]
                    dve.tensor_tensor(two, two, banks[6 + n % 2][:, :].rearrange("p (t d) -> p t d", t=2),
                                      ALU.add).then_inc(b2_added, 1)
                dve.wait_ge(b2_added, NT // 2)

            def expert(i, par, first=False, last=False):
                add_output(i, par, 0)
                add_output(i, par, 1)
                if first:
                    gated_bias()
                if not last:
                    split_weights(i + par, 1 - par)
                add_output(i, par, 2)
                add_output(i, par, 3)

            dve.wait_ge(small_done, 1)
            split_weights(0, 1)
            weigh_first()
            expert(0, 1, first=True)
            with dve.Fori(1, E // 2 - 1) as i:
                for par in range(2):
                    expert(i, par)
            expert(E // 2 - 1, 0)
            expert(E // 2 - 1, 1, last=True)
            for t in range(NT):
                dve.wait_ge(back_psum, t + 1)
                dve.tensor_tensor(x_sb[:, t, :], x_sb[:, t, :], banks[t % 2][:, 0:D], ALU.add).then_inc(x_done, 1)
            dve.wait_ge(x_done, NT)


def latent_attention(nc, k, x_sb, banks, w):
    INNER = 1024
    HD = 64
    NU = INNER // P
    KT = 5
    LK = S2 + S
    ALL = KT * P
    PROJ = 34
    with ExitStack() as ctx:
        tools = Tools(nc, ctx, "lat")
        sem = lambda name: k.stage_sem("lat_" + name)
        norm_x = NormStats(tools, NT, sem("x_stats"), sem("x_rstd"), "x")
        norm_c = NormStats(tools, 4, sem("c_stats"), sem("c_rstd"), "c")
        xl = tools.sb("xl", [P, NT, D])
        g_kv, b_kv, g_l, b_l = (tools.sb(n, [P, KD]) for n in ("g_kv", "b_kv", "g_l", "b_l"))
        wq, wk, wv = (tools.sb(n, [P, 2, KD, INNER], F32R) for n in ("wq", "wk", "wv"))
        wo = tools.sb("wo", [P, 2, NU, D], F32R)
        ctx_raw = tools.sb("ctx_raw", [P, 4, D])
        ctx_n = tools.sb("ctx_n", [P, 4, D])
        kv_t = tools.sb("kv_t", [P, 2, KD, 6 * P], F32R)
        kv_f = tools.sb("kv_f", [P, 2, 512])
        q_bd = tools.sb("q_bd", [P, 2, 2, NU, P], F32R)
        kt = tools.sb("kt", [P, 2, 2, ALL], F32R)
        v = tools.sb("v", [P, 2, 2, KT, 2 * P], F32R)
        p = tools.sb("p", [P, 4, 3 * P])
        pt = tools.sb("pt", [P, 2, 3, 2, P], F32R)
        at = tools.sb("at", [P, 2, NU, P], F32R)
        at_c, at_f = tools.sb("at_c", [P, 2, P]), tools.sb("at_f", [P, 2, P])

        def own_sum(hp, h, c):
            return o_bank[hp % 2][h * HD:(h + 1) * HD, :].rearrange("p (b c h q) -> p b c h q", b=2, c=2, h=2)[:, :, c, h, :]

        def own_rows(dst, hp, h):
            return dst[h * HD:(h + 1) * HD, hp % 2, :].rearrange("p (b q) -> p b q", q=S)

        raw = [tools.sb(f"raw{n}", [P, KD * INNER]) for n in range(2)]
        neg_max, rsum, rinv = (tools.sb(n, [P, 16]) for n in ("neg_max", "rsum", "rinv"))
        loads, consts, w_hi, w_lo = sem("loads"), sem("consts"), sem("w_hi"), sem("w_lo")
        w_in = [sem("w_in0"), sem("w_in1")]
        ctx_in, ctx_ready, xl_ready = sem("ctx_in"), sem("ctx_ready"), sem("xl_ready")
        proj_psum, proj_hi, proj_f, proj_lo = sem("proj_psum"), sem("proj_hi"), sem("proj_f"), sem("proj_lo")
        s_psum, s_max, p_exp, p_inv, p_ready = sem("s_psum"), sem("s_max"), sem("p_exp"), sem("p_inv"), sem("p_ready")
        pt_psum, pt_hi, pt_lo = sem("pt_psum"), sem("pt_hi"), sem("pt_lo")
        o_psum, o_part, o_sum, o_hi, o_lo, wo_psum, x_done = sem("o_psum"), sem("o_part"), sem("o_sum"), sem("o_hi"), sem("o_lo"), sem("wo_psum"), sem("x_done")
        proj_bank, s_bank, pt_bank, o_bank, wo_bank = banks[0:2], banks[2:4], (banks[4], banks[7]), banks[5:7], banks[7]
        weights = ((wq, "L0_xattn_Wq", 0), (wk, "L0_xattn_Wkv", 0), (wv, "L0_xattn_Wkv", INNER), (wo, "L0_xattn_Wo", None))

        def fillers(u):
            steps = []
            hp = u // 2 + 1
            if hp < NU:
                steps.append(("k", hp, u % 2))
            if u % 4 < 3:
                steps.append(("v", u // 4, u % 4))
            return steps

        def numbered():
            steps = [("t", kd, n) for kd in range(KD) for n in range(2)] + [("q", 0, 0), ("q", 1, 0), ("k", 0, 0), ("k", 0, 1)]
            for u in range(16):
                steps += fillers(u)
            assert len(steps) == PROJ
            return {s: n for n, s in enumerate(steps)}

        number = numbered()
        HI = PROJ - 4 + 2

        def hi_number(n):
            return n + 1 - 4 + 2

        def both_contexts(part, kd):
            return kv_t[:, part, kd, :].rearrange("p (n c) -> p n c", n=2)[:, :, 0:2 * P]

        t_hi = sem("t_hi")
        xl_now = tools.sb("xl_now", [P, D])

        block = ctx.enter_context(nc.Block())

        @block.sync
        def _(sp):
            with nc.allow_non_contiguous_dma(reason="vectors as columns"):
                for dst, n in ((g_kv, "ln1_g"), (b_kv, "ln1_b"), (g_l, "ln2_g"), (b_l, "ln2_b")):
                    sp.dma_start(dst[:, :], column(w["L0_xattn_" + n])).then_inc(loads, 16)
            pairs = w["ctx_1024"].rearrange("(t p) d -> p t d", p=P)
            sp.dma_start(ctx_raw[:, :, :], pairs[:, 0:4, :]).then_inc(ctx_in, 16)
            for n, (dst, name, col) in enumerate(weights):
                if n >= 2:
                    sp.wait_ge(w_lo, n - 1)
                stage = raw[n % 2][:, :]
                if col is None:
                    sp.dma_start(stage.rearrange("p (k n) -> p k n", n=D), rows(w[name])).then_inc(w_in[n % 2], 16)
                else:
                    sp.dma_start(stage.rearrange("p (k n) -> p k n", n=INNER),
                                 rows(w[name])[:, :, col:col + INNER]).then_inc(w_in[n % 2], 16)
            with sp.Fori(1, NT) as i:
                sp.wait_ge(ctx_ready, 4 * i)
                sp.dma_start(ctx_raw[:, :, :], pairs[:, bass.ds(4 * i, 4), :]).then_inc(ctx_in, 16)
            sp.wait_ge(ctx_in, 16 * NT)
            sp.wait_ge(loads, 64)
            for n in range(2):
                sp.wait_ge(w_in[n], 32)

        @block.gpsimd
        def _(pool):
            norm_x.power_setup(pool, consts)
            norm_c.power_setup(pool, consts)
            pool.memset(p[:, :, :], 0.0).then_inc(consts, 1)
            pool.memset(q_bd[:, :, :, :, :].bitcast(F32), 0.0).then_inc(consts, 1)
            pool.wait_ge(consts, 4)
            norm_c.power(pool, 0)
            norm_x.power(pool, 0)

            def split_weights(n, dst):
                pool.wait_ge(w_hi, n + 1)
                pool.tensor_tensor(dst[:, 1].rearrange("p k n -> p (k n)"), raw[n % 2][:, :],
                                   dst[:, 0].rearrange("p k n -> p (k n)").bitcast(F32), ALU.subtract).then_inc(w_lo, 1)

            for n in range(2):
                split_weights(n, weights[n][0])
            norm_x.power(pool, norm_x.steps)
            for n in range(2, 4):
                split_weights(n, weights[n][0])

            def output(i, hp):
                pool.wait_ge(o_hi, NU * i + hp + 1)
                pool.tensor_tensor(at[:, 1, hp, :], at_f[:, hp % 2, :], at[:, 0, hp, :].bitcast(F32),
                                   ALU.subtract).then_inc(o_lo, 1)

            def pair(i, last=False):
                for hp in range(NU):
                    output(i, hp)
                    if hp == 1 and not last:
                        norm_c.power(pool, (i + 1) * norm_c.steps)

            with pool.Fori(0, NT - 1) as i:
                pair(i)
            pair(NT - 1, last=True)

        @block.tensor
        def _(pe):
            def bank(i, kind, a, b):
                n = number[kind, a, b]
                wait(pe, proj_lo, PROJ * i + n - 1)
                return proj_bank[n % 2]

            def turn_keys(i, kd):
                for half in range(2):
                    dst = bank(i, "t", kd, half)
                    if kd == 0 and half == 0:
                        pe.wait_ge(ctx_ready, 4 * i + 4)
                    for n, t in enumerate((0, 1, 2, 3) if half == 0 else (None,)):
                        src = xl_now[:, kd * P:(kd + 1) * P] if t is None else ctx_n[:, t, kd * P:(kd + 1) * P]
                        mm = pe.transpose(dst[:, n * P:(n + 1) * P], src, k.ident[:, :])
                    mm.then_inc(proj_psum, 1)

            def queries(i, half):
                dst = bank(i, "q", half, 0)
                if half == 0:
                    pe.wait_ge(proj_lo, PROJ * i + 4)
                for n in range(4):
                    u = 4 * half + n
                    mm = product3(pe, dst[:, n * P:(n + 1) * P], lambda a, kd: wq[:, a, kd, u * P:(u + 1) * P],
                                  lambda a, kd: kv_t[:, a, kd, 2 * P:3 * P])
                mm.then_inc(proj_psum, 1)

            def keys_proj(i, hp, half):
                dst = bank(i, "k", hp, half)
                product3(pe, dst[:, 0:LK], lambda a, kd: wk[:, a, kd, hp * P:(hp + 1) * P],
                         lambda a, kd: kv_t[:, a, kd, half * LK:(half + 1) * LK]).then_inc(proj_psum, 1)

            def values_proj(i, vp, part):
                dst = bank(i, "v", vp, part)
                for n, t in enumerate(range(2 * part, min(2 * part + 2, KT))):
                    mm = product3(pe, dst[:, n * 256:(n + 1) * 256], lambda a, kd: kv_t[:, a, kd, t * P:(t + 1) * P],
                                  lambda a, kd: wv[:, a, kd, vp * 256:(vp + 1) * 256])
                mm.then_inc(proj_psum, 1)

            def energies(i, u):
                hp, b = u // 2, u % 2
                pe.wait_ge(proj_lo, PROJ * i + number["k", hp, b] + 1)
                wait(pe, p_exp, 16 * i + u - 1)
                for j, (a, c) in enumerate(PASSES):
                    mm = pe.matmul(s_bank[b][:, 0:LK], q_bd[:, a, b, hp, :], kt[:, hp % 2, c, b * LK:(b + 1) * LK],
                                   start=j == 0, stop=j == 2)
                mm.then_inc(s_psum, 1)

            def turn(i, u):
                pe.wait_ge(p_ready, 16 * i + u + 1)
                wait(pe, pt_lo, 16 * i + u - 1)
                if u == 1:
                    wait(pe, x_done, i)
                for t in range(3):
                    mm = pe.transpose(pt_bank[u % 2][:, t * P:(t + 1) * P], p[:, u % 4, t * P:(t + 1) * P], k.ident[:, :])
                mm.then_inc(pt_psum, 1)

            def weigh(i, u):
                hp, b = u // 2, u % 2
                pe.wait_ge(pt_lo, 16 * i + u + 1)
                if u % 4 == 0:
                    pe.wait_ge(proj_lo, PROJ * i + number["v", hp // 2, 2] + 1)
                if b == 0:
                    wait(pe, o_sum, 2 * (NU * i + hp) - 2)
                col = hp % 2 * P
                for t in range(3):
                    both, first = o_bank[hp % 2][:, b * 2 * P:(b + 1) * 2 * P], o_bank[hp % 2][:, b * 2 * P:b * 2 * P + P]
                    of = lambda a: v[:, hp // 2 % 2, a, 2 * b + t, col:col + P]
                    if t == 2:
                        pe.matmul(first, of(1), pt[:, u % 2, t, 0, :], start=False, stop=False)
                    mm = pe.matmul(both, of(0), pt[:, u % 2, t].rearrange("p c n -> p (c n)"), start=t == 0, stop=t == 2)
                    if t < 2:
                        pe.matmul(first, of(1), pt[:, u % 2, t, 0, :], start=False, stop=False)
                if b == 1:
                    mm.then_inc(o_psum, 1)

            def project_output(i):
                pe.wait_ge(o_lo, NU * i + NU)
                wait(pe, x_done, i)
                for hp in range(NU):
                    for j, (a, c) in enumerate(PASSES):
                        mm = pe.matmul(wo_bank[:, 0:D], at[:, a, hp, :], wo[:, c, hp, :], start=hp == 0 and j == 0,
                                       stop=hp == NU - 1 and j == 2)
                mm.then_inc(wo_psum, 1)

            def rest(i, last=False):
                weigh(i, 12)
                turn(i, 14)
                if not last:
                    turn_keys(i + 1, 1)
                weigh(i, 13)
                turn(i, 15)
                weigh(i, 14)
                weigh(i, 15)

            def pair(i, first=False, last=False):
                if first:
                    pe.wait_ge(w_lo, 1)
                else:
                    rest(i - 1)
                for half in range(2):
                    queries(i, half)
                if first:
                    pe.wait_ge(w_lo, 2)
                else:
                    project_output(i - 1)
                for half in range(2):
                    keys_proj(i, 0, half)
                if first:
                    pe.wait_ge(w_lo, 4)
                for u in range(16):
                    energies(i, u)
                    if u == 15 and not last:
                        turn_keys(i + 1, 0)
                    if u >= 3:
                        turn(i, u - 3)
                    steps = fillers(u)
                    for kind, a, b in steps:
                        if kind == "k":
                            keys_proj(i, a, b)
                    if u >= 4:
                        weigh(i, u - 4)
                    for kind, a, b in steps:
                        if kind == "v":
                            values_proj(i, a, b)
                turn(i, 13)

            for kd in range(KD):
                turn_keys(0, kd)
            pair(0, first=True)
            with pe.Fori(1, NT - 1) as i:
                pair(i)
            pair(NT - 1, last=True)
            rest(NT - 1, last=True)
            project_output(NT - 1)

        @block.scalar
        def _(act):
            for n, (dst, _, col) in enumerate(weights):
                act.wait_ge(w_in[n % 2], 16 * (n // 2) + 16)
                act.copy(dst[:, 0].rearrange("p k n -> p (k n)"), raw[n % 2][:, :]).then_inc(w_hi, 1)
            act.wait_ge(loads, 64)
            act.wait_ge(consts, 4)

            def turned(i, kd):
                for half, g, b in ((0, g_kv, b_kv), (1, g_l, b_l)):
                    n = number["t", kd, half]
                    act.wait_ge(proj_psum, PROJ * i + n + 1)
                    src = proj_bank[n % 2][:, 0:512] if half == 0 else proj_bank[n % 2][:, 0:P]
                    act.activation(kv_f[:, n % 2, 0:512] if half == 0 else kv_f[:, n % 2, 0:P], src, ACT.Identity,
                                   bias=b[:, kd:kd + 1], scale=g[:, kd:kd + 1]).then_inc(proj_f, 1)

            def queries(i, half):
                act.wait_ge(proj_psum, PROJ * i + number["q", half, 0] + 1)
                src = proj_bank[number["q", half, 0] % 2][:, :].rearrange("p (u b q) -> p b u q", b=2, q=S)
                for h in range(2):
                    act.activation(q_bd[h * HD:(h + 1) * HD, 0, :, 4 * half:4 * half + 4, h * S:(h + 1) * S],
                                   src[h * HD:(h + 1) * HD], ACT.Identity, scale=1.0 / 8).then_inc(proj_hi, 1)

            def keys_proj(i, hp, half):
                n = number["k", hp, half]
                act.wait_ge(proj_psum, PROJ * i + n + 1)
                act.copy(kt[:, hp % 2, 0, half * LK:(half + 1) * LK], proj_bank[n % 2][:, 0:LK]).then_inc(proj_hi, 1)

            def values_proj(i, vp, part):
                n = number["v", vp, part]
                act.wait_ge(proj_psum, PROJ * i + n + 1)
                wide = min(KT - 2 * part, 2)
                act.copy(v[:, vp % 2, 0, 2 * part:2 * part + wide, :].rearrange("p t n -> p (t n)"),
                         proj_bank[n % 2][:, 0:wide * 256]).then_inc(proj_hi, 1)

            def weights_of(i, u):
                act.wait_ge(s_max, 16 * i + u + 1)
                at_col = 0 if u % 2 == 0 else S
                act.activation(p[:, u % 4, at_col:at_col + LK], s_bank[u % 2][:, 0:LK], ACT.Exp,
                               bias=neg_max[:, u:u + 1], accum_out=rsum[:, u:u + 1]).then_inc(p_exp, 1)

            def turn(i, u):
                act.wait_ge(pt_psum, 16 * i + u + 1)
                act.copy(pt[:, u % 2, :, 0, :], pt_bank[u % 2][:, 0:3 * P].rearrange("p (t n) -> p t n", n=P)).then_inc(pt_hi, 1)

            def output(i, hp):
                act.wait_ge(o_psum, NU * i + hp + 1)
                for h in range(2):
                    act.copy(own_rows(at_c, hp, h), own_sum(hp, h, 1)).then_inc(o_part, 1)

            def output_hi(i, hp):
                act.wait_ge(o_sum, 2 * (NU * i + hp) + 2)
                act.copy(at[:, 0, hp, :], at_f[:, hp % 2, :]).then_inc(o_hi, 1)

            def rest(i, last=False):
                turn(i, 14)
                if not last:
                    turned(i + 1, 1)
                output(i, 6)
                turn(i, 15)
                output_hi(i, 6)
                output(i, 7)
                output_hi(i, 7)

            def pair(i, first=False, last=False):
                if not first:
                    rest(i - 1)
                for half in range(2):
                    queries(i, half)
                for half in range(2):
                    keys_proj(i, 0, half)
                for u in range(16):
                    for kind, a, b in fillers(u - 1) if u else ():
                        if kind == "v":
                            values_proj(i, a, b)
                    if u >= 3:
                        turn(i, u - 3)
                    weights_of(i, u)
                    if u == 15 and not last:
                        turned(i + 1, 0)
                    for kind, a, b in fillers(u):
                        if kind == "k":
                            keys_proj(i, a, b)
                    if u >= 4 and u % 2 == 1:
                        output(i, (u - 4) // 2)
                    if u >= 6 and u % 2 == 0:
                        output_hi(i, (u - 6) // 2)
                turn(i, 13)
                output_hi(i, 5)

            for kd in range(KD):
                turned(0, kd)
            pair(0, first=True)
            with act.Fori(1, NT - 1) as i:
                pair(i)
            pair(NT - 1, last=True)
            rest(NT - 1, last=True)

        @block.vector
        def _(dve):
            def context_stats(i):
                dve.wait_ge(ctx_in, 16 * i + 16)
                norm_c.gather(dve, lambda t: ctx_raw[:, t, :], i * norm_c.steps)

            context_stats(0)
            norm_x.gather(dve, lambda t: x_sb[:, t, :], 0)
            dve.wait_ge(norm_x.rstd_ready, 1)
            for t in range(NT):
                norm_x.apply(dve, xl[:, t, :], x_sb[:, t, :], t).then_inc(xl_ready, 1)
            dve.wait_ge(xl_ready, NT)
            norm_x.gather(dve, lambda t: xl[:, t, :], norm_x.steps)
            dve.wait_ge(norm_x.rstd_ready, 2)
            norm_x.apply(dve, xl[:, 0, :], xl[:, 0, :], 0).then_inc(xl_ready, 1)
            dve.wait_ge(xl_ready, NT + 1)

            def context_apply(i):
                dve.wait_ge(norm_c.rstd_ready, i + 1)
                wait(dve, proj_psum, PROJ * (i - 1) + 4)
                dve.tensor_copy(xl_now[:, :], xl[:, bass.ds(i, 1), :].rearrange("p a d -> p (a d)")).then_inc(xl_ready, 1)
                for t in range(4):
                    norm_c.apply(dve, ctx_n[:, t, :], ctx_raw[:, t, :], t).then_inc(ctx_ready, 1)

            def turned(i, kd):
                for half in range(2):
                    n = number["t", kd, half]
                    dve.wait_ge(proj_f, 4 * i + n + 1)
                    part = (lambda c: both_contexts(c, kd)) if half == 0 else (lambda c: kv_t[:, c, kd, 2 * P:3 * P])
                    full = kv_f[:, n % 2, :].rearrange("p (n c) -> p n c", n=2) if half == 0 else kv_f[:, n % 2, 0:P]
                    dve.tensor_copy(part(0), full).then_inc(t_hi, 1)
                    dve.wait_ge(t_hi, 4 * i + n + 1)
                    dve.tensor_tensor(part(1), full, part(0).bitcast(F32), ALU.subtract).then_inc(proj_lo, 1)

            def queries(i, half):
                n = number["q", half, 0]
                dve.wait_ge(proj_hi, HI * i + 2 * half + 2)
                src = proj_bank[n % 2][:, :].rearrange("p (u b q) -> p b u q", b=2, q=S)
                for h in range(2):
                    for b in range(2):
                        block_of = lambda part: q_bd[h * HD:(h + 1) * HD, part, b, 4 * half:4 * half + 4, h * S:(h + 1) * S]
                        ins = dve.scalar_tensor_tensor(out=block_of(1), in0=src[h * HD:(h + 1) * HD, b], scalar=1.0 / 8,
                                                       in1=block_of(0).bitcast(F32), op0=ALU.mult, op1=ALU.subtract)
                ins.then_inc(proj_lo, 1)

            def keys_proj(i, hp, half):
                n = number["k", hp, half]
                dve.wait_ge(proj_hi, HI * i + hi_number(n))
                dve.tensor_tensor(kt[:, hp % 2, 1, half * LK:(half + 1) * LK], proj_bank[n % 2][:, 0:LK],
                                  kt[:, hp % 2, 0, half * LK:(half + 1) * LK].bitcast(F32), ALU.subtract).then_inc(proj_lo, 1)

            def values_proj(i, vp, part):
                n = number["v", vp, part]
                dve.wait_ge(proj_hi, HI * i + hi_number(n))
                wide = min(KT - 2 * part, 2)
                cols = lambda c: v[:, vp % 2, c, 2 * part:2 * part + wide, :].rearrange("p t n -> p (t n)")
                dve.tensor_tensor(cols(1), proj_bank[n % 2][:, 0:wide * 256], cols(0).bitcast(F32),
                                  ALU.subtract).then_inc(proj_lo, 1)

            def maximum(i, u):
                dve.wait_ge(s_psum, 16 * i + u + 1)
                dve.tensor_reduce(neg_max[:, u:u + 1], s_bank[u % 2][:, 0:LK], AX.X, ALU.max, negate=True).then_inc(s_max, 1)

            def normalise(i, u):
                dve.wait_ge(p_exp, 16 * i + u + 1)
                dve.reciprocal(rinv[:, u:u + 1], rsum[:, u:u + 1]).then_inc(p_inv, 1)
                dve.wait_ge(p_inv, 16 * i + u + 1)
                at_col = 0 if u % 2 == 0 else S
                cols = p[:, u % 4, at_col:at_col + LK]
                dve.tensor_scalar(cols, cols, rinv[:, u:u + 1], None, ALU.mult).then_inc(p_ready, 1)

            def turn(i, u):
                dve.wait_ge(pt_hi, 16 * i + u + 1)
                dve.tensor_tensor(pt[:, u % 2, :, 1, :], pt_bank[u % 2][:, 0:3 * P].rearrange("p (t n) -> p t n", n=P),
                                  pt[:, u % 2, :, 0, :].bitcast(F32),
                                  ALU.subtract).then_inc(pt_lo, 1)

            def output(i, hp):
                wait(dve, o_lo, NU * i + hp - 1)
                dve.wait_ge(o_part, 2 * (NU * i + hp) + 2)
                for h in range(2):
                    dve.tensor_tensor(own_rows(at_f, hp, h), own_sum(hp, h, 0), own_rows(at_c, hp, h),
                                      ALU.add).then_inc(o_sum, 1)

            def residual(i):
                dve.wait_ge(wo_psum, i + 1)
                row = x_sb[:, bass.ds(i, 1), :].rearrange("p a d -> p (a d)")
                dve.tensor_tensor(row, row, wo_bank[:, 0:D], ALU.add).then_inc(x_done, 1)

            def rest(i, last=False):
                turn(i, 14)
                if not last:
                    turned(i + 1, 1)
                output(i, 6)
                turn(i, 15)
                output(i, 7)

            def pair(i, first=False, last=False):
                if not first:
                    rest(i - 1)
                for half in range(2):
                    queries(i, half)
                for half in range(2):
                    keys_proj(i, 0, half)
                for u in range(16):
                    maximum(i, u)
                    if u == 0 and not first:
                        residual(i - 1)
                    for kind, a, b in fillers(u - 1) if u else ():
                        if kind == "v":
                            values_proj(i, a, b)
                    if u >= 3:
                        turn(i, u - 3)
                    if u >= 1:
                        normalise(i, u - 1)
                    if u == 15 and not last:
                        turned(i + 1, 0)
                    for kind, a, b in fillers(u):
                        if kind == "k":
                            keys_proj(i, a, b)
                    if u >= 4 and u % 2 == 1:
                        output(i, (u - 4) // 2)
                    if u == 8 and not last:
                        context_stats(i + 1)
                    if u == 12 and not last:
                        context_apply(i + 1)
                normalise(i, 15)
                turn(i, 13)

            context_apply(0)
            for kd in range(KD):
                turned(0, kd)
            for t in range(1, NT):
                norm_x.apply(dve, xl[:, t, :], xl[:, t, :], t).then_inc(xl_ready, 1)
            dve.wait_ge(xl_ready, 2 * NT + 1)
            pair(0, first=True)
            with dve.Fori(1, NT - 1) as i:
                pair(i)
            pair(NT - 1, last=True)
            rest(NT - 1, last=True)
            residual(NT - 1)
            dve.wait_ge(x_done, NT)


STAGE_BODIES = {"latent_attention": latent_attention, "masked_attention": masked_attention, "experts": experts, "linear_attention": linear_attention, "feed_forward": feed_forward, "recurrence": recurrence}


class Shared:

    def __init__(self, nc, ctx):
        self.nc, self.ctx, self.of_stage = nc, ctx, []

    def sem(self, name):
        return self.ctx.enter_context(self.nc.semaphore(name))

    def stage_sem(self, name):
        self.of_stage.append(self.nc.alloc_semaphore(name=name))
        return self.of_stage[-1]

    def end_stage(self):
        self.nc.clear_and_free_semaphores(self.of_stage)
        self.nc.all_engine_barrier()
        self.of_stage = []


def constants_and_input(nc, k, x_sb, w):
    loads, made = k.sem("io_loads"), k.sem("io_made")
    with nc.Block() as block:

        @block.sync
        def _(sp):
            sp.dma_start(x_sb[:, :, :], w["x"].rearrange("(t p) d -> p t d", p=P)).then_inc(loads, 16)
            sp.wait_ge(loads, 16)

        @block.gpsimd
        def _(pool):
            pool.memset(k.ident[:, :], 0.0).then_inc(made, 1)
            pool.memset(k.head_mask[:, :], 1.0).then_inc(made, 1)
            pool.wait_ge(made, 2)
            pool.affine_select(out=k.ident[:, :], in_=k.ident[:, :], compare_op=ALU.not_equal, fill=1.0, base=0,
                               pattern=[[-1, P]], channel_multiplier=1).then_inc(made, 1)
            pool.affine_select(out=k.head_mask[:, :], in_=k.head_mask[:, :], compare_op=ALU.is_ge, fill=0.0, base=0,
                               pattern=[[-16, 8]], channel_multiplier=1).then_inc(made, 1)
            pool.wait_ge(made, 4)
            pool.affine_select(out=k.head_mask[:, :], in_=k.head_mask[:, :], compare_op=ALU.is_ge, fill=0.0, base=15,
                               pattern=[[16, 8]], channel_multiplier=-1).then_inc(made, 1)
            pool.wait_ge(made, 5)


def result(nc, k, x_sb, out):
    stored = k.sem("io_stored")
    with nc.Block() as block:

        @block.sync
        def _(sp):
            sp.dma_start(out.rearrange("(t p) d -> p t d", p=P), x_sb[:, :, :]).then_inc(stored, 16)
            sp.wait_ge(stored, 16)


STAGES = ["latent_attention", "linear_attention", "feed_forward", "masked_attention", "recurrence", "experts"]


def perceiver(nc, w, scratch, out):
    ctx = ExitStack()
    with ctx:
        k = Shared(nc, ctx)
        x_sb = ctx.enter_context(nc.sbuf_tensor("x_sb", [P, NT, D], F32))
        k.ident = ctx.enter_context(nc.sbuf_tensor("ident", [P, P], F32))
        k.head_mask = ctx.enter_context(nc.sbuf_tensor("head_mask", [P, 8], F32))
        banks = [ctx.enter_context(nc.psum_tensor(f"bank{i}", [P, 512], F32)) for i in range(8)]
        k.scratch = scratch
        constants_and_input(nc, k, x_sb, w)
        for stage in STAGES:
            STAGE_BODIES[stage](nc, k, x_sb, banks, w)
            k.end_stage()
        result(nc, k, x_sb, out)


_TURNED = ["L0_attn_Wq", "L0_attn_Wk", "L0_attn_Wv", "L0_ffn_w_gate", "L0_ffn_w_up", "L0_ffn_w_down",
           "L1_xattn_Wq", "L1_xattn_Wk", "L1_xattn_Wv", "L1_xattn_Wo",
           "L1_attn_Wi", "L1_attn_Wf", "L1_attn_Wz", "L1_attn_Wo", "L1_attn_Wp"]


def kernel(**inputs):
    import numpy as _np
    import concourse.bacc as _bacc
    from concourse import mybir as _mybir
    from concourse.bass_utils import run_bass_kernel_spmd as _run

    nc = _bacc.Bacc("TRN2", target_bir_lowering=False, num_devices=1)
    laid = {n: _np.asarray(a) for n, a in inputs.items()}
    laid["x"] = laid["x"].reshape(T, D)
    laid["ctx_1024"] = laid["ctx_1024"].reshape(B * S2, D)
    laid["ctx_turned"] = laid["ctx_1024"].T
    laid["mask_1x1xSxS2_ik1"] = laid["mask_1x1xSxS2_ik1"].reshape(S, S2)
    for n in _TURNED:
        laid[n] = laid[n].T
    arrays, aps = {}, {}
    for n, a in laid.items():
        a = _np.ascontiguousarray(a)
        arrays[f"in_{n}"] = a
        aps[n] = nc.dram_tensor(f"in_{n}", a.shape, _mybir.dt.from_np(a.dtype), kind="ExternalInput").ap()
    scratch = nc.dram_tensor("gate_rows", (NT, 8, P), F32, kind="Internal").ap()
    out = nc.dram_tensor("out_x", (T, D), F32, kind="ExternalOutput").ap()
    perceiver(nc, aps, scratch, out)
    r = _run(nc, [arrays], core_ids=[0])
    return r.results[0]["out_x"].reshape(B, S, D)
```
